# Optimizing a Trainium2 kernel written in Bass

```python
import numpy as np
import jax
import jax.numpy as jnp

def _softmax(x, axis=-1):
    return jax.nn.softmax(x, axis=axis)

def _gelu(x):
    return jax.nn.gelu(x, approximate=True)

def _silu(x):
    return jax.nn.silu(x)

def _sigmoid(x):
    return jax.nn.sigmoid(x)

def _layernorm(x, axis=-1, eps=1e-05):
    m = jnp.mean(x, axis=axis, keepdims=True)
    v = jnp.var(x, axis=axis, keepdims=True)
    return (x - m) / jnp.sqrt(v + eps)

def _scatter_add(tgt, idx, src, axis=0):
    return tgt.at[idx].add(src)

def _segment_sum(src, seg, n):
    return jax.ops.segment_sum(src, seg, n)
kernel_name = 'mk_adaln_ffn_d2_seqx_r4_eee41f'

def setup_inputs(seed: int=0):
    np.random.seed(seed)
    _w = jnp.asarray

    def _rec_inputs():
        import jax
        import jax.numpy as jnp
        _rk = jax.random.key(seed)
        x = 8.748e-05 + 1 * jax.random.normal(jax.random.fold_in(_rk, 1), (4, 512, 512), jnp.float32)
        _lenS = 512 - jax.random.randint(jax.random.fold_in(_rk, 7), (4,), 0, max(1, 512 // 4) + 1, jnp.int32)
        _lenS2 = 512 - jax.random.randint(jax.random.fold_in(_rk, 8), (4,), 0, max(1, 512 // 4) + 1, jnp.int32)
        fside_BxSx1_0 = -0.00499425 + 1.0058 * jax.random.normal(jax.random.fold_in(_rk, 11), (4, 512, 1), jnp.float32)
        cond_2048 = 0.00513981 + 1.0024 * jax.random.normal(jax.random.fold_in(_rk, 12), (4, 512), jnp.float32)
        return (x, fside_BxSx1_0, cond_2048)
    x, fside_BxSx1_0, cond_2048 = _rec_inputs()

    def _L0_cond_setup():
        import jax, jax.numpy as jnp
        import numpy as np
        G, N, K = (16, 512, 5120)
        key = jax.random.key(seed)
        k1, k2, k3 = jax.random.split(key, 3)
        return {'emb_s': jax.random.normal(k1, (G, N, 1), dtype=jnp.float32), 'emb_t': jax.random.normal(k2, (G, 1, N), dtype=jnp.float32), 'attention_weights': jax.random.normal(k3, (G, N, N), dtype=jnp.float32), 'k': K}
    _L0_cond_all = _L0_cond_setup()
    _L0_cond_in = {k: v for k, v in _L0_cond_all.items() if k in ()}
    del _L0_cond_all

    def _L0_ffn_setup():
        import jax, jax.numpy as jnp
        import numpy as np
        H = 512
        F = 352
        E = 64
        TOP_K = 6
        CAP = 128
        SCALE = 1.0
        F_SH = 2 * F
        B, S = (1, 512)
        key = jax.random.key(seed)
        ks = jax.random.split(key, 8)
        s = 0.02
        return {'hidden_states': jax.random.normal(ks[0], (B, S, H), jnp.float32), 'gate_w': jax.random.normal(ks[1], (E, H), jnp.float32) * s, 'w_gate': jax.random.normal(ks[2], (E, H, F), jnp.float32) * s, 'w_up': jax.random.normal(ks[3], (E, H, F), jnp.float32) * s, 'w_down': jax.random.normal(ks[4], (E, F, H), jnp.float32) * s, 'sh_gate': jax.random.normal(ks[5], (F_SH, H), jnp.float32) * s, 'sh_up': jax.random.normal(ks[6], (F_SH, H), jnp.float32) * s, 'sh_down': jax.random.normal(ks[7], (H, F_SH), jnp.float32) * s}
    _L0_ffn_all = _L0_ffn_setup()
    _L0_ffn_in = {k: v for k, v in _L0_ffn_all.items() if k in ('gate_w', 'w_gate', 'w_up', 'w_down', 'sh_gate', 'sh_up', 'sh_down')}
    del _L0_ffn_all

    def _L1_cond_setup():
        import jax, jax.numpy as jnp
        import numpy as np
        key = jax.random.key(seed)
        k1, k2, k3 = jax.random.split(key, 3)
        B, L, D, K = (4, 1024, 512, 4)
        x = jax.random.normal(k1, (B, L, D), dtype=jnp.float32)
        w = jax.random.normal(k2, (K, 1, D), dtype=jnp.float32) * 0.1
        b = jax.random.normal(k3, (D,), dtype=jnp.float32) * 0.1
        return {'x': x, 'w': w, 'b': b}
    _L1_cond_all = _L1_cond_setup()
    _L1_cond_in = {k: v for k, v in _L1_cond_all.items() if k in ('b',)}
    del _L1_cond_all

    def _L1_ffn_setup():
        import jax, jax.numpy as jnp
        import numpy as np
        NUM_ROUTED = 7
        TOP_K = 3
        D = 512
        H = 512
        B, S = (4, 512)

        def _expert_ffn(x, w1, wg, w2):
            return jax.nn.silu(x @ w1) * (x @ wg) @ w2
        key = jax.random.key(seed)
        ks = jax.random.split(key, 8)
        s = 0.02
        return {'x': jax.random.normal(ks[0], (B, S, D), jnp.float32), 'W1': jax.random.normal(ks[1], (NUM_ROUTED, D, H), jnp.float32) * s, 'Wg': jax.random.normal(ks[2], (NUM_ROUTED, D, H), jnp.float32) * s, 'W2': jax.random.normal(ks[3], (NUM_ROUTED, H, D), jnp.float32) * s, 'Ws1': jax.random.normal(ks[4], (D, H), jnp.float32) * s, 'Wsg': jax.random.normal(ks[5], (D, H), jnp.float32) * s, 'Ws2': jax.random.normal(ks[6], (H, D), jnp.float32) * s, 'gate_w': jax.random.normal(ks[7], (D, NUM_ROUTED), jnp.float32) * s, 'gate_b': jnp.zeros((NUM_ROUTED,), jnp.float32), 'biases': jnp.zeros((NUM_ROUTED,), jnp.float32)}
    _L1_ffn_all = _L1_ffn_setup()
    _L1_ffn_in = {k: v for k, v in _L1_ffn_all.items() if k in ('W1', 'Wg', 'W2', 'Ws1', 'Wsg', 'Ws2', 'gate_w', 'gate_b', 'biases')}
    del _L1_ffn_all
    return {'x': x, 'fside_BxSx1_0': fside_BxSx1_0, 'cond_2048': cond_2048, 'L0_ffn_gate_w': _L0_ffn_in['gate_w'], 'L0_ffn_w_gate': _L0_ffn_in['w_gate'], 'L0_ffn_w_up': _L0_ffn_in['w_up'], 'L0_ffn_w_down': _L0_ffn_in['w_down'], 'L0_ffn_sh_gate': _L0_ffn_in['sh_gate'], 'L0_ffn_sh_up': _L0_ffn_in['sh_up'], 'L0_ffn_sh_down': _L0_ffn_in['sh_down'], 'L1_cond_b': _L1_cond_in['b'], 'L1_ffn_W1': _L1_ffn_in['W1'], 'L1_ffn_Wg': _L1_ffn_in['Wg'], 'L1_ffn_W2': _L1_ffn_in['W2'], 'L1_ffn_Ws1': _L1_ffn_in['Ws1'], 'L1_ffn_Wsg': _L1_ffn_in['Wsg'], 'L1_ffn_Ws2': _L1_ffn_in['Ws2'], 'L1_ffn_gate_w': _L1_ffn_in['gate_w'], 'L1_ffn_gate_b': _L1_ffn_in['gate_b'], 'L1_ffn_biases': _L1_ffn_in['biases']}

def reference(x, fside_BxSx1_0, cond_2048, L0_ffn_gate_w, L0_ffn_w_gate, L0_ffn_w_up, L0_ffn_w_down, L0_ffn_sh_gate, L0_ffn_sh_up, L0_ffn_sh_down, L1_cond_b, L1_ffn_W1, L1_ffn_Wg, L1_ffn_W2, L1_ffn_Ws1, L1_ffn_Wsg, L1_ffn_Ws2, L1_ffn_gate_w, L1_ffn_gate_b, L1_ffn_biases):
    import jax
    import jax.numpy as jnp

    def _L0_cond_ref(emb_s, emb_t, attention_weights, k):
        import jax, jax.numpy as jnp
        import numpy as np
        G, N, K = (16, 512, 5120)
        g, n = (emb_s.shape[0], emb_s.shape[1])
        adj = emb_s * emb_t
        att = jax.nn.softmax(attention_weights, axis=-1) * (1.0 / np.sqrt(n).astype(np.float32))
        adj = adj * att
        diag = jnp.arange(n)
        adj = adj.at[:, diag, diag].set(-jnp.inf)
        flat = adj.reshape(g, n * n)
        _, idx = jax.lax.top_k(flat, k)
        rows = jnp.arange(g)[:, None]
        out = jnp.zeros((g, n * n), dtype=adj.dtype).at[rows, idx].set(1.0)
        return out.reshape(g, n, n)

    def _L0_ffn_ref(hidden_states, gate_w, w_gate, w_up, w_down, sh_gate, sh_up, sh_down):
        import jax, jax.numpy as jnp
        import numpy as np
        H = 512
        F = 352
        E = 64
        TOP_K = 6
        CAP = 128
        SCALE = 1.0
        F_SH = 2 * F
        B, S = (1, 512)
        b, s, _ = hidden_states.shape
        x = hidden_states.reshape(-1, H)
        T = x.shape[0]
        logits = x.astype(jnp.float32) @ gate_w.astype(jnp.float32).T
        scores = jax.nn.softmax(logits, axis=-1)
        topk_w, topk_idx = jax.lax.top_k(scores, TOP_K)
        topk_w = topk_w * SCALE
        eid = topk_idx.reshape(-1)
        x_exp = jnp.repeat(x, TOP_K, axis=0)
        order = jnp.argsort(eid)
        eid_s = eid[order]
        counts = jnp.bincount(eid, length=E)
        starts = jnp.cumsum(counts) - counts
        pos = jnp.arange(T * TOP_K) - starts[eid_s]
        valid = pos < CAP
        pos_c = jnp.where(valid, pos, CAP)
        buf = jnp.zeros((E, CAP + 1, H), x.dtype).at[eid_s, pos_c].set(x_exp[order])
        g = jax.nn.silu(jnp.einsum('ech,ehf->ecf', buf, w_gate))
        u = jnp.einsum('ech,ehf->ecf', buf, w_up)
        d = jnp.einsum('ecf,efh->ech', g * u, w_down)
        out_s = jnp.where(valid[:, None], d[eid_s, pos_c], 0.0)
        out_exp = jnp.zeros_like(out_s).at[order].set(out_s)
        y = jnp.einsum('tkh,tk->th', out_exp.reshape(T, TOP_K, H), topk_w)
        y = y.astype(x.dtype).reshape(b, s, H)
        gs = jax.nn.silu(hidden_states @ sh_gate.T)
        us = hidden_states @ sh_up.T
        y = y + gs * us @ sh_down.T
        return y

    def _L1_cond_ref(x, w, b):
        import jax, jax.numpy as jnp
        import numpy as np
        'Depthwise causal conv1d, channel-last.\n            x: (B, L, D); w: (K, 1, D); b: (D,). Returns (B, L, D).\n            Matches torch: Conv1d(D, D, K, groups=D, padding=K-1)(x.T)[..., :L].T\n            which is exactly a causal conv (left pad K-1, trim to L).\n            '
        K = w.shape[0]
        D = x.shape[-1]
        y = jax.lax.conv_general_dilated(x, w, window_strides=(1,), padding=[(K - 1, 0)], feature_group_count=D, dimension_numbers=('NWC', 'WIO', 'NWC'))
        return y + b

    def _L1_ffn_ref(x, W1, Wg, W2, Ws1, Wsg, Ws2, gate_w, gate_b, biases):
        import jax, jax.numpy as jnp
        import numpy as np
        NUM_ROUTED = 7
        TOP_K = 3
        D = 512
        H = 512
        B, S = (4, 512)

        def _expert_ffn(x, w1, wg, w2):
            return jax.nn.silu(x @ w1) * (x @ wg) @ w2
        output = _expert_ffn(x, Ws1, Wsg, Ws2)
        gate_logits = x @ gate_w + gate_b
        gate_probas = jax.nn.softmax(gate_logits, axis=-1)
        biased_probas = gate_probas + biases
        _, topk_idxs = jax.lax.top_k(biased_probas, TOP_K)
        topk_probas = jnp.take_along_axis(gate_probas, topk_idxs, axis=-1)
        topk_probas = topk_probas / jnp.sum(topk_probas, axis=-1, keepdims=True)
        for e in range(NUM_ROUTED):
            w_e = jnp.sum(topk_probas * (topk_idxs == e), axis=-1)
            output = output + _expert_ffn(x, W1[e], Wg[e], W2[e]) * w_e[..., None]
        return output
    x = x + _L0_ffn_ref(_L0_cond_ref(fside_BxSx1_0, cond_2048[:, None, :], x, 5120), L0_ffn_gate_w, L0_ffn_w_gate, L0_ffn_w_up, L0_ffn_w_down, L0_ffn_sh_gate, L0_ffn_sh_up, L0_ffn_sh_down)
    x = x + _L1_ffn_ref(_L1_cond_ref(x, cond_2048[:, None, :], L1_cond_b), L1_ffn_W1, L1_ffn_Wg, L1_ffn_W2, L1_ffn_Ws1, L1_ffn_Wsg, L1_ffn_Ws2, L1_ffn_gate_w, L1_ffn_gate_b, L1_ffn_biases)
    return x

_drawn_inputs = setup_inputs


def setup_inputs(seed=0):
    import zlib

    import numpy as np

    out = dict(_drawn_inputs(seed))
    spreads = {'L1_ffn_gate_b': (0.0, 0.348), 'L1_ffn_biases': (0.0, 0.1)}
    factors = {'fside_BxSx1_0': 8.0,
     'L0_ffn_gate_w': 8.0,
     'L0_ffn_w_gate': 8.0,
     'L0_ffn_w_up': 8.0,
     'L0_ffn_w_down': 8.0,
     'L0_ffn_sh_gate': 8.0,
     'L0_ffn_sh_up': 8.0,
     'L0_ffn_sh_down': 8.0}
    for name, (base, spread) in spreads.items():
        noise = np.random.default_rng([zlib.crc32(name.encode()), seed]).standard_normal(out[name].shape)
        drawn = base * np.exp(spread * noise) if base else spread * noise
        out[name] = jnp.asarray(drawn.astype(out[name].dtype))
    for name, factor in factors.items():
        out[name] = (out[name] * factor).astype(out[name].dtype)
    return out
```

```python
from contextlib import ExitStack

import concourse.bass as bass
from concourse import mybir

ALU = mybir.AluOpType
ACT = mybir.ActivationFunctionType
AX = mybir.AxisListType.X
F32, F32R, BF16 = mybir.dt.float32, mybir.dt.float32r, mybir.dt.bfloat16
I32, U32 = mybir.dt.int32, mybir.dt.uint32

P = 128
B, S, D = 4, 512, 512
T = B * S
TB = S // P
TT = T // P
DC = D // P
KEEP = 5120
E0, K0, F0, CAP = 64, 6, 352, 128
HALVES = 2
F0C = [(0, 128), (128, 128), (256, 96)]
E1, K1 = 7, 3
BINS = E1 * TT
COLS1 = BINS + 1
TILES1 = T * K1 // P + E1 - 1
STEPS = 32
DIAG = -3.0e38
INV_SQRT_N = 0.04419417306780815
OUT_OF_BOUNDS = 1.0e6
COARSE, FINE = 1152, 896
ABOVE = 1.0 + 2.0 ** -10
PER_BATCH = 38
PER_BATCH_C = 80

CF_ID, CF_ONE, CF_TRI, CF_BIT, CF_I64 = 0, 128, 256, 384, 416
CF_J, CF_I8 = 480, 480 + TILES1
CF_HALF = CF_I8 + 8
NCF = CF_HALF + P
CI_BIT, CI_TOK, CI_PAD = 0, 32, 48


class Chain:

    def __init__(self, eng, sem):
        self.eng, self.sem, self.n, self.i, self.per = eng, sem, 0, None, 0

    def did(self, ins):
        ins.then_inc(self.sem, 1)
        self.n += 1
        return self.n

    def at(self, n):
        return n if self.i is None else self.i * self.per + n

    def wait(self, n=None):
        self.eng.wait_ge(self.sem, self.at(self.n if n is None else n))

    def loop(self, i, per, first=0):
        self.start, self.i, self.per, self.first = self.n, i, per, first
        self.n = self.start - first * per

    def end(self, count):
        assert self.n == self.start - self.first * self.per + self.per, (self.n, self.start, self.per)
        self.i, self.n = None, self.start + count * self.per


def build(nc, x, fside, cond, gate0, w_gate, w_up, w_down, sh_in, sh_down, conv_b, w_res,
          gate1, gate1_b, biases, c_f32, c_i32, out):
    with ExitStack() as ctx:
        def sb(name, shape, dt=F32, till=ctx):
            return till.enter_context(nc.sbuf_tensor(name, shape, dt))

        def sem(name):
            return ctx.enter_context(nc.semaphore(name))

        def dram(name, shape, dt=F32):
            return nc.dram_tensor(name, shape, dt, kind="Internal").ap()

        mask_rows = dram("mask_rows", (T + P, D), BF16)
        acc0 = dram("acc0", (T + P, D))
        y_rows = dram("y_rows", (T + P, D))
        slots0 = dram("slots0", (P * E0, 2))
        slots1 = dram("slots1", (P * COLS1, 2))

        SLOT = 3 * DC * D
        misc = sb("misc", [P, 9000])
        cf = sb("cf", [P, NCF])
        cb = sb("cb", [P, 384], BF16)
        ci = sb("ci", [P, 49], I32)
        early = ctx.enter_context(ExitStack())
        front = sb("front", [P, 8192 + 6 * D + DC * E0 + 15488], till=early)
        sh_parts = sb("sh_parts", [P, 2 * DC * 4 * F0], F32R, till=early)
        mask_cols = sb("mask_cols", [P, TB * DC * P], F32R, till=early)
        PS = [ctx.enter_context(nc.psum_tensor(f"ps{i}", [P, 512], F32)) for i in range(8)]

        ident, ones, tri = cf[:, CF_ID:CF_ID + P], cf[:, CF_ONE:CF_ONE + P], cf[:, CF_TRI:CF_TRI + P]
        identb, trib, onesb = (cb[:, c:c + P] for c in (CF_ID, CF_TRI, CF_ONE))

        def take(region, at, words, dt=F32):
            v = region[:, at:at + words]
            return v if dt == F32 else v.bitcast(dt)

        def later(b, t=0):
            return t > 0 or not isinstance(b, int) or b > 0

        val = take(front, 0, TT * S)
        sh_dw = take(front, TT * S, 6 * D).rearrange("p (c n) -> p c n", c=6)
        gate0_w = take(front, TT * S + 6 * D, DC * E0).rearrange("p (c e) -> p c e", c=DC)
        A2 = TT * S + 6 * D + DC * E0
        junk = take(front, A2, 1024, BF16)
        junk_a = take(front, A2 + 1024, 1024, BF16)
        cond_bc = take(front, A2 + 2048, B * S)
        val16 = take(front, A2 + 4096, TT * S // 2, BF16)
        sh_w = take(front, A2 + 8192, DC * 4 * F0).rearrange("p (c f) -> p c f", c=DC)
        sh_hi, sh_lo = (sh_parts[:, i * DC * 4 * F0:(i + 1) * DC * 4 * F0].rearrange("p (c f) -> p c f", c=DC)
                        for i in range(2))

        fs = take(misc, 0, TT)
        rmax = take(misc, 16, TT)
        nmax = take(misc, 32, TT)
        esum = take(misc, 48, TT)
        rsum = take(misc, 64, TT)
        fac = take(misc, 80, TT)
        cnt = take(misc, 96, B)
        cand = take(misc, 100, B, I32)
        incr = take(misc, 104, B, I32)
        candf = take(misc, 100, B)
        cand16 = candf.bitcast(BF16)[:, 1:2 * B:2]
        cnt_a = take(misc, 340 + D, B)
        step_f = take(misc, 348 + D, B)
        step_i = take(misc, 352 + D, B, I32)
        empty = take(misc, 110, COLS1 * 2, I32).rearrange("p (c w) -> p c w", w=2)
        MZ = 110 + COLS1 * 2
        zeros = take(misc, MZ, D)
        M2 = MZ + D + 20
        assert MZ == 336

        x_t = x.rearrange("(t p) d -> p t d", p=P)
        x_in = [sem(f"x_in{b}") for b in range(B)]
        const_in, side_in, shw_in, init_out = sem("const_in"), sem("side_in"), sem("shw_in"), sem("init_out")
        empty_ready, cand_ready, counted_a, halved = sem("empty_ready"), sem("cand_ready"), sem("counted_a"), sem("halved")
        max_ready, exp_ready, scored, diag_set = sem("max_ready"), sem("exp_ready"), sem("scored"), sem("diag_set")
        counted, totalled, split = sem("counted"), sem("totalled"), sem("split")
        dve_did = sem("dve_did")

        with nc.Block() as block:
            @block.sync
            def _(sp):
                for b in range(B):
                    sp.dma_start(val[:, b * TB * S:(b + 1) * TB * S].rearrange("p (t d) -> p t d", t=TB),
                                 x_t[:, b * TB:(b + 1) * TB, :]).then_inc(x_in[b], 16)
                    if b == 0:
                        sp.dma_start(cf[:, :], c_f32).then_inc(const_in, 16)
                        sp.dma_start(ci[:, :], c_i32).then_inc(const_in, 16)
                        sp.dma_start(fs, fside).then_inc(side_in, 16)
                        sp.dma_start(cond_bc, cond.rearrange("b d -> (b d)").partition_broadcast(P)).then_inc(side_in, 16)
                sp.dma_start(sh_w, sh_in.rearrange("(p c) f -> p c f", c=DC)).then_inc(shw_in, 16)
                for h in range(HALVES):
                    sp.dma_start(sh_dw[:, 3 * h:3 * h + 2, :],
                                 sh_down[h * F0:h * F0 + 256, :].rearrange("(c p) n -> p c n", p=P)).then_inc(shw_in, 16)
                    sp.dma_start(sh_dw[0:96, 3 * h + 2, :], sh_down[h * F0 + 256:(h + 1) * F0, :]).then_inc(shw_in, 16)
                sp.dma_start(gate0_w, gate0.rearrange("(p c) e -> p c e", c=DC)).then_inc(shw_in, 16)
                sp.wait_ge(shw_in, 96)
                sp.wait_ge(empty_ready, 3)
                sp.dma_start(slots0.rearrange("(p c) w -> p (c w)", p=P), empty[:, 0:E0, :].rearrange("p c w -> p (c w)")
                             .bitcast(F32)).then_inc(init_out, 16)
                sp.dma_start(slots1.rearrange("(p c) w -> p (c w)", p=P), empty.rearrange("p c w -> p (c w)")
                             .bitcast(F32)).then_inc(init_out, 16)
                sp.dma_start(mask_rows[T:T + P, :], zeros[:, 0:D // 2].bitcast(BF16)).then_inc(init_out, 16)
                for rows in (acc0, y_rows, out):
                    sp.dma_start(rows[T:T + P, :], zeros).then_inc(init_out, 16)
                sp.wait_ge(init_out, 96)

            @block.vector
            def _(dve):
                own = Chain(dve, dve_did)
                dve.memset(zeros, 0.0).then_inc(empty_ready, 1)
                dve.memset(empty[:, :, 1], 0).then_inc(empty_ready, 1)
                own.did(dve.memset(cand, 0))
                dve.wait_ge(const_in, 32)
                own.did(dve.tensor_copy(cb[:, :], cf[:, 0:3 * P]))
                dve.tensor_copy(empty[:, :, 0], ci[:, CI_PAD:CI_PAD + 1].broadcast_to([P, COLS1])).then_inc(empty_ready, 1)
                for b in range(B):
                    t4 = slice(b * TB, (b + 1) * TB)
                    dve.wait_ge(x_in[b], 16)
                    own.did(dve.tensor_reduce(rmax[:, t4], val[:, b * TB * S:(b + 1) * TB * S]
                                              .rearrange("p (t d) -> p t d", t=TB), AX, ALU.max))
                    own.wait()
                    dve.tensor_scalar(nmax[:, t4], rmax[:, t4], -1.0, None, ALU.mult).then_inc(max_ready, 1)
                dve.wait_ge(side_in, 32)
                for b in range(B):
                    t4 = slice(b * TB, (b + 1) * TB)
                    dve.wait_ge(exp_ready, TB * (b + 1))
                    own.did(dve.reciprocal(rsum[:, t4], esum[:, t4]))
                    own.wait()
                    own.did(dve.tensor_scalar(rsum[:, t4], rsum[:, t4], INV_SQRT_N, None, ALU.mult))
                    own.wait()
                    own.did(dve.tensor_tensor(fac[:, t4], rsum[:, t4], fs[:, t4], ALU.mult))
                    own.wait()
                    for t in range(b * TB, (b + 1) * TB):
                        v = val[:, t * S:(t + 1) * S]
                        dve.scalar_tensor_tensor(v, v, fac[:, t:t + 1], cond_bc[:, b * S:(b + 1) * S],
                                                 ALU.mult, ALU.mult).then_inc(scored, 1)

                def count(b, i, coarse):
                    if later(i, b):
                        dve.wait_ge(counted, 4 * i + b)
                    own_, at, n = (val16, cand16, COARSE) if coarse else (val, candf, FINE)
                    dve.tensor_scalar(junk[:, 0:n], own_[:, b * TB * S:b * TB * S + n], at[:, b:b + 1], 0.0,
                                      ALU.is_ge, ALU.add, accum_out=cnt[:, b:b + 1]).then_inc(counted, 1)

                def decide(c, i, coarse):
                    dve.wait_ge(totalled, 4 * i + c + 2)
                    signs = TB * S - (COARSE if coarse else FINE)
                    own.did(dve.tensor_scalar(incr[:, c:c + 2], PS[c // 2][:, c:c + 2], KEEP - 0.5 - signs * P / 2,
                                              cf[:, bass.ds(i + CF_BIT, 1)], ALU.is_lt, ALU.mult))
                    own.wait()
                    dve.scalar_tensor_tensor(cand[:, c:c + 2], incr[:, c:c + 2], ci[:, bass.ds(i + CI_BIT, 1)],
                                             cand[:, c:c + 2], ALU.bitwise_xor, ALU.bitwise_xor).then_inc(cand_ready, 1)

                def rounds(i, coarse, before):
                    dve.wait_ge(cand_ready, 2 * i)
                    count(0, i, coarse)
                    count(1, i, coarse)
                    decide(2, i - 1, before)
                    dve.wait_ge(cand_ready, 2 * i + 1)
                    count(2, i, coarse)
                    count(3, i, coarse)
                    decide(0, i, coarse)

                dve.sem_inc(cand_ready, 1)
                for b in range(B):
                    dve.wait_ge(halved, b + 1)
                    count(b, 0, True)
                decide(0, 0, True)
                HALF = STEPS // 2
                rounds(1, True, True)
                with dve.Fori(1, HALF // 2) as j:
                    own.loop(j, 4, 1)
                    rounds(2 * j, True, True)
                    rounds(2 * j + 1, True, True)
                    own.end(HALF // 2 - 1)
                rounds(HALF, False, True)
                rounds(HALF + 1, False, False)
                with dve.Fori(HALF // 2 + 1, STEPS // 2) as j:
                    own.loop(j, 4, HALF // 2 + 1)
                    rounds(2 * j, False, False)
                    rounds(2 * j + 1, False, False)
                    own.end(HALF // 2 - 1)
                decide(2, STEPS - 1, False)
                dve.wait_ge(cand_ready, 2 * STEPS + 1)
                own.did(dve.tensor_scalar(step_f, candf, 0.0, -2.0, ALU.is_lt, ALU.mult))
                own.wait()
                own.did(dve.tensor_scalar(step_f, step_f, 1.0, None, ALU.add))
                own.wait()
                own.did(dve.tensor_copy(step_i, step_f))
                own.wait()
                own.did(dve.tensor_tensor(cand, cand, step_i, ALU.add))
                own.wait()
                for b in range(B):
                    dve.wait_ge(counted, B * STEPS + b)
                    dve.tensor_scalar(junk[:, 0:TB * S], val[:, b * TB * S:(b + 1) * TB * S], candf[:, b:b + 1], 0.0,
                                      ALU.is_ge, ALU.add, accum_out=cnt[:, b:b + 1]).then_inc(counted, 1)
                for c in (0, 2):
                    dve.wait_ge(totalled, 4 * STEPS + c + 2)
                    own.did(dve.tensor_scalar(step_f[:, c:c + 2], PS[c // 2][:, c:c + 2], float(KEEP), None, ALU.is_lt))
                own.wait()
                own.did(dve.scalar_tensor_tensor(step_f, step_f, -1.0, step_i, ALU.mult, ALU.mult))
                own.wait()
                own.did(dve.tensor_copy(step_i, step_f))
                own.wait()
                own.did(dve.tensor_tensor(cand, cand, step_i, ALU.add))
                own.wait()

            @block.scalar
            def _(act):
                for b in range(B):
                    act.wait_ge(max_ready, b + 1)
                    for t in range(b * TB, (b + 1) * TB):
                        v = val[:, t * S:(t + 1) * S]
                        act.activation(v, v, ACT.Exp, bias=nmax[:, t:t + 1], accum_out=esum[:, t:t + 1]).then_inc(exp_ready, 1)
                upper = val.bitcast(BF16)[:, 1:2 * TT * S:2]
                for b in range(B):
                    c = slice(b * TB * S, (b + 1) * TB * S)
                    act.wait_ge(diag_set, b + 1)
                    act.copy(val16[:, c], upper[:, c]).then_inc(halved, 1)

                def count(b, i, coarse):
                    if b % 2 == 0:
                        act.wait_ge(cand_ready, 2 * i + b // 2 if later(i) else 1)
                    if later(i, b):
                        act.wait_ge(counted_a, 4 * i + b)
                    if later(i):
                        act.wait_ge(totalled, 4 * (i - 1) + b + 1)
                    own_, n = (val16, COARSE) if coarse else (val, FINE)
                    act.activation(junk_a[:, 0:TB * S - n], own_[:, b * TB * S + n:(b + 1) * TB * S], ACT.Sign,
                                   scale=-ABOVE if coarse else -1.0, bias=candf[:, b:b + 1], accum_out=cnt_a[:, b:b + 1]).then_inc(counted_a, 1)
                act.wait_ge(halved, B)
                for b in range(B):
                    count(b, 0, True)
                for b in range(B):
                    count(b, 1, True)
                for first, last, coarse in ((1, STEPS // 4, True), (STEPS // 4, STEPS // 2, False)):
                    with act.Fori(first, last) as j:
                        for u in range(2):
                            for b in range(B):
                                count(b, 2 * j + u, coarse)

            @block.gpsimd
            def _(pool):
                for b in range(B):
                    pool.wait_ge(scored, TB * (b + 1))
                    v = val[:, b * TB * S:(b + 1) * TB * S].rearrange("p (t d) -> p t d", t=TB)
                    pool.affine_select(out=v, in_=v, compare_op=ALU.not_equal, fill=DIAG, base=0,
                                       pattern=[[P, TB], [-1, S]], channel_multiplier=1).then_inc(diag_set, 1)
                pool.wait_ge(shw_in, 96)
                pool.tensor_copy(sh_hi, sh_w).then_inc(split, 1)
                pool.wait_ge(split, 1)
                pool.tensor_tensor(sh_lo, sh_w, sh_hi, ALU.subtract).then_inc(split, 1)

            @block.tensor
            def _(pe):
                half = cf[:, CF_HALF:CF_HALF + P]

                def total(b, i):
                    pe.wait_ge(counted, 4 * i + b + 1)
                    pe.matmul(PS[b // 2][:, b:b + 1], ones, cnt[:, b:b + 1], start=True, stop=False)
                    pe.wait_ge(counted_a, 4 * i + b + 1)
                    pe.matmul(PS[b // 2][:, b:b + 1], half, cnt_a[:, b:b + 1], start=False, stop=True).then_inc(totalled, 1)
                pe.wait_ge(const_in, 32)
                for i in range(2):
                    for b in range(B):
                        total(b, i)
                with pe.Fori(1, STEPS // 2) as j:
                    for u in range(2):
                        for b in range(B):
                            total(b, 2 * j + u)
                for b in range(B):
                    pe.wait_ge(counted, 4 * STEPS + b + 1)
                    pe.matmul(PS[b // 2][:, b:b + 1], ones, cnt[:, b:b + 1], start=True, stop=True).then_inc(totalled, 1)

        xTn = take(front, A2, TB * DC * P)
        xT = mask_cols
        ge = take(front, A2 + 2048, TB * S)
        eq = take(front, A2 + 4096, TB * S)
        cum = take(front, A2 + 6144, TB * S)
        mask = take(front, A2 + 8192, TB * S // 2, BF16)
        oh = take(front, A2 + 9216, TB * K0 * E0)
        prod = take(front, A2 + 10752, TB * K0 * E0)
        x_res = [take(front, A2 + 12288 + i * D, D) for i in range(2)]
        ob = [take(front, A2 + 13312 + i * D, D) for i in range(2)]
        sil = take(front, A2 + 14336, F0)
        gu = take(front, A2 + 14720, F0)
        hT = take(front, A2 + 15104, 384).rearrange("p (c n) -> p c n", c=3)
        gecnt = take(misc, M2, 1)
        rc = take(misc, M2 + 4, TB)
        rcex = take(misc, M2 + 8, 5)
        lim = take(misc, M2 + 16, 5)
        top = take(misc, M2 + 24, TB * 8).rearrange("p (t k) -> p t k", k=8)
        idx = take(misc, M2 + 56, TB * 8, U32).rearrange("p (t k) -> p t k", k=8)
        idxf = take(misc, M2 + 88, TB * K0)
        es = take(misc, M2 + 112, TB)
        td = take(misc, M2 + 116, TB * 8).rearrange("p (t k) -> p t k", k=8)
        posk = take(misc, M2 + 148, TB * K0)
        over = take(misc, M2 + 172, TB * K0)
        dest = take(misc, M2 + 196, TB * K0, I32)
        pairs = take(misc, M2 + 220, TB * K0 * 2)
        lm = take(misc, M2 + 268, TB * E0).rearrange("p (t e) -> p t e", e=E0)
        selb = take(misc, M2 + 524, TB * E0 // 2, BF16).rearrange("p (t e) -> p t e", e=E0)
        carry = take(misc, M2 + 652, E0 // 2, BF16)
        seltot = take(misc, M2 + 684, E0)
        M3 = M2 + 748

        names = ("g_ready sil_ready u_ready gu_ready t_ready ht_ready d_ready o_ready tie_in tie_ready mask_ready "
                 "xt_ready xtn_ready xt_moved log_ready lm_ready exp_done sel_ready pos_ready scat_ready scat_done "
                 "mask_out pool_step dve_step dve2")
        (g_ready, sil_ready, u_ready, gu_ready, t_ready, ht_ready, d_ready, o_ready, tie_in, tie_ready, mask_ready,
         xt_ready, xtn_ready, xt_moved, log_ready, lm_ready, exp_done, sel_ready, pos_ready, scat_ready, scat_done,
         mask_out, pool_step, dve_step, dve2) = (sem(n) for n in names.split())
        o_out = [sem(f"o_out{i}") for i in range(2)]
        xr_in = [sem(f"xr_in{i}") for i in range(2)]
        gate_ps, up_ps, t_ps, d_ps, xt_ps, tie_ps, log_ps, pos_ps = PS
        xt_psb = xt_ps[:, 0:DC * P // 2].bitcast(BF16)
        ITEMS = TB * HALVES
        acc0_t = acc0[0:T].rearrange("(t p) d -> t p d", p=P)
        x_tp = x.rearrange("(t p) d -> t p d", p=P)
        mask_bt = mask_rows[0:T].rearrange("(b t p) d -> b p t d", p=P, t=TB)

        with nc.Block() as block:
            @block.sync
            def _(sp):
                def load_x(b, t):
                    sp.dma_start(x_res[t % 2], x_tp[b * TB + t]).then_inc(xr_in[t % 2], 16)

                def mask_store(b):
                    sp.wait_ge(mask_ready, b + 1)
                    sp.dma_start(mask_bt[b], mask.rearrange("p (t d) -> p t d", t=TB)).then_inc(mask_out, 16)

                def batch(b, more):
                    for t in range(TB):
                        if t == 2 and more:
                            mask_store(b + 1)
                        sp.wait_ge(o_ready, b * TB + t + 1)
                        sp.dma_start(acc0_t[b * TB + t], ob[t % 2]).then_inc(o_out[t % 2], 16)
                        if t < 2 or more:
                            load_x(b if t < 2 else b + 1, (t + 2) % TB)
                load_x(0, 0)
                load_x(0, 1)
                mask_store(0)
                batch(0, True)
                with sp.Fori(1, B - 1) as i:
                    batch(i, True)
                batch(B - 1, False)
                sp.wait_ge(mask_out, 16 * B)
                for i in range(2):
                    sp.wait_ge(o_out[i], 16 * TT // 2)

            @block.gpsimd
            def _(pool):
                with pool.Fori(0, B) as b:
                    pool.wait_ge(scat_ready, b + 1)
                    pool.sem_inc(pool_step, 1)
                    for j in range(TB * K0):
                        pool.indirect_dma_start(slots0, bass.IndirectOffsetOnAxis(dest[:, j:j + 1].bitcast(U32), 0),
                                                pairs[:, 2 * j:2 * j + 2], None, bounds_check=P * E0 - 1,
                                                oob_is_err=False).then_inc(scat_done, 16)
                pool.wait_ge(scat_done, 16 * TT * K0)

            @block.scalar
            def _(act):
                def copy_x(b, t):
                    act.wait_ge(xt_ready, b * TB + t + 1)
                    act.copy(xTn[:, t * DC * P:(t + 1) * DC * P], xt_psb).then_inc(xtn_ready, 1)

                def softmax(b):
                    act.wait_ge(lm_ready, 2 * b + 2)
                    act.activation(lm, lm, ACT.Exp).then_inc(exp_done, 1)
                    act.activation(td, td, ACT.Exp).then_inc(exp_done, 1)

                def item(b, m):
                    n = b * ITEMS + m
                    act.wait_ge(g_ready, n + 1)
                    if later(b, m):
                        act.wait_ge(gu_ready, n)
                    act.activation(sil, gate_ps[:, 0:F0], ACT.Silu).then_inc(sil_ready, 1)

                def copy_h(b, m):
                    act.wait_ge(t_ready, b * ITEMS + m + 1)
                    act.copy(hT[:, 0:2, :], t_ps[:, 0:256].rearrange("p (c n) -> p c n", c=2))
                    act.copy(hT[0:96, 2, :], t_ps[0:96, 256:384]).then_inc(ht_ready, 1)

                def batch(b, more):
                    act.wait_ge(xtn_ready, TB * (b + 1))
                    act.wait_ge(log_ready, b + 1)
                    if later(b):
                        act.wait_ge(u_ready, b * ITEMS)
                    act.copy(xT[:, :], xTn).then_inc(xt_moved, 1)
                    if more:
                        act.wait_ge(xt_moved, b + 1)
                    for m in range(ITEMS):
                        item(b, m)
                        if m:
                            copy_h(b, m - 1)
                        if more and m in (4, 5):
                            copy_x(b + 1, 2 * m - 8)
                            copy_x(b + 1, 2 * m - 7)
                        if more and m == 7:
                            softmax(b + 1)
                    copy_h(b, ITEMS - 1)
                for t in range(TB):
                    copy_x(0, t)
                softmax(0)
                batch(0, True)
                with act.Fori(1, B - 1) as i:
                    batch(i, True)
                batch(B - 1, False)

            @block.vector
            def _(dve):
                own = Chain(dve, dve2)

                def at_value(b):
                    v = val[:, bass.ds(b * TB * S, TB * S)]
                    thr = candf[:, bass.ds(b, 1)]
                    own.did(dve.tensor_scalar(eq, v, thr, None, ALU.is_equal))
                    own.did(dve.tensor_scalar(ge, v, thr, 0.0, ALU.is_ge, ALU.add, accum_out=gecnt))
                    own.wait()

                def scan(t):
                    c = slice(t * S, (t + 1) * S)
                    own.did(dve.tensor_tensor_scan(cum[:, c], eq[:, c], eq[:, c], 0.0, ALU.add, ALU.max))

                def tie_counts():
                    last = cum.rearrange("p (t s) -> p t s", t=TB)[:, :, S - 1]
                    own.wait()
                    own.did(dve.tensor_copy(rc, last))
                    own.did(dve.memset(rcex[:, 0:1], 0.0))
                    own.wait()
                    for t in range(TB):
                        own.did(dve.tensor_tensor(rcex[:, t + 1:t + 2], rcex[:, t:t + 1], rc[:, t:t + 1], ALU.add))
                        own.wait()
                    dve.tensor_tensor(rcex[:, 4:5], gecnt, rcex[:, 4:5], ALU.subtract).then_inc(tie_in, 1)

                def make_mask(b):
                    dve.wait_ge(tie_ready, b + 1)
                    own.did(dve.tensor_scalar(lim[:, 4:5], tie_ps[:, 4:5], -1.0, float(KEEP), ALU.mult, ALU.add))
                    own.wait()
                    own.did(dve.tensor_scalar(lim[:, 0:4], tie_ps[:, 0:4], lim[:, 4:5], -1.0, ALU.subtract, ALU.mult))
                    own.wait()
                    for t in range(TB):
                        c = slice(t * S, (t + 1) * S)
                        own.did(dve.scalar_tensor_tensor(eq[:, c], cum[:, c], lim[:, t:t + 1], eq[:, c],
                                                         ALU.is_gt, ALU.mult))
                    own.wait()
                    if later(b):
                        dve.wait_ge(mask_out, 16 * b)
                        dve.wait_ge(xt_ready, TB * b)
                    dve.tensor_tensor(mask, ge, eq, ALU.subtract).then_inc(mask_ready, 1)

                def best(b):
                    dve.wait_ge(log_ready, b + 1)
                    dve.sem_inc(dve_step, 1)
                    for t in range(TB):
                        own.did(dve.max(top[:, t, :], log_ps[:, t * E0:(t + 1) * E0]))
                    own.wait()
                    dve.sem_inc(dve_step, 1)
                    for t in range(TB):
                        own.did(dve.max_index(idx[:, t, :], top[:, t, :], log_ps[:, t * E0:(t + 1) * E0]))
                    largest = top[:, :, 0:1]
                    dve.tensor_tensor(lm, log_ps[:, 0:TB * E0].rearrange("p (t e) -> p t e", e=E0),
                                      largest.broadcast_to([P, TB, E0]), ALU.subtract).then_inc(lm_ready, 1)
                    dve.tensor_tensor(td, top, largest.broadcast_to([P, TB, 8]), ALU.subtract).then_inc(lm_ready, 1)
                    own.wait()
                    own.did(dve.tensor_copy(idxf.rearrange("p (t k) -> p t k", k=K0), idx[:, :, 0:K0]))
                    own.wait()

                ohv = oh.rearrange("p (j e) -> p j e", e=E0)

                def one_hot(b):
                    own.did(dve.tensor_tensor(ohv, cf[:, CF_I64:CF_I64 + E0].unsqueeze(1).broadcast_to([P, TB * K0, E0]),
                                              idxf.unsqueeze(2).broadcast_to([P, TB * K0, E0]), ALU.is_equal))
                    own.wait()
                    with nc.allow_low_precision("0 or 1"):
                        dve.tensor_reduce(selb, oh.rearrange("p (t k e) -> p t e k", k=K0, e=E0), AX,
                                          ALU.add).then_inc(sel_ready, 1)

                def weights(b):
                    dve.wait_ge(exp_done, 2 * b + 2)
                    own.did(dve.tensor_reduce(es, lm, AX, ALU.add))
                    own.wait()
                    own.did(dve.reciprocal(es, es))
                    own.wait()
                    if later(b):
                        dve.wait_ge(scat_done, 16 * TB * K0 * b)
                    pv = pairs.rearrange("p (t k w) -> p t k w", k=K0, w=2)
                    own.did(dve.tensor_tensor(pv[:, :, :, 1], td[:, :, 0:K0],
                                              es.unsqueeze(2).broadcast_to([P, TB, K0]), ALU.mult))
                    own.did(dve.tensor_copy(pv[:, :, :, 0].bitcast(I32), ci[:, bass.ds(b * TB + CI_TOK, TB)]
                                            .unsqueeze(2).broadcast_to([P, TB, K0])))

                def place(b):
                    dve.wait_ge(pos_ready, b + 1)
                    own.did(dve.tensor_reduce(seltot, selb.rearrange("p t e -> p e t"), AX, ALU.add))
                    pos = pos_ps[:, 0:TB * E0].rearrange("p (t e) -> p t e", e=E0)
                    own.did(dve.tensor_tensor(prod.rearrange("p (t k e) -> p t k e", k=K0, e=E0),
                                              oh.rearrange("p (t k e) -> p t k e", k=K0, e=E0),
                                              pos.unsqueeze(2).broadcast_to([P, TB, K0, E0]), ALU.mult))
                    own.wait()
                    own.did(dve.tensor_tensor(carry, carry, seltot, ALU.add))
                    own.did(dve.tensor_reduce(posk, prod.rearrange("p (j e) -> p j e", e=E0), AX, ALU.add))
                    own.wait()
                    own.did(dve.tensor_scalar(over, posk, float(CAP), OUT_OF_BOUNDS, ALU.is_ge, ALU.mult))
                    own.did(dve.scalar_tensor_tensor(posk, posk, float(E0), idxf, ALU.mult, ALU.add))
                    own.wait()
                    dve.tensor_tensor(dest, posk, over, ALU.add).then_inc(scat_ready, 1)

                def item(b, m):
                    n = b * ITEMS + m
                    dve.wait_ge(u_ready, n + 1)
                    dve.wait_ge(sil_ready, n + 1)
                    dve.tensor_tensor(gu, sil, up_ps[:, 0:F0], ALU.mult).then_inc(gu_ready, 1)

                def residual(b, t):
                    n = b * TB + t
                    dve.wait_ge(d_ready, n + 1)
                    dve.wait_ge(xr_in[t % 2], 16 * (b * 2 + t // 2 + 1))
                    if t >= 2 or later(b):
                        dve.wait_ge(o_out[t % 2], 16 * (b * 2 + t // 2))
                    dve.tensor_tensor(ob[t % 2], x_res[t % 2], d_ps[:, :], ALU.add).then_inc(o_ready, 1)

                def batch(b, more):
                    nxt = b + 1
                    for m in range(ITEMS):
                        item(b, m)
                        if m and m % 2 == 0:
                            residual(b, m // 2 - 1)
                        if not more:
                            continue
                        if m == 0:
                            at_value(nxt)
                            scan(0)
                            scan(1)
                        elif m == 1:
                            scan(2)
                            scan(3)
                            tie_counts()
                        elif m == 2:
                            make_mask(nxt)
                        elif m == 6:
                            best(nxt)
                            one_hot(nxt)
                    residual(b, TB - 1)
                    if more:
                        weights(nxt)
                        place(nxt)

                own.did(dve.memset(carry, 0.0))
                at_value(0)
                for t in range(TB):
                    scan(t)
                tie_counts()
                make_mask(0)
                best(0)
                one_hot(0)
                weights(0)
                place(0)
                batch(0, True)
                with dve.Fori(1, B - 1) as i:
                    own.loop(i, PER_BATCH, 1)
                    own.wait()
                    batch(i, True)
                    own.end(B - 2)
                batch(B - 1, False)

            @block.tensor
            def _(pe):
                def tie(b):
                    pe.wait_ge(tie_in, b + 1)
                    pe.matmul(tie_ps[:, 0:5], ones, rcex, start=True, stop=False)
                    pe.matmul(tie_ps[:, 0:4], tri, rc, start=False, stop=True).then_inc(tie_ready, 1)

                def turn(b, t):
                    pe.wait_ge(mask_ready, b + 1)
                    if later(b, t):
                        pe.wait_ge(xtn_ready, b * TB + t)
                    for c in range(DC):
                        mm = pe.transpose(xt_psb[:, c * P:(c + 1) * P], mask[:, t * S + c:(t + 1) * S:DC], identb)
                    mm.then_inc(xt_ready, 1)

                def logits(b):
                    pe.wait_ge(xtn_ready, TB * (b + 1))
                    for t in range(TB):
                        for c in range(DC):
                            mm = pe.matmul(log_ps[:, t * E0:(t + 1) * E0], xTn[:, (t * DC + c) * P:(t * DC + c + 1) * P],
                                           gate0_w[:, c, :], start=c == 0, stop=c == DC - 1)
                    mm.then_inc(log_ready, 1)

                def positions(b):
                    pe.wait_ge(sel_ready, b + 1)
                    for t in range(TB):
                        to = pos_ps[:, t * E0:(t + 1) * E0]
                        pe.matmul(to, trib, selb[:, t, :], start=True, stop=False)
                        for s in range(t):
                            pe.matmul(to, onesb, selb[:, s, :], start=False, stop=False)
                        mm = pe.matmul(to, onesb, carry, start=False, stop=True)
                    mm.then_inc(pos_ready, 1)

                def product(m, bank, column):
                    for c in range(DC):
                        for part in (sh_hi, sh_lo):
                            mm = pe.matmul(bank[:, 0:F0], xT[:, (m // 2 * DC + c) * P:(m // 2 * DC + c + 1) * P],
                                           part[:, c, column:column + F0], start=c == 0 and part is sh_hi,
                                           stop=c == DC - 1 and part is sh_lo)
                    return mm

                def gate(b, m):
                    if later(b, m):
                        pe.wait_ge(sil_ready, b * ITEMS + m)
                    product(m, gate_ps, (m % 2) * 2 * F0).then_inc(g_ready, 1)

                def up(b, m):
                    if later(b, m):
                        pe.wait_ge(gu_ready, b * ITEMS + m)
                    product(m, up_ps, (m % 2) * 2 * F0 + F0).then_inc(u_ready, 1)

                def turn_h(b, m):
                    n = b * ITEMS + m
                    pe.wait_ge(gu_ready, n + 1)
                    if later(b, m):
                        pe.wait_ge(ht_ready, n)
                    for c, (f, k) in enumerate(F0C):
                        mm = pe.transpose(t_ps[0:k, c * P:(c + 1) * P], gu[:, f:f + k], ident)
                    mm.then_inc(t_ready, 1)

                def down(b, m):
                    n = b * ITEMS + m
                    pe.wait_ge(ht_ready, n + 1)
                    if m % 2 == 0 and later(b, m):
                        pe.wait_ge(o_ready, b * TB + m // 2)
                    for c, (f, k) in enumerate(F0C):
                        mm = pe.matmul(d_ps[:, :], hT[0:k, c, :], sh_dw[0:k, 3 * (m % 2) + c, :],
                                       start=m % 2 == 0 and c == 0, stop=m % 2 == 1 and c == 2)
                    if m % 2:
                        mm.then_inc(d_ready, 1)

                def batch(b, more):
                    pe.wait_ge(xt_moved, b + 1)
                    for m in range(ITEMS):
                        gate(b, m)
                        if m:
                            turn_h(b, m - 1)
                        up(b, m)
                        if more and m == 2:
                            tie(b + 1)
                        if more and m in (4, 5):
                            turn(b + 1, 2 * m - 8)
                            turn(b + 1, 2 * m - 7)
                        if more and m == 6:
                            logits(b + 1)
                        if m:
                            down(b, m - 1)
                    turn_h(b, ITEMS - 1)
                    if more:
                        positions(b + 1)
                    down(b, ITEMS - 1)
                tie(0)
                for t in range(TB):
                    turn(0, t)
                logits(0)
                positions(0)
                batch(0, True)
                with pe.Fori(1, B - 1) as i:
                    batch(i, True)
                batch(B - 1, False)

        early.close()
        arena = sb("arena", [P, E1 * SLOT])

        def expert_stage(name, items, F, chunks, row_dt, rows, slots, cols, acc, region, table_at, loads, tile_cols=None, last_in=None):
            nch = len(chunks)
            rw = D // 2 if row_dt == BF16 else D
            at = [region]

            def buf(words, dt=F32):
                at[0] += words
                return take(arena if loads else misc, at[0] - words, words, dt)
            xrow = [buf(rw, row_dt) for _ in range(2)]
            xT = [buf(D).rearrange("p (c n) -> p c n", c=DC) for _ in range(2)]
            sil, gu, hT = buf(512), buf(512), buf(512).rearrange("p (c n) -> p c n", c=4)
            ob = [buf(D) for _ in range(2)]
            table = take(misc, table_at, 2 * cols)
            idx_get = [take(misc, table_at + 2 * cols + i, 1, I32) for i in range(2)]
            idx_add = [take(misc, table_at + 2 * cols + 2 + i, 1, I32) for i in range(2)]
            gate_ps, up_ps, h_ps, d_ps, x_ps = PS[0:5]
            x_psv = x_ps[:, 0:rw] if row_dt == F32 else x_ps[:, 0:rw].bitcast(BF16)
            idm = ident if row_dt == F32 else identb

            def sm(n):
                return sem(f"{name}_{n}")
            table_in, pool_did, pool_step = sm("table_in"), sm("pool_did"), sm("pool_step")
            rows_in = [sm(f"rows_in{i}") for i in range(2)]
            add_done = [sm(f"add_done{i}") for i in range(2)]
            x_turned, x_copied, g_ready, sil_ready = sm("x_turned"), sm("x_copied"), sm("g_ready"), sm("sil_ready")
            u_ready, gu_ready, h_turned, h_copied = sm("u_ready"), sm("gu_ready"), sm("h_turned"), sm("h_copied")
            d_ready, o_ready = sm("d_ready"), sm("o_ready")
            if loads:
                wg_in, wu_in, wd_in = ([sm(f"w{k}_in{i}") for i in range(2)] for k in "gud")

            class Tile:

                def __init__(self, n, u, h, early=False):
                    self.n, self.u, self.h, self.early = n, u, h, early
                    self.first = early and u == 0

            def fixed(n):
                return Tile(n, n % 2, n // 2, n < 2)

            def inside(j, k, ahead=0):
                o = 1 + k + ahead
                return Tile(2 * j + o, o % 2, j + o // 2)
            PAIRS = (items - 2) // 2

            def pipeline(eng, slot):
                slot(None, fixed(0), fixed(1))
                for n in (1, 2):
                    slot(fixed(n - 1), fixed(n), fixed(n + 1))
                with eng.Fori(1, PAIRS) as j:
                    for k in range(2):
                        slot(inside(j, k, -1), inside(j, k), inside(j, k, 1))
                slot(fixed(items - 2), fixed(items - 1), None)

            with nc.Block() as block:
                @block.sync
                def _(sp):
                    if loads:
                        sp.dma_start(table, slots.rearrange("(p c) w -> p (c w)", p=P)).then_inc(table_in, 16)
                        sp.wait_ge(table_in, 16)
                        (dg, du, dd), (bg, bu, bd), beside = loads

                        def in_load(t, dst, src, free, arrived):
                            if not t.early:
                                sp.wait_ge(free, t.n - 1)
                            sp.dma_start(dst[t.u], src[bass.ds(t.n, 1)].rearrange("e (p c) f -> p (e c f)", p=P)).then_inc(arrived[t.u], 16)

                        def down_load(t):
                            if not t.early:
                                sp.wait_ge(d_ready, t.n - 1)
                            sp.dma_start(bd[t.u][:, 0:2 * D].rearrange("p (c n) -> p c n", c=2),
                                         dd[bass.ds(t.n, 1), 0:2 * P, :].rearrange("e (c p) n -> p (e c) n", p=P)).then_inc(wd_in[t.u], 16)
                            sp.dma_start(bd[t.u][0:F - 2 * P, 2 * D:3 * D],
                                         dd[bass.ds(t.n, 1), 2 * P:F, :].rearrange("e p n -> p (e n)")).then_inc(wd_in[t.u], 16)

                        for n in range(2):
                            in_load(fixed(n), bg, dg, g_ready, wg_in)
                            in_load(fixed(n), bu, du, u_ready, wu_in)
                        down_load(fixed(0))
                        in_load(fixed(2), bg, dg, g_ready, wg_in)
                        in_load(fixed(2), bu, du, u_ready, wu_in)
                        down_load(fixed(1))

                        def slot(j, k):
                            t = inside(j, k, 2)
                            in_load(t, bg, dg, g_ready, wg_in)
                            in_load(t, bu, du, u_ready, wu_in)
                            down_load(inside(j, k, 1))
                        for j0, j1, piece in beside:
                            with sp.Fori(j0, j1) as j:
                                slot(j, 0)
                                piece(sp, j)
                                slot(j, 1)
                        slot(PAIRS - 1, 0)
                        down_load(fixed(items - 1))
                        for j in range(PAIRS - 1, 32):
                            piece(sp, j)
                        sp.wait_ge(beside_in, 16 * 32)

                @block.gpsimd
                def _(pool):
                    own = Chain(pool, pool_did)

                    def column(t):
                        if tile_cols is None:
                            return t.n * 2
                        return pool.value_load(tile_cols[0][0:1, bass.ds(t.n, 1)], min_val=0, max_val=cols - 1) * 2

                    def gather(t):
                        if not t.early:
                            pool.wait_ge(rows_in[t.u], t.h * 16)
                        own.did(pool.tensor_copy(idx_get[t.u], table[:, bass.ds(column(t), 1)].bitcast(I32)))
                        own.wait()
                        if not t.early:
                            pool.wait_ge(x_turned, t.n - 1)
                        pool.sem_inc(pool_step, 1)
                        pool.indirect_dma_start(xrow[t.u], None, rows, bass.IndirectOffsetOnAxis(idx_get[t.u].bitcast(U32), 0)
                                                ).then_inc(rows_in[t.u], 16)

                    def add(t):
                        if not t.first:
                            pool.wait_ge(add_done[1 - t.u], (t.h + t.u) * 16)
                        own.did(pool.tensor_copy(idx_add[t.u], table[:, bass.ds(column(t), 1)].bitcast(I32)))
                        own.wait()
                        pool.wait_ge(o_ready, t.n + 1)
                        pool.sem_inc(pool_step, 1)
                        pool.indirect_dma_start(acc, bass.IndirectOffsetOnAxis(idx_add[t.u].bitcast(U32), 0), ob[t.u], None,
                                                compute_op=ALU.add).then_inc(add_done[t.u], 16)
                    if loads:
                        pool.wait_ge(table_in, 16)
                    for n in range(3):
                        gather(fixed(n))
                    for n in range(2):
                        gather(fixed(n + 3))
                        add(fixed(n))
                    with pool.Fori(1, PAIRS - 1) as j:
                        own.loop(j, 4, 1)
                        for k in range(2):
                            gather(inside(j, k, 2))
                            add(inside(j, k, -1))
                        own.end(PAIRS - 2)
                    gather(fixed(items - 1))
                    add(fixed(items - 4))
                    add(fixed(items - 3))
                    add(fixed(items - 2))
                    add(fixed(items - 1))
                    for u in range(2):
                        pool.wait_ge(add_done[u], items // 2 * 16)

                @block.scalar
                def _(act):
                    def silu(t):
                        act.wait_ge(g_ready, t.n + 1)
                        if not t.first:
                            act.wait_ge(gu_ready, t.n)
                        act.activation(sil[:, 0:F], gate_ps[:, 0:F], ACT.Silu).then_inc(sil_ready, 1)

                    def scale(t):
                        if not t.early:
                            act.wait_ge(add_done[t.u], t.h * 16)
                        col = t.n * 2 if tile_cols is None else act.value_load(
                            tile_cols[0][0:1, bass.ds(t.n, 1)], min_val=0, max_val=cols - 1) * 2
                        act.wait_ge(d_ready, t.n + 1)
                        act.activation(ob[t.u], d_ps[:, :], ACT.Copy, scale=table[:, bass.ds(col + 1, 1)]).then_inc(o_ready, 1)

                    def slot(prev, this, nxt):
                        silu(this)
                        if prev:
                            scale(prev)
                    if loads:
                        act.wait_ge(table_in, 16)
                    pipeline(act, slot)
                    scale(fixed(items - 1))

                @block.vector
                def _(dve):
                    def copy_h(t):
                        dve.wait_ge(h_turned, t.n + 1)
                        full = [c for c, (_, k) in enumerate(chunks) if k == P]
                        mm = dve.tensor_copy(hT[:, 0:len(full), :].rearrange("p c n -> p (c n)"), h_ps[:, 0:len(full) * P])
                        for c, (_, k) in enumerate(chunks):
                            if k < P:
                                dve.tensor_copy(hT[0:k, c, :], h_ps[0:k, c * P:(c + 1) * P]).then_inc(h_copied, 1)
                                mm.then_inc(h_copied, 1)
                                return
                        mm.then_inc(h_copied, 2)

                    def product(t):
                        dve.wait_ge(sil_ready, t.n + 1)
                        dve.wait_ge(u_ready, t.n + 1)
                        dve.tensor_tensor(gu[:, 0:F], sil[:, 0:F], up_ps[:, 0:F], ALU.mult).then_inc(gu_ready, 1)

                    def copy_x(t):
                        dve.wait_ge(x_turned, t.n + 1)
                        if not t.early:
                            dve.wait_ge(u_ready, t.n - 1)
                        dve.tensor_copy(xT[t.u].rearrange("p c n -> p (c n)"), x_psv).then_inc(x_copied, 1)

                    def slot(prev, this, nxt):
                        if prev:
                            copy_h(prev)
                        product(this)
                        if nxt:
                            copy_x(nxt)
                    copy_x(fixed(0))
                    pipeline(dve, slot)
                    copy_h(fixed(items - 1))

                @block.tensor
                def _(pe):
                    def turn_x(t):
                        pe.wait_ge(rows_in[t.u], 16 * (t.h + 1))
                        if not t.first:
                            pe.wait_ge(x_copied, t.n)
                        for c in range(DC):
                            mm = pe.transpose(x_psv[:, c * P:(c + 1) * P], xrow[t.u][:, c:D:DC], idm)
                        mm.then_inc(x_turned, 1)

                    def weight(t, m, c):
                        if loads:
                            return loads[1][m][t.u][:, c * F:(c + 1) * F] if m < 2 else loads[1][m][t.u][0:chunks[c][1], c * D:(c + 1) * D]
                        return arena[:, bass.ds(t.at + (m * DC * D + c * D), D)]

                    def find(t):
                        if not loads:
                            t.at = pe.value_load(tile_cols[1][0:1, bass.ds(t.n, 1)], min_val=0, max_val=E1 - 1) * SLOT

                    def gate(t):
                        pe.wait_ge(x_copied, t.n + 1)
                        if not t.first:
                            pe.wait_ge(sil_ready, t.n)
                        if loads:
                            pe.wait_ge(wg_in[t.u], 16 * (t.h + 1))
                        for c in range(DC):
                            mm = pe.matmul(gate_ps[:, 0:F], xT[t.u][:, c, :], weight(t, 0, c), start=c == 0, stop=c == DC - 1)
                        mm.then_inc(g_ready, 1)

                    def up(t):
                        if not t.first:
                            pe.wait_ge(gu_ready, t.n)
                        if loads:
                            pe.wait_ge(wu_in[t.u], 16 * (t.h + 1))
                        for c in range(DC):
                            mm = pe.matmul(up_ps[:, 0:F], xT[t.u][:, c, :], weight(t, 1, c), start=c == 0, stop=c == DC - 1)
                        mm.then_inc(u_ready, 1)

                    def turn_h(t):
                        pe.wait_ge(gu_ready, t.n + 1)
                        if not t.first:
                            pe.wait_ge(h_copied, 2 * t.n)
                        for c, (f, k) in enumerate(chunks):
                            src = gu[:, f:f + k] if loads else gu[:, c:F:DC]
                            mm = pe.transpose(h_ps[0:k, c * P:(c + 1) * P], src, ident)
                        mm.then_inc(h_turned, 1)

                    def down(t):
                        pe.wait_ge(h_copied, 2 * (t.n + 1))
                        if not t.first:
                            pe.wait_ge(o_ready, t.n)
                        if loads:
                            pe.wait_ge(wd_in[t.u], 32 * (t.h + 1))
                        for c, (f, k) in enumerate(chunks):
                            mm = pe.matmul(d_ps[:, :], hT[0:k, c, :], weight(t, 2, c), start=c == 0, stop=c == nch - 1)
                        mm.then_inc(d_ready, 1)

                    def slot(prev, this, nxt):
                        if not loads and isinstance(this.n, int) and this.n == 2:
                            pe.wait_ge(last_in, 16)
                        if prev:
                            find(prev)
                        find(this)
                        gate(this)
                        if prev:
                            turn_h(prev)
                        up(this)
                        if nxt:
                            turn_x(nxt)
                        if prev:
                            down(prev)
                    turn_x(fixed(0))
                    pipeline(pe, slot)
                    last = fixed(items - 1)
                    find(last)
                    turn_h(last)
                    down(last)

        PIECE = SLOT // 8
        beside_in = sem("beside_in")

        def piece(to):
            def load(sp, j):
                sp.dma_start(arena[:, bass.ds(j * PIECE + to, PIECE)], w_res[:, bass.ds(j * PIECE, PIECE)]).then_inc(beside_in, 16)
            return load
        wbuf = [[take(arena, 3 * SLOT + u * 4352 + o, w) for u in range(2)] for o, w in ((0, 1408), (1408, 1408), (2816, 1536))]
        assert 3 * SLOT + 2 * 4352 <= 5 * SLOT
        NP0 = (E0 - 2) // 2
        expert_stage("e0", E0, F0, F0C, BF16, mask_rows, slots0, E0, acc0, 5 * SLOT, M2,
                     ((w_gate, w_up, w_down), wbuf, ((0, 24, piece(0)), (24, NP0 - 1, piece(3 * SLOT)))))
        C0 = 5 * SLOT
        x1 = [take(arena, C0 + i * D, D) for i in range(TB)]
        HIST = 3
        x1T = [take(arena, C0 + 2048 + i * 528, DC * (P + HIST)).rearrange("p (c n) -> p c n", c=DC) for i in range(2)]
        yT = [take(arena, C0 + 3104 + i * D, D).rearrange("p (c n) -> p c n", c=DC) for i in range(2)]
        y_row = [take(arena, C0 + 4128 + i * D, D) for i in range(2)]
        sil1 = take(misc, M3, D)
        gu1 = take(misc, M3 + 512, D)
        hT1 = take(misc, M3 + 1024, D).rearrange("p (c n) -> p c n", c=DC)
        ob1 = [take(misc, M3 + 1536 + i * D, D) for i in range(2)]
        M4 = M3 + 2560
        conv_w = take(misc, M4, 4 * DC).rearrange("p (k c) -> p k c", k=4)
        conv_bias = take(misc, M4 + 16, DC)
        gate1_w = take(misc, M4 + 20, DC * E1).rearrange("p (c e) -> p c e", c=DC)
        gb_bc = take(misc, M4 + 48, E1)
        bias_bc = take(misc, M4 + 56, E1)
        lg1 = take(misc, M4 + 64, TB * 8).rearrange("p (t e) -> p t e", e=8)
        prob = take(misc, M4 + 96, TB * 8).rearrange("p (t e) -> p t e", e=8)
        biased = take(misc, M4 + 128, TB * 8).rearrange("p (t e) -> p t e", e=8)
        top1 = take(misc, M4 + 160, TB * 8).rearrange("p (t e) -> p t e", e=8)
        idx1 = take(misc, M4 + 192, TB * 8, U32).rearrange("p (t e) -> p t e", e=8)
        mx1 = take(misc, M4 + 224, TB)
        idxf1 = take(misc, M4 + 228, TB * K1)
        oh1 = take(misc, M4 + 240, TB * K1 * 8)
        prod1 = take(misc, M4 + 336, TB * K1 * 8)
        pk1 = take(misc, M4 + 432, TB * K1)
        s3 = take(misc, M4 + 444, TB)
        pp1 = take(misc, M4 + 448, TB * K1)
        posi = take(misc, M4 + 460, TB * K1, I32)
        hi_i = take(misc, M4 + 472, TB * K1, I32)
        lo_i = take(misc, M4 + 484, TB * K1, I32)
        hi_f = take(misc, M4 + 496, TB * K1)
        lo_f = take(misc, M4 + 508, TB * K1)
        dest1 = take(misc, M4 + 520, TB * K1, I32)
        pairs1 = take(misc, M4 + 532, TB * K1 * 2)
        sel1 = take(misc, M4 + 556, TB * 4, BF16).rearrange("p (t e) -> p t e", e=8)
        carry1 = take(misc, M4 + 572, 4, BF16)
        seltot1 = take(misc, M4 + 576, 8)
        M5 = 8300
        assert M4 + 584 <= M5 and M3 + 4608 <= M5

        names = ("small_in c_x_turned c_x_copied conv_done c_log_ready y_turned y_copied c_g c_sil c_u c_gu c_ht c_hc c_d c_o "
                 "c_lm c_exp c_sel c_pos c_scat c_scat_done c_dve c_step c_pstep w34_in c_act")
        (small_in, c_x_turned, c_x_copied, conv_done, c_log_ready, y_turned, y_copied, c_g, c_sil, c_u, c_gu, c_ht, c_hc,
         c_d, c_o, c_lm, c_exp, c_sel, c_pos, c_scat, c_scat_done, c_dve, c_step, c_pstep, w34_in, c_act) = (
            sem(n) for n in names.split())
        x1_in = [sem(f"x1_in{i}") for i in range(TB)]
        y_out = [sem(f"y_out{i}") for i in range(2)]
        out_out = [sem(f"out_out{i}") for i in range(2)]
        out_t = out[0:T].rearrange("(t p) d -> t p d", p=P)
        y_t = y_rows[0:T].rearrange("(t p) d -> t p d", p=P)
        ybk_ps, log1_ps, pos1_ps = PS[5:8]
        log1 = log1_ps[:, 0:TB * 8].rearrange("p (t e) -> p t e", e=8)

        def nxt_tile(b, t):
            return (b, t + 1) if t + 1 < TB else (b + 1, 0)

        with nc.Block() as block:
            @block.sync
            def _(sp):
                sp.dma_start(gate1_w, gate1.rearrange("(p c) e -> p c e", c=DC)).then_inc(small_in, 16)
                sp.dma_start(conv_w, cond.rearrange("k (p c) -> p k c", c=DC)).then_inc(small_in, 16)
                sp.dma_start(conv_bias, conv_b.rearrange("(p c) -> p c", c=DC)).then_inc(small_in, 16)
                sp.dma_start(gb_bc, gate1_b.partition_broadcast(P)).then_inc(small_in, 16)
                sp.dma_start(bias_bc, biases.partition_broadcast(P)).then_inc(small_in, 16)

                def batch(b, more):
                    for t in range(TB):
                        n = b * TB + t
                        if more or t < TB - 1:
                            nb, nt = nxt_tile(b, t)
                            sp.wait_ge(y_copied, n + 2)
                            sp.dma_start(y_t[nb * TB + nt], y_row[nt % 2]).then_inc(y_out[nt % 2], 16)
                        sp.wait_ge(c_o, n + 1)
                        sp.dma_start(out_t[n], ob1[t % 2]).then_inc(out_out[t % 2], 16)
                        if more:
                            sp.dma_start(x1[t], acc0_t[n + TB]).then_inc(x1_in[t], 16)
                for t in range(TB):
                    sp.dma_start(x1[t], acc0_t[t]).then_inc(x1_in[t], 16)
                sp.dma_start(arena[:, 3 * SLOT:5 * SLOT], w_res[:, 4 * SLOT:6 * SLOT]).then_inc(w34_in, 16)
                sp.wait_ge(y_copied, 1)
                sp.dma_start(y_t[0], y_row[0]).then_inc(y_out[0], 16)
                batch(0, True)
                with sp.Fori(1, B - 1) as b:
                    batch(b, True)
                batch(B - 1, False)
                for i in range(2):
                    sp.wait_ge(y_out[i], 16 * TT // 2)
                    sp.wait_ge(out_out[i], 16 * TT // 2)
                sp.wait_ge(w34_in, 16)

            @block.gpsimd
            def _(pool):
                with pool.Fori(0, B) as b:
                    pool.wait_ge(c_scat, b + 1)
                    pool.sem_inc(c_pstep, 1)
                    for j in range(TB * K1):
                        pool.indirect_dma_start(slots1, bass.IndirectOffsetOnAxis(dest1[:, j:j + 1].bitcast(U32), 0),
                                                pairs1[:, 2 * j:2 * j + 2], None).then_inc(c_scat_done, 16)
                pool.wait_ge(c_scat_done, 16 * TT * K1)

            @block.scalar
            def _(act):
                def copy_x(b, t):
                    n = b * TB + t
                    act.wait_ge(c_x_turned, n + 1)
                    if t == 0:
                        if later(b):
                            act.wait_ge(conv_done, n)
                        act.activation(x1T[0][:, :, 0:HIST], cf[:, CF_ONE:CF_ONE + DC * HIST].rearrange("p (c n) -> p c n", c=DC),
                                       ACT.Copy, scale=0.0).then_inc(c_act, 1)
                    else:
                        act.wait_ge(conv_done, n - 1)
                        act.wait_ge(c_x_copied, n)
                        act.copy(x1T[t % 2][:, :, 0:HIST], x1T[1 - t % 2][:, :, P:P + HIST]).then_inc(c_act, 1)
                    act.copy(x1T[t % 2][:, :, HIST:HIST + P], PS[4][:, :].rearrange("p (c n) -> p c n", c=DC)).then_inc(c_x_copied, 1)

                def copy_y(b, t):
                    n = b * TB + t
                    act.wait_ge(y_turned, n + 1)
                    if later(b) or t >= 2:
                        act.wait_ge(y_out[t % 2], 16 * (b * 2 + t // 2))
                    act.copy(y_row[t % 2], ybk_ps[:, :]).then_inc(y_copied, 1)

                def silu(b, t):
                    n = b * TB + t
                    act.wait_ge(c_g, n + 1)
                    if later(b, t):
                        act.wait_ge(c_gu, n)
                    act.activation(sil1, PS[0][:, :], ACT.Silu).then_inc(c_sil, 1)

                def batch(b, more):
                    for t in range(TB):
                        front = more or t < TB - 1
                        if front:
                            copy_x(*nxt_tile(b, t))
                        silu(b, t)
                        if front:
                            copy_y(*nxt_tile(b, t))
                        if t == TB - 1:
                            act.wait_ge(c_lm, b + 1)
                            act.activation(lg1[:, :, 0:E1], lg1[:, :, 0:E1], ACT.Exp).then_inc(c_exp, 1)
                copy_x(0, 0)
                copy_y(0, 0)
                batch(0, True)
                with act.Fori(1, B - 1) as b:
                    batch(b, True)
                batch(B - 1, False)

            @block.vector
            def _(dve):
                own = Chain(dve, c_dve)

                def conv(b, t):
                    n = b * TB + t
                    xs, ys = x1T[t % 2], yT[t % 2]
                    dve.wait_ge(c_x_copied, n + 1)
                    dve.wait_ge(c_act, n + 1)
                    if later(b) or t >= 2:
                        dve.wait_ge(c_u, n - 1)
                        dve.wait_ge(y_turned, n - 1)
                    for c in range(DC):
                        own.did(dve.tensor_scalar(ys[:, c, :], xs[:, c, 3:3 + P], conv_w[:, 3, c:c + 1], conv_bias[:, c:c + 1],
                                                  ALU.mult, ALU.add))
                    for k in (2, 1):
                        for c in range(DC):
                            own.wait(own.n - 3)
                            own.did(dve.scalar_tensor_tensor(ys[:, c, :], xs[:, c, k:k + P], conv_w[:, k, c:c + 1], ys[:, c, :],
                                                             ALU.mult, ALU.add))
                    for c in range(DC):
                        own.wait(own.n - 3 + c)
                        dve.scalar_tensor_tensor(ys[:, c, :], xs[:, c, 0:P], conv_w[:, 0, c:c + 1], ys[:, c, :],
                                                 ALU.mult, ALU.add).then_inc(conv_done if c == DC - 1 else c_step, 1)

                def copy_h(b, t):
                    dve.wait_ge(c_ht, b * TB + t + 1)
                    dve.tensor_copy(hT1.rearrange("p c n -> p (c n)"), PS[2][:, :]).then_inc(c_hc, 1)

                def product(b, t):
                    n = b * TB + t
                    dve.wait_ge(c_sil, n + 1)
                    dve.wait_ge(c_u, n + 1)
                    dve.tensor_tensor(gu1, sil1, PS[1][:, :], ALU.mult).then_inc(c_gu, 1)

                def residual(b, t):
                    n = b * TB + t
                    dve.wait_ge(c_d, n + 1)
                    if later(b) or t >= 2:
                        dve.wait_ge(out_out[t % 2], 16 * (b * 2 + t // 2))
                    dve.tensor_tensor(ob1[t % 2], x1[t], PS[3][:, :], ALU.add).then_inc(c_o, 1)

                def scores(b):
                    dve.wait_ge(c_log_ready, TB * (b + 1))
                    own.did(dve.tensor_tensor(lg1[:, :, 0:E1], log1[:, :, 0:E1], gb_bc.unsqueeze(1).broadcast_to([P, TB, E1]), ALU.add))
                    own.wait()
                    own.did(dve.tensor_reduce(mx1, lg1[:, :, 0:E1], AX, ALU.max))
                    own.wait()
                    dve.tensor_tensor(lg1[:, :, 0:E1], lg1[:, :, 0:E1], mx1.unsqueeze(2).broadcast_to([P, TB, E1]),
                                      ALU.subtract).then_inc(c_lm, 1)

                def choose(b):
                    dve.wait_ge(c_exp, b + 1)
                    own.did(dve.tensor_reduce(mx1, lg1[:, :, 0:E1], AX, ALU.add))
                    own.wait()
                    own.did(dve.reciprocal(mx1, mx1))
                    own.wait()
                    own.did(dve.tensor_tensor(prob[:, :, 0:E1], lg1[:, :, 0:E1], mx1.unsqueeze(2).broadcast_to([P, TB, E1]), ALU.mult))
                    own.wait()
                    own.did(dve.tensor_tensor(biased[:, :, 0:E1], prob[:, :, 0:E1], bias_bc.unsqueeze(1).broadcast_to([P, TB, E1]), ALU.add))
                    own.wait()
                    dve.sem_inc(c_step, 1)
                    for t in range(TB):
                        own.did(dve.max(top1[:, t, :], biased[:, t, :]))
                    own.wait()
                    dve.sem_inc(c_step, 1)
                    for t in range(TB):
                        own.did(dve.max_index(idx1[:, t, :], top1[:, t, :], biased[:, t, :]))
                    own.wait()
                    own.did(dve.tensor_copy(idxf1.rearrange("p (t k) -> p t k", k=K1), idx1[:, :, 0:K1]))
                    own.wait()
                    own.did(dve.tensor_tensor(oh1.rearrange("p (j e) -> p j e", e=8),
                                              cf[:, CF_I8:CF_I8 + 8].unsqueeze(1).broadcast_to([P, TB * K1, 8]),
                                              idxf1.unsqueeze(2).broadcast_to([P, TB * K1, 8]), ALU.is_equal))
                    own.wait()
                    with nc.allow_low_precision("0 or 1"):
                        dve.tensor_reduce(sel1, oh1.rearrange("p (t k e) -> p t e k", k=K1, e=8), AX, ALU.add).then_inc(c_sel, 1)
                    ohv1 = oh1.rearrange("p (t k e) -> p t k e", k=K1, e=8)
                    prv1 = prod1.rearrange("p (t k e) -> p t k e", k=K1, e=8)
                    own.did(dve.tensor_tensor(prv1, ohv1, prob.unsqueeze(2).broadcast_to([P, TB, K1, 8]), ALU.mult))
                    own.wait()
                    own.did(dve.tensor_reduce(pk1, prod1.rearrange("p (j e) -> p j e", e=8), AX, ALU.add))
                    own.wait()
                    own.did(dve.tensor_reduce(s3, pk1.rearrange("p (t k) -> p t k", k=K1), AX, ALU.add))
                    own.wait()
                    own.did(dve.reciprocal(s3, s3))
                    own.wait()
                    if later(b):
                        dve.wait_ge(c_scat_done, 16 * TB * K1 * b)
                    pv = pairs1.rearrange("p (t k w) -> p t k w", k=K1, w=2)
                    own.did(dve.tensor_tensor(pv[:, :, :, 1], pk1.rearrange("p (t k) -> p t k", k=K1),
                                              s3.unsqueeze(2).broadcast_to([P, TB, K1]), ALU.mult))
                    own.did(dve.tensor_copy(pv[:, :, :, 0].bitcast(I32), ci[:, bass.ds(b * TB + CI_TOK, TB)]
                                            .unsqueeze(2).broadcast_to([P, TB, K1])))

                def place(b):
                    dve.wait_ge(c_pos, b + 1)
                    own.did(dve.tensor_reduce(seltot1, sel1.rearrange("p t e -> p e t"), AX, ALU.add))
                    own.did(dve.tensor_tensor(prod1.rearrange("p (t k e) -> p t k e", k=K1, e=8),
                                              oh1.rearrange("p (t k e) -> p t k e", k=K1, e=8),
                                              pos1_ps[:, 0:TB * 8].rearrange("p (t e) -> p t e", e=8).unsqueeze(2)
                                              .broadcast_to([P, TB, K1, 8]), ALU.mult))
                    own.wait()
                    own.did(dve.tensor_tensor(carry1, carry1, seltot1, ALU.add))
                    own.did(dve.tensor_reduce(pp1, prod1.rearrange("p (j e) -> p j e", e=8), AX, ALU.add))
                    own.wait()
                    own.did(dve.tensor_copy(posi, pp1))
                    own.wait()
                    own.did(dve.tensor_scalar(hi_i, posi, 7, None, ALU.logical_shift_right))
                    own.did(dve.tensor_scalar(lo_i, posi, P - 1, None, ALU.bitwise_and))
                    own.wait()
                    own.did(dve.tensor_copy(hi_f, hi_i))
                    own.did(dve.tensor_copy(lo_f, lo_i))
                    own.wait()
                    own.did(dve.scalar_tensor_tensor(hi_f, idxf1, float(TT), hi_f, ALU.mult, ALU.add))
                    own.wait()
                    dve.scalar_tensor_tensor(dest1, lo_f, float(COLS1), hi_f, ALU.mult, ALU.add).then_inc(c_scat, 1)

                def batch(b, more):
                    for t in range(TB):
                        if t == TB - 1:
                            scores(b)
                        if t >= 2:
                            residual(b, t - 2)
                        elif later(b):
                            residual(b - 1, TB - 2 + t)
                        if more or t < TB - 1:
                            conv(*nxt_tile(b, t))
                        if t:
                            copy_h(b, t - 1)
                        elif later(b):
                            copy_h(b - 1, TB - 1)
                        product(b, t)
                        if t == TB - 1:
                            choose(b)
                            place(b)
                own.did(dve.memset(prob, 0.0))
                own.did(dve.memset(biased, -1.0e30))
                own.did(dve.memset(carry1, 0.0))
                dve.wait_ge(small_in, 80)
                own.wait()
                conv(0, 0)
                batch(0, True)
                with dve.Fori(1, B - 1) as b:
                    own.loop(b, PER_BATCH_C, 1)
                    own.wait()
                    batch(b, True)
                    own.end(B - 2)
                batch(B - 1, False)
                residual(B - 1, TB - 2)
                copy_h(B - 1, TB - 1)
                residual(B - 1, TB - 1)

            @block.tensor
            def _(pe):
                def turn_x(b, t):
                    n = b * TB + t
                    pe.wait_ge(x1_in[t], 16 * (b + 1))
                    if later(b, t):
                        pe.wait_ge(c_x_copied, n)
                    for c in range(DC):
                        mm = pe.transpose(PS[4][:, c * P:(c + 1) * P], x1[t][:, c:D:DC], ident)
                    mm.then_inc(c_x_turned, 1)

                def logits_and_rows(b, t):
                    n = b * TB + t
                    pe.wait_ge(conv_done, n + 1)
                    if t == 0 and later(b):
                        pe.wait_ge(c_lm, b)
                    for c in range(DC):
                        mm = pe.matmul(log1[:, t, 0:E1], yT[t % 2][:, c, :], gate1_w[:, c, :], start=c == 0, stop=c == DC - 1)
                    mm.then_inc(c_log_ready, 1)
                    if later(b, t):
                        pe.wait_ge(y_copied, n)
                    for c in range(DC):
                        mm = pe.transpose(ybk_ps[:, c:D:DC], yT[t % 2][:, c, :], ident)
                    mm.then_inc(y_turned, 1)

                def products(b, t, m, bank, done, free):
                    n = b * TB + t
                    if later(b, t):
                        pe.wait_ge(free, n)
                    for c in range(DC):
                        mm = pe.matmul(bank[:, :], yT[t % 2][:, c, :], arena[:, 6 * SLOT + (m * DC + c) * D:6 * SLOT + (m * DC + c + 1) * D],
                                       start=c == 0, stop=c == DC - 1)
                    mm.then_inc(done, 1)

                def turn_h(b, t):
                    n = b * TB + t
                    pe.wait_ge(c_gu, n + 1)
                    if later(b, t):
                        pe.wait_ge(c_hc, n)
                    for c in range(DC):
                        mm = pe.transpose(PS[2][:, c * P:(c + 1) * P], gu1[:, c:D:DC], ident)
                    mm.then_inc(c_ht, 1)

                def down(b, t):
                    n = b * TB + t
                    pe.wait_ge(c_hc, n + 1)
                    if later(b, t):
                        pe.wait_ge(c_o, n)
                    for c in range(DC):
                        mm = pe.matmul(PS[3][:, :], hT1[:, c, :], arena[:, 6 * SLOT + (2 * DC + c) * D:6 * SLOT + (2 * DC + c + 1) * D],
                                       start=c == 0, stop=c == DC - 1)
                    mm.then_inc(c_d, 1)

                def positions(b):
                    pe.wait_ge(c_sel, b + 1)
                    for t in range(TB):
                        to = pos1_ps[:, t * 8:(t + 1) * 8]
                        pe.matmul(to, trib, sel1[:, t, :], start=True, stop=False)
                        for s in range(t):
                            pe.matmul(to, onesb, sel1[:, s, :], start=False, stop=False)
                        mm = pe.matmul(to, onesb, carry1, start=False, stop=True)
                    mm.then_inc(c_pos, 1)

                def batch(b, more, first=False):
                    for t in range(TB):
                        prev = None if first and t == 0 else ((b, t - 1) if t else (b - 1, TB - 1))
                        if more or t < TB - 1:
                            turn_x(*nxt_tile(b, t))
                        products(b, t, 0, PS[0], c_g, c_sil)
                        if prev:
                            turn_h(*prev)
                        products(b, t, 1, PS[1], c_u, c_gu)
                        if more or t < TB - 1:
                            logits_and_rows(*nxt_tile(b, t))
                        if prev:
                            down(*prev)
                        if t == TB - 1:
                            positions(b)
                pe.wait_ge(small_in, 80)
                turn_x(0, 0)
                logits_and_rows(0, 0)
                batch(0, True, True)
                with pe.Fori(1, B - 1) as b:
                    batch(b, True)
                batch(B - 1, False)
                turn_h(B - 1, TB - 1)
                down(B - 1, TB - 1)

        n_e = take(misc, M2, 8)
        nf = take(misc, M2 + 8, 8)
        ni = take(misc, M2 + 16, 8, I32)
        tiles_e = take(misc, M2 + 24, 8)
        ends = take(misc, M2 + 32, 8)
        past = take(misc, M2 + 40, TILES1 * E1).rearrange("p (j e) -> p j e", e=E1)
        past_n = take(misc, M2 + 420, TILES1 * E1).rearrange("p (j e) -> p j e", e=E1)
        tile_e = take(misc, M5, TILES1)
        tile_b = take(misc, M5 + 54, TILES1)
        expert_i = take(misc, M5 + 108, TILES1, I32)
        column_i = take(misc, M5 + 162, TILES1, I32)
        M6 = M5 + 216
        w56_in, table1_in, l_pe, l_dve = sem("w56_in"), sem("table1_in"), sem("l_pe"), sem("l_dve")
        with nc.Block() as block:
            @block.sync
            def _(sp):
                sp.dma_start(take(misc, M6, 2 * COLS1), slots1.rearrange("(p c) w -> p (c w)", p=P)).then_inc(table1_in, 16)
                sp.dma_start(arena[:, 5 * SLOT:7 * SLOT], w_res[:, 6 * SLOT:8 * SLOT]).then_inc(w56_in, 16)
                sp.wait_ge(table1_in, 16)

            @block.tensor
            def _(pe):
                pe.matmul(PS[7][:, 0:8], onesb, carry1, start=True, stop=True).then_inc(l_pe, 1)

            @block.vector
            def _(dve):
                own = Chain(dve, l_dve)

                def step(ins):
                    own.did(ins)
                    own.wait()
                dve.wait_ge(l_pe, 1)
                step(dve.tensor_scalar(n_e, PS[7][:, 0:8], float(P - 1), None, ALU.add))
                step(dve.tensor_copy(ni, n_e))
                step(dve.tensor_scalar(ni, ni, 7, None, ALU.logical_shift_right))
                step(dve.tensor_copy(tiles_e, ni))
                step(dve.tensor_copy(ends, tiles_e))
                for e in range(1, E1):
                    step(dve.tensor_tensor(ends[:, e:e + 1], ends[:, e - 1:e], tiles_e[:, e:e + 1], ALU.add))
                step(dve.tensor_tensor(past, cf[:, CF_J:CF_J + TILES1].unsqueeze(2).broadcast_to([P, TILES1, E1]),
                                       ends[:, 0:E1].unsqueeze(1).broadcast_to([P, TILES1, E1]), ALU.is_ge))
                step(dve.tensor_tensor(past_n, past, tiles_e[:, 0:E1].unsqueeze(1).broadcast_to([P, TILES1, E1]), ALU.mult))
                step(dve.tensor_reduce(tile_e, past, AX, ALU.add))
                step(dve.tensor_reduce(tile_b, past_n, AX, ALU.add))
                step(dve.tensor_tensor(tile_b, cf[:, CF_J:CF_J + TILES1], tile_b, ALU.subtract))
                step(dve.scalar_tensor_tensor(tile_b, tile_e, float(TT), tile_b, ALU.mult, ALU.add))
                step(dve.tensor_scalar(column_i, tile_b, float(BINS), None, ALU.min))
                step(dve.tensor_scalar(expert_i, tile_e, float(E1 - 1), None, ALU.min))

        expert_stage("e1", TILES1, D, [(0, P)] * DC, F32, y_rows, slots1, COLS1, out, M3, M6, None,
                     (column_i, expert_i), w56_in)


def layout(inputs):
    import numpy as np
    g = {k: np.asarray(v) for k, v in inputs.items()}
    sg, su = g["L0_ffn_sh_gate"].T, g["L0_ffn_sh_up"].T
    cf = np.zeros((P, NCF), np.float32)
    cf[:, CF_ID:CF_ID + P] = np.eye(P)
    cf[:, CF_ONE:CF_ONE + P] = 1
    cf[:, CF_TRI:CF_TRI + P] = np.triu(np.ones((P, P)), 1)
    cf[:, CF_BIT:CF_BIT + STEPS] = [-1.0] + [2.0 ** (30 - i) for i in range(31)]
    cf[:, CF_I64:CF_I64 + E0] = np.arange(E0)
    cf[:, CF_J:CF_J + TILES1] = np.arange(TILES1)
    cf[:, CF_I8:CF_I8 + 8] = np.arange(8)
    cf[:, CF_HALF:CF_HALF + P] = -0.5
    ci = np.zeros((P, 49), np.int32)
    ci[:, CI_BIT:CI_BIT + STEPS] = [2 ** (30 - i) for i in range(31)] + [0]
    ci[:, CI_TOK:CI_TOK + TT] = np.arange(T).reshape(TT, P).T
    ci[:, CI_PAD] = T + np.arange(P)
    routed = [g["L1_ffn_W1"], g["L1_ffn_Wg"], g["L1_ffn_W2"]]
    experts = [[w[e] for w in routed] for e in range(E1)]
    experts.insert(3, [g["L1_ffn_Ws1"], g["L1_ffn_Wsg"], g["L1_ffn_Ws2"]])
    w_res = np.concatenate([w.reshape(P, DC * D) for e in experts for w in e], 1)
    return {
        "x": g["x"].reshape(T, D), "fside": g["fside_BxSx1_0"].reshape(TT, P).T, "cond": g["cond_2048"],
        "gate0": g["L0_ffn_gate_w"].T, "w_gate": g["L0_ffn_w_gate"], "w_up": g["L0_ffn_w_up"],
        "w_down": g["L0_ffn_w_down"],
        "sh_in": np.concatenate([sg[:, :F0], su[:, :F0], sg[:, F0:], su[:, F0:]], 1),
        "sh_down": g["L0_ffn_sh_down"].T, "conv_b": g["L1_cond_b"], "w_res": w_res,
        "gate1": g["L1_ffn_gate_w"], "gate1_b": g["L1_ffn_gate_b"], "biases": g["L1_ffn_biases"],
        "c_f32": cf, "c_i32": ci,
    }


def kernel(**inputs):
    import numpy as np
    import concourse.bacc as bacc
    from concourse.bass_utils import run_bass_kernel_spmd

    arrays = {n: np.ascontiguousarray(a) for n, a in layout(inputs).items()}
    nc = bacc.Bacc("TRN2", target_bir_lowering=False, num_devices=1)
    args = {n: nc.dram_tensor(f"in_{n}", a.shape, mybir.dt.from_np(a.dtype), kind="ExternalInput").ap()
            for n, a in arrays.items()}
    result = nc.dram_tensor("out_rows", (T + P, D), F32, kind="ExternalOutput").ap()
    build(nc, out=result, **args)
    ran = run_bass_kernel_spmd(nc, [{f"in_{n}": a for n, a in arrays.items()}], core_ids=[0])
    return ran.results[0]["out_rows"][:T].reshape(B, S, D)
```

```python
from contextlib import ExitStack

import concourse.bass as bass
from concourse import mybir

ALU = mybir.AluOpType
ACT = mybir.ActivationFunctionType
AX = mybir.AxisListType.X
F32, F32R, BF16 = mybir.dt.float32, mybir.dt.float32r, mybir.dt.bfloat16
I32, U32 = mybir.dt.int32, mybir.dt.uint32

P = 128
B, S, D = 4, 512, 512
T = B * S
TB = S // P
TT = T // P
DC = D // P
KEEP = 5120
E0, K0, F0, CAP = 64, 6, 352, 128
HALVES = 2
F0C = [(0, 128), (128, 128), (256, 96)]
E1, K1 = 7, 3
BINS = E1 * TT
COLS1 = BINS + 1
TILES1 = T * K1 // P + E1 - 1
STEPS = 32
DIAG = -3.0e38
INV_SQRT_N = 0.04419417306780815
OUT_OF_BOUNDS = 1.0e6
COARSE, FINE = 1152, 896
ABOVE = 1.0 + 2.0 ** -10
PER_BATCH = 38
PER_BATCH_C = 80

CF_ID, CF_ONE, CF_TRI, CF_BIT, CF_I64 = 0, 128, 256, 384, 416
CF_J, CF_I8 = 480, 480 + TILES1
CF_HALF = CF_I8 + 8
NCF = CF_HALF + P
CI_BIT, CI_TOK, CI_PAD = 0, 32, 48


class Chain:

    def __init__(self, eng, sem):
        self.eng, self.sem, self.n, self.i, self.per = eng, sem, 0, None, 0

    def did(self, ins):
        ins.then_inc(self.sem, 1)
        self.n += 1
        return self.n

    def at(self, n):
        return n if self.i is None else self.i * self.per + n

    def wait(self, n=None):
        self.eng.wait_ge(self.sem, self.at(self.n if n is None else n))

    def loop(self, i, per, first=0):
        self.start, self.i, self.per, self.first = self.n, i, per, first
        self.n = self.start - first * per

    def end(self, count):
        assert self.n == self.start - self.first * self.per + self.per, (self.n, self.start, self.per)
        self.i, self.n = None, self.start + count * self.per


def build(nc, x, fside, cond, gate0, w_gate, w_up, w_down, sh_in, sh_down, conv_b, w_res,
          gate1, gate1_b, biases, c_f32, c_i32, out):
    with ExitStack() as ctx:
        def sb(name, shape, dt=F32, till=ctx):
            return till.enter_context(nc.sbuf_tensor(name, shape, dt))

        def sem(name):
            return ctx.enter_context(nc.semaphore(name))

        def dram(name, shape, dt=F32):
            return nc.dram_tensor(name, shape, dt, kind="Internal").ap()

        mask_rows = dram("mask_rows", (T + P, D), BF16)
        acc0 = dram("acc0", (T + P, D))
        y_rows = dram("y_rows", (T + P, D))
        slots0 = dram("slots0", (P * E0, 2))
        slots1 = dram("slots1", (P * COLS1, 2))

        SLOT = 3 * DC * D
        misc = sb("misc", [P, 9000])
        cf = sb("cf", [P, NCF])
        cb = sb("cb", [P, 384], BF16)
        ci = sb("ci", [P, 49], I32)
        early = ctx.enter_context(ExitStack())
        front = sb("front", [P, 8192 + 6 * D + DC * E0 + 15488], till=early)
        sh_parts = sb("sh_parts", [P, 2 * DC * 4 * F0], F32R, till=early)
        mask_cols = sb("mask_cols", [P, TB * DC * P], F32R, till=early)
        PS = [ctx.enter_context(nc.psum_tensor(f"ps{i}", [P, 512], F32)) for i in range(8)]

        ident, ones, tri = cf[:, CF_ID:CF_ID + P], cf[:, CF_ONE:CF_ONE + P], cf[:, CF_TRI:CF_TRI + P]
        identb, trib, onesb = (cb[:, c:c + P] for c in (CF_ID, CF_TRI, CF_ONE))

        def take(region, at, words, dt=F32):
            v = region[:, at:at + words]
            return v if dt == F32 else v.bitcast(dt)

        def later(b, t=0):
            return t > 0 or not isinstance(b, int) or b > 0

        val = take(front, 0, TT * S)
        sh_dw = take(front, TT * S, 6 * D).rearrange("p (c n) -> p c n", c=6)
        gate0_w = take(front, TT * S + 6 * D, DC * E0).rearrange("p (c e) -> p c e", c=DC)
        A2 = TT * S + 6 * D + DC * E0
        junk = take(front, A2, 1024, BF16)
        junk_a = take(front, A2 + 1024, 1024, BF16)
        cond_bc = take(front, A2 + 2048, B * S)
        val16 = take(front, A2 + 4096, TT * S // 2, BF16)
        sh_w = take(front, A2 + 8192, DC * 4 * F0).rearrange("p (c f) -> p c f", c=DC)
        sh_hi, sh_lo = (sh_parts[:, i * DC * 4 * F0:(i + 1) * DC * 4 * F0].rearrange("p (c f) -> p c f", c=DC)
                        for i in range(2))

        gate0_parts = take(misc, 8192, 3 * DC * E0 // 2, BF16).rearrange("p (k c e) -> p k c e", k=3, c=DC)
        gate0_left = take(misc, 8192 + 3 * DC * E0 // 2, DC * E0).rearrange("p (c e) -> p c e", c=DC)

        fs = take(misc, 0, TT)
        rmax = take(misc, 16, TT)
        nmax = take(misc, 32, TT)
        esum = take(misc, 48, TT)
        rsum = take(misc, 64, TT)
        fac = take(misc, 80, TT)
        cnt = take(misc, 96, B)
        cand = take(misc, 100, B, I32)
        incr = take(misc, 104, B, I32)
        candf = take(misc, 100, B)
        cand16 = candf.bitcast(BF16)[:, 1:2 * B:2]
        cnt_a = take(misc, 340 + D, B)
        step_f = take(misc, 348 + D, B)
        step_i = take(misc, 352 + D, B, I32)
        empty = take(misc, 110, COLS1 * 2, I32).rearrange("p (c w) -> p c w", w=2)
        MZ = 110 + COLS1 * 2
        zeros = take(misc, MZ, D)
        M2 = MZ + D + 20
        assert MZ == 336

        x_t = x.rearrange("(t p) d -> p t d", p=P)
        x_in = [sem(f"x_in{b}") for b in range(B)]
        const_in, side_in, shw_in, init_out = sem("const_in"), sem("side_in"), sem("shw_in"), sem("init_out")
        empty_ready, cand_ready, counted_a, halved = sem("empty_ready"), sem("cand_ready"), sem("counted_a"), sem("halved")
        max_ready, exp_ready, scored, diag_set = sem("max_ready"), sem("exp_ready"), sem("scored"), sem("diag_set")
        counted, totalled, split = sem("counted"), sem("totalled"), sem("split")
        dve_did = sem("dve_did")

        with nc.Block() as block:
            @block.sync
            def _(sp):
                for b in range(B):
                    sp.dma_start(val[:, b * TB * S:(b + 1) * TB * S].rearrange("p (t d) -> p t d", t=TB),
                                 x_t[:, b * TB:(b + 1) * TB, :]).then_inc(x_in[b], 16)
                    if b == 0:
                        sp.dma_start(cf[:, :], c_f32).then_inc(const_in, 16)
                        sp.dma_start(ci[:, :], c_i32).then_inc(const_in, 16)
                        sp.dma_start(fs, fside).then_inc(side_in, 16)
                        sp.dma_start(cond_bc, cond.rearrange("b d -> (b d)").partition_broadcast(P)).then_inc(side_in, 16)
                sp.dma_start(sh_w, sh_in.rearrange("(p c) f -> p c f", c=DC)).then_inc(shw_in, 16)
                for h in range(HALVES):
                    sp.dma_start(sh_dw[:, 3 * h:3 * h + 2, :],
                                 sh_down[h * F0:h * F0 + 256, :].rearrange("(c p) n -> p c n", p=P)).then_inc(shw_in, 16)
                    sp.dma_start(sh_dw[0:96, 3 * h + 2, :], sh_down[h * F0 + 256:(h + 1) * F0, :]).then_inc(shw_in, 16)
                sp.dma_start(gate0_w, gate0.rearrange("(p c) e -> p c e", c=DC)).then_inc(shw_in, 16)
                sp.wait_ge(shw_in, 96)
                sp.wait_ge(empty_ready, 3)
                sp.dma_start(slots0.rearrange("(p c) w -> p (c w)", p=P), empty[:, 0:E0, :].rearrange("p c w -> p (c w)")
                             .bitcast(F32)).then_inc(init_out, 16)
                sp.dma_start(slots1.rearrange("(p c) w -> p (c w)", p=P), empty.rearrange("p c w -> p (c w)")
                             .bitcast(F32)).then_inc(init_out, 16)
                sp.dma_start(mask_rows[T:T + P, :], zeros[:, 0:D // 2].bitcast(BF16)).then_inc(init_out, 16)
                for rows in (acc0, y_rows, out):
                    sp.dma_start(rows[T:T + P, :], zeros).then_inc(init_out, 16)
                sp.wait_ge(init_out, 96)

            @block.vector
            def _(dve):
                own = Chain(dve, dve_did)
                dve.memset(zeros, 0.0).then_inc(empty_ready, 1)
                dve.memset(empty[:, :, 1], 0).then_inc(empty_ready, 1)
                own.did(dve.memset(cand, 0))
                dve.wait_ge(const_in, 32)
                own.did(dve.tensor_copy(cb[:, :], cf[:, 0:3 * P]))
                dve.tensor_copy(empty[:, :, 0], ci[:, CI_PAD:CI_PAD + 1].broadcast_to([P, COLS1])).then_inc(empty_ready, 1)

                def maxima(b):
                    t4 = slice(b * TB, (b + 1) * TB)
                    dve.wait_ge(x_in[b], 16)
                    own.did(dve.tensor_reduce(rmax[:, t4], val[:, b * TB * S:(b + 1) * TB * S]
                                              .rearrange("p (t d) -> p t d", t=TB), AX, ALU.max))
                    own.wait()
                    dve.tensor_scalar(nmax[:, t4], rmax[:, t4], -1.0, None, ALU.mult).then_inc(max_ready, 1)

                def score(b):
                    t4 = slice(b * TB, (b + 1) * TB)
                    dve.wait_ge(exp_ready, TB * (b + 1))
                    own.did(dve.reciprocal(rsum[:, t4], esum[:, t4]))
                    own.wait()
                    own.did(dve.tensor_scalar(rsum[:, t4], rsum[:, t4], INV_SQRT_N, None, ALU.mult))
                    own.wait()
                    own.did(dve.tensor_tensor(fac[:, t4], rsum[:, t4], fs[:, t4], ALU.mult))
                    own.wait()
                    for t in range(b * TB, (b + 1) * TB):
                        v = val[:, t * S:(t + 1) * S]
                        dve.scalar_tensor_tensor(v, v, fac[:, t:t + 1], cond_bc[:, b * S:(b + 1) * S],
                                                 ALU.mult, ALU.mult).then_inc(scored, 1)
                maxima(0)
                dve.wait_ge(side_in, 32)
                for b in range(1, B):
                    maxima(b)
                    score(b - 1)
                score(B - 1)

                def count(b, i, coarse):
                    if later(i, b):
                        dve.wait_ge(counted, 4 * i + b)
                    own_, at, n = (val16, cand16, COARSE) if coarse else (val, candf, FINE)
                    dve.tensor_scalar(junk[:, 0:n], own_[:, b * TB * S:b * TB * S + n], at[:, b:b + 1], 0.0,
                                      ALU.is_ge, ALU.add, accum_out=cnt[:, b:b + 1]).then_inc(counted, 1)

                def judge(c, i, coarse):
                    dve.wait_ge(totalled, 4 * i + c + 2)
                    signs = TB * S - (COARSE if coarse else FINE)
                    own.did(dve.tensor_scalar(incr[:, c:c + 2], PS[c // 2][:, c:c + 2], KEEP - 0.5 - signs * P / 2,
                                              cf[:, bass.ds(i + CF_BIT, 1)], ALU.is_lt, ALU.mult))

                def next_bit(c, i):
                    own.wait()
                    dve.scalar_tensor_tensor(cand[:, c:c + 2], incr[:, c:c + 2], ci[:, bass.ds(i + CI_BIT, 1)],
                                             cand[:, c:c + 2], ALU.bitwise_xor, ALU.bitwise_xor).then_inc(cand_ready, 1)

                def rounds(i, coarse, before):
                    dve.wait_ge(cand_ready, 2 * i)
                    count(0, i, coarse)
                    judge(2, i - 1, before)
                    count(1, i, coarse)
                    next_bit(2, i - 1)
                    dve.wait_ge(cand_ready, 2 * i + 1)
                    count(2, i, coarse)
                    judge(0, i, coarse)
                    count(3, i, coarse)
                    next_bit(0, i)

                dve.sem_inc(cand_ready, 1)
                for b in range(B):
                    dve.wait_ge(halved, b + 1)
                    count(b, 0, True)
                judge(0, 0, True)
                next_bit(0, 0)
                HALF = STEPS // 2
                rounds(1, True, True)
                with dve.Fori(1, HALF // 2) as j:
                    own.loop(j, 4, 1)
                    rounds(2 * j, True, True)
                    rounds(2 * j + 1, True, True)
                    own.end(HALF // 2 - 1)
                rounds(HALF, False, True)
                rounds(HALF + 1, False, False)
                with dve.Fori(HALF // 2 + 1, STEPS // 2) as j:
                    own.loop(j, 4, HALF // 2 + 1)
                    rounds(2 * j, False, False)
                    rounds(2 * j + 1, False, False)
                    own.end(HALF // 2 - 1)
                judge(2, STEPS - 1, False)
                next_bit(2, STEPS - 1)
                dve.wait_ge(cand_ready, 2 * STEPS + 1)
                own.did(dve.tensor_scalar(step_f, candf, 0.0, -2.0, ALU.is_lt, ALU.mult))
                own.wait()
                own.did(dve.tensor_scalar(step_f, step_f, 1.0, None, ALU.add))
                own.wait()
                own.did(dve.tensor_copy(step_i, step_f))
                own.wait()
                own.did(dve.tensor_tensor(cand, cand, step_i, ALU.add))
                own.wait()
                for b in range(B):
                    dve.wait_ge(counted, B * STEPS + b)
                    dve.tensor_scalar(junk[:, 0:TB * S], val[:, b * TB * S:(b + 1) * TB * S], candf[:, b:b + 1], 0.0,
                                      ALU.is_ge, ALU.add, accum_out=cnt[:, b:b + 1]).then_inc(counted, 1)
                for c in (0, 2):
                    dve.wait_ge(totalled, 4 * STEPS + c + 2)
                    own.did(dve.tensor_scalar(step_f[:, c:c + 2], PS[c // 2][:, c:c + 2], float(KEEP), None, ALU.is_lt))
                own.wait()
                own.did(dve.scalar_tensor_tensor(step_f, step_f, -1.0, step_i, ALU.mult, ALU.mult))
                own.wait()
                own.did(dve.tensor_copy(step_i, step_f))
                own.wait()
                own.did(dve.tensor_tensor(cand, cand, step_i, ALU.add))
                own.wait()

            @block.scalar
            def _(act):
                for b in range(B):
                    act.wait_ge(max_ready, b + 1)
                    for t in range(b * TB, (b + 1) * TB):
                        v = val[:, t * S:(t + 1) * S]
                        act.activation(v, v, ACT.Exp, bias=nmax[:, t:t + 1], accum_out=esum[:, t:t + 1]).then_inc(exp_ready, 1)
                upper = val.bitcast(BF16)[:, 1:2 * TT * S:2]
                for b in range(B):
                    c = slice(b * TB * S, (b + 1) * TB * S)
                    act.wait_ge(diag_set, b + 1)
                    act.copy(val16[:, c], upper[:, c]).then_inc(halved, 1)

                def count(b, i, coarse):
                    if b % 2 == 0:
                        act.wait_ge(cand_ready, 2 * i + b // 2 if later(i) else 1)
                    if later(i, b):
                        act.wait_ge(counted_a, 4 * i + b)
                    if later(i):
                        act.wait_ge(totalled, 4 * (i - 1) + b + 1)
                    own_, n = (val16, COARSE) if coarse else (val, FINE)
                    act.activation(junk_a[:, 0:TB * S - n], own_[:, b * TB * S + n:(b + 1) * TB * S], ACT.Sign,
                                   scale=-ABOVE if coarse else -1.0, bias=candf[:, b:b + 1], accum_out=cnt_a[:, b:b + 1]).then_inc(counted_a, 1)
                act.wait_ge(halved, B)
                for b in range(B):
                    count(b, 0, True)
                for b in range(B):
                    count(b, 1, True)
                for first, last, coarse in ((1, STEPS // 4, True), (STEPS // 4, STEPS // 2, False)):
                    with act.Fori(first, last) as j:
                        for u in range(2):
                            for b in range(B):
                                count(b, 2 * j + u, coarse)

            @block.gpsimd
            def _(pool):
                for b in range(B):
                    pool.wait_ge(scored, TB * (b + 1))
                    v = val[:, b * TB * S:(b + 1) * TB * S].rearrange("p (t d) -> p t d", t=TB)
                    pool.affine_select(out=v, in_=v, compare_op=ALU.not_equal, fill=DIAG, base=0,
                                       pattern=[[P, TB], [-1, S]], channel_multiplier=1).then_inc(diag_set, 1)
                pool.wait_ge(shw_in, 96)
                pool.tensor_copy(sh_hi, sh_w).then_inc(split, 1)
                pool.wait_ge(split, 1)
                pool.tensor_tensor(sh_lo, sh_w, sh_hi, ALU.subtract).then_inc(split, 1)
                pool.tensor_copy(gate0_parts[:, 0], gate0_w).then_inc(split, 1)
                pool.wait_ge(split, 3)
                pool.tensor_tensor(gate0_left, gate0_w, gate0_parts[:, 0], ALU.subtract).then_inc(split, 1)
                pool.wait_ge(split, 4)
                pool.tensor_copy(gate0_parts[:, 1], gate0_left).then_inc(split, 1)
                pool.wait_ge(split, 5)
                pool.tensor_tensor(gate0_left, gate0_left, gate0_parts[:, 1], ALU.subtract).then_inc(split, 1)
                pool.wait_ge(split, 6)
                pool.tensor_copy(gate0_parts[:, 2], gate0_left).then_inc(split, 1)

            @block.tensor
            def _(pe):
                half = cf[:, CF_HALF:CF_HALF + P]

                def total(b, i):
                    pe.wait_ge(counted, 4 * i + b + 1)
                    pe.matmul(PS[b // 2][:, b:b + 1], ones, cnt[:, b:b + 1], start=True, stop=False)
                    pe.wait_ge(counted_a, 4 * i + b + 1)
                    pe.matmul(PS[b // 2][:, b:b + 1], half, cnt_a[:, b:b + 1], start=False, stop=True).then_inc(totalled, 1)
                pe.wait_ge(const_in, 32)
                for i in range(2):
                    for b in range(B):
                        total(b, i)
                with pe.Fori(1, STEPS // 2) as j:
                    for u in range(2):
                        for b in range(B):
                            total(b, 2 * j + u)
                for b in range(B):
                    pe.wait_ge(counted, 4 * STEPS + b + 1)
                    pe.matmul(PS[b // 2][:, b:b + 1], ones, cnt[:, b:b + 1], start=True, stop=True).then_inc(totalled, 1)

        xTn = take(front, A2, TB * DC * P // 2, BF16)
        xT = mask_cols
        ge = take(front, A2 + 2048, TB * S)
        eq = take(front, A2 + 4096, TB * S)
        cum = take(front, A2 + 6144, TB * S)
        mask = take(front, A2 + 8192, TB * S // 2, BF16)
        oh = take(front, A2 + 9216, TB * K0 * E0)
        prod = take(front, A2 + 10752, TB * K0 * E0)
        x_res = [take(front, A2 + 12288 + i * D, D) for i in range(2)]
        ob = [take(front, A2 + 13312 + i * D, D) for i in range(2)]
        sil = take(front, A2 + 14336, F0)
        gu = take(front, A2 + 14720, F0)
        hT = take(front, A2 + 15104, 384).rearrange("p (c n) -> p c n", c=3)
        gecnt = take(misc, M2, 1)
        rc = take(misc, M2 + 4, TB)
        rcex = take(misc, M2 + 8, 5)
        lim = take(misc, M2 + 16, 5)
        top = take(misc, M2 + 24, TB * 8).rearrange("p (t k) -> p t k", k=8)
        idx = take(misc, M2 + 56, TB * 8, U32).rearrange("p (t k) -> p t k", k=8)
        idxf = take(misc, M2 + 88, TB * K0)
        es = take(misc, M2 + 112, TB)
        td = take(misc, M2 + 116, TB * 8).rearrange("p (t k) -> p t k", k=8)
        posk = take(misc, M2 + 148, TB * K0)
        over = take(misc, M2 + 172, TB * K0)
        dest = take(misc, M2 + 196, TB * K0, I32)
        pairs = take(misc, M2 + 220, TB * K0 * 2)
        lm = take(misc, M2 + 268, TB * E0).rearrange("p (t e) -> p t e", e=E0)
        selb = take(misc, M2 + 524, TB * E0 // 2, BF16).rearrange("p (t e) -> p t e", e=E0)
        carry = take(misc, M2 + 652, E0 // 2, BF16)
        seltot = take(misc, M2 + 684, E0)
        M3 = M2 + 748

        names = ("g_ready sil_ready u_ready gu_ready t_ready ht_ready d_ready o_ready tie_in tie_ready mask_ready "
                 "xt_ready xtn_ready xt_moved log_ready lm_ready exp_done sel_ready pos_ready scat_ready scat_done "
                 "mask_out pool_step dve_step dve2")
        (g_ready, sil_ready, u_ready, gu_ready, t_ready, ht_ready, d_ready, o_ready, tie_in, tie_ready, mask_ready,
         xt_ready, xtn_ready, xt_moved, log_ready, lm_ready, exp_done, sel_ready, pos_ready, scat_ready, scat_done,
         mask_out, pool_step, dve_step, dve2) = (sem(n) for n in names.split())
        o_out = [sem(f"o_out{i}") for i in range(2)]
        xr_in = [sem(f"xr_in{i}") for i in range(2)]
        gate_ps, up_ps, t_ps, d_ps, xt_ps, tie_ps, log_ps, pos_ps = PS
        xt_psb = xt_ps[:, 0:DC * P // 2].bitcast(BF16)
        ITEMS = TB * HALVES
        acc0_t = acc0[0:T].rearrange("(t p) d -> t p d", p=P)
        x_tp = x.rearrange("(t p) d -> t p d", p=P)
        mask_bt = mask_rows[0:T].rearrange("(b t p) d -> b p t d", p=P, t=TB)

        with nc.Block() as block:
            @block.sync
            def _(sp):
                def load_x(b, t):
                    sp.dma_start(x_res[t % 2], x_tp[b * TB + t]).then_inc(xr_in[t % 2], 16)

                def mask_store(b):
                    sp.wait_ge(mask_ready, b + 1)
                    sp.dma_start(mask_bt[b], mask.rearrange("p (t d) -> p t d", t=TB)).then_inc(mask_out, 16)

                def batch(b, more):
                    for t in range(TB):
                        if t == 2 and more:
                            mask_store(b + 1)
                        sp.wait_ge(o_ready, b * TB + t + 1)
                        sp.dma_start(acc0_t[b * TB + t], ob[t % 2]).then_inc(o_out[t % 2], 16)
                        if t < 2 or more:
                            load_x(b if t < 2 else b + 1, (t + 2) % TB)
                load_x(0, 0)
                load_x(0, 1)
                mask_store(0)
                batch(0, True)
                with sp.Fori(1, B - 1) as i:
                    batch(i, True)
                batch(B - 1, False)
                sp.wait_ge(mask_out, 16 * B)
                for i in range(2):
                    sp.wait_ge(o_out[i], 16 * TT // 2)

            @block.gpsimd
            def _(pool):
                with pool.Fori(0, B) as b:
                    pool.wait_ge(scat_ready, b + 1)
                    pool.sem_inc(pool_step, 1)
                    for j in range(TB * K0):
                        pool.indirect_dma_start(slots0, bass.IndirectOffsetOnAxis(dest[:, j:j + 1].bitcast(U32), 0),
                                                pairs[:, 2 * j:2 * j + 2], None, bounds_check=P * E0 - 1,
                                                oob_is_err=False).then_inc(scat_done, 16)
                pool.wait_ge(scat_done, 16 * TT * K0)

            @block.scalar
            def _(act):
                def copy_x(b, t):
                    act.wait_ge(xt_ready, b * TB + t + 1)
                    act.copy(xTn[:, t * DC * P:(t + 1) * DC * P], xt_psb).then_inc(xtn_ready, 1)

                def softmax(b):
                    act.wait_ge(lm_ready, 2 * b + 2)
                    act.activation(lm, lm, ACT.Exp).then_inc(exp_done, 1)
                    act.activation(td, td, ACT.Exp).then_inc(exp_done, 1)

                def item(b, m):
                    n = b * ITEMS + m
                    act.wait_ge(g_ready, n + 1)
                    if later(b, m):
                        act.wait_ge(gu_ready, n)
                    act.activation(sil, gate_ps[:, 0:F0], ACT.Silu).then_inc(sil_ready, 1)

                def copy_h(b, m):
                    act.wait_ge(t_ready, b * ITEMS + m + 1)
                    act.copy(hT[:, 0:2, :], t_ps[:, 0:256].rearrange("p (c n) -> p c n", c=2))
                    act.copy(hT[0:96, 2, :], t_ps[0:96, 256:384]).then_inc(ht_ready, 1)

                def move(b, t):
                    act.wait_ge(xtn_ready, b * TB + t + 1)
                    if later(b):
                        act.wait_ge(u_ready, (b - 1) * ITEMS + 2 * t + 2)
                    c = slice(t * DC * P, (t + 1) * DC * P)
                    act.copy(xT[:, c], xTn[:, c]).then_inc(xt_moved, 1)

                def batch(b, more):
                    if more:
                        act.wait_ge(xt_moved, TB * (b + 1))
                        act.wait_ge(log_ready, b + 1)
                    for m in range(ITEMS):
                        item(b, m)
                        if m:
                            copy_h(b, m - 1)
                        if more and m in (4, 5):
                            copy_x(b + 1, 2 * m - 8)
                            copy_x(b + 1, 2 * m - 7)
                        if more and m == 7:
                            for t in range(TB - 1):
                                move(b + 1, t)
                            softmax(b + 1)
                    copy_h(b, ITEMS - 1)
                    if more:
                        move(b + 1, TB - 1)
                for t in range(TB):
                    copy_x(0, t)
                    move(0, t)
                softmax(0)
                batch(0, True)
                with act.Fori(1, B - 1) as i:
                    batch(i, True)
                batch(B - 1, False)

            @block.vector
            def _(dve):
                own = Chain(dve, dve2)

                def at_value(b):
                    v = val[:, bass.ds(b * TB * S, TB * S)]
                    thr = candf[:, bass.ds(b, 1)]
                    own.did(dve.tensor_scalar(eq, v, thr, None, ALU.is_equal))
                    own.did(dve.tensor_scalar(ge, v, thr, 0.0, ALU.is_ge, ALU.add, accum_out=gecnt))
                    own.wait()

                def scan(t):
                    c = slice(t * S, (t + 1) * S)
                    own.did(dve.tensor_tensor_scan(cum[:, c], eq[:, c], eq[:, c], 0.0, ALU.add, ALU.max))

                def tie_counts():
                    last = cum.rearrange("p (t s) -> p t s", t=TB)[:, :, S - 1]
                    own.wait()
                    own.did(dve.tensor_copy(rc, last))
                    own.did(dve.memset(rcex[:, 0:1], 0.0))
                    own.wait()
                    for t in range(TB):
                        own.did(dve.tensor_tensor(rcex[:, t + 1:t + 2], rcex[:, t:t + 1], rc[:, t:t + 1], ALU.add))
                        own.wait()
                    dve.tensor_tensor(rcex[:, 4:5], gecnt, rcex[:, 4:5], ALU.subtract).then_inc(tie_in, 1)

                def make_mask(b):
                    dve.wait_ge(tie_ready, b + 1)
                    own.did(dve.tensor_scalar(lim[:, 4:5], tie_ps[:, 4:5], -1.0, float(KEEP), ALU.mult, ALU.add))
                    own.wait()
                    own.did(dve.tensor_scalar(lim[:, 0:4], tie_ps[:, 0:4], lim[:, 4:5], -1.0, ALU.subtract, ALU.mult))
                    own.wait()
                    for t in range(TB):
                        c = slice(t * S, (t + 1) * S)
                        own.did(dve.scalar_tensor_tensor(eq[:, c], cum[:, c], lim[:, t:t + 1], eq[:, c],
                                                         ALU.is_gt, ALU.mult))
                    own.wait()
                    if later(b):
                        dve.wait_ge(mask_out, 16 * b)
                        dve.wait_ge(xt_ready, TB * b)
                    dve.tensor_tensor(mask, ge, eq, ALU.subtract).then_inc(mask_ready, 1)

                def best(b):
                    dve.wait_ge(log_ready, b + 1)
                    dve.sem_inc(dve_step, 1)
                    for t in range(TB):
                        own.did(dve.max(top[:, t, :], log_ps[:, t * E0:(t + 1) * E0]))
                    own.wait()
                    dve.sem_inc(dve_step, 1)
                    for t in range(TB):
                        own.did(dve.max_index(idx[:, t, :], top[:, t, :], log_ps[:, t * E0:(t + 1) * E0]))
                    largest = top[:, :, 0:1]
                    dve.tensor_tensor(lm, log_ps[:, 0:TB * E0].rearrange("p (t e) -> p t e", e=E0),
                                      largest.broadcast_to([P, TB, E0]), ALU.subtract).then_inc(lm_ready, 1)
                    dve.tensor_tensor(td, top, largest.broadcast_to([P, TB, 8]), ALU.subtract).then_inc(lm_ready, 1)
                    own.wait()
                    own.did(dve.tensor_copy(idxf.rearrange("p (t k) -> p t k", k=K0), idx[:, :, 0:K0]))
                    own.wait()

                ohv = oh.rearrange("p (j e) -> p j e", e=E0)

                def one_hot(b):
                    own.did(dve.tensor_tensor(ohv, cf[:, CF_I64:CF_I64 + E0].unsqueeze(1).broadcast_to([P, TB * K0, E0]),
                                              idxf.unsqueeze(2).broadcast_to([P, TB * K0, E0]), ALU.is_equal))
                    own.wait()
                    with nc.allow_low_precision("0 or 1"):
                        dve.tensor_reduce(selb, oh.rearrange("p (t k e) -> p t e k", k=K0, e=E0), AX,
                                          ALU.add).then_inc(sel_ready, 1)

                def weights(b):
                    dve.wait_ge(exp_done, 2 * b + 2)
                    own.did(dve.tensor_reduce(es, lm, AX, ALU.add))
                    own.wait()
                    own.did(dve.reciprocal(es, es))
                    own.wait()
                    if later(b):
                        dve.wait_ge(scat_done, 16 * TB * K0 * b)
                    pv = pairs.rearrange("p (t k w) -> p t k w", k=K0, w=2)
                    own.did(dve.tensor_tensor(pv[:, :, :, 1], td[:, :, 0:K0],
                                              es.unsqueeze(2).broadcast_to([P, TB, K0]), ALU.mult))
                    own.did(dve.tensor_copy(pv[:, :, :, 0].bitcast(I32), ci[:, bass.ds(b * TB + CI_TOK, TB)]
                                            .unsqueeze(2).broadcast_to([P, TB, K0])))

                def place(b):
                    dve.wait_ge(pos_ready, b + 1)
                    own.did(dve.tensor_reduce(seltot, selb.rearrange("p t e -> p e t"), AX, ALU.add))
                    pos = pos_ps[:, 0:TB * E0].rearrange("p (t e) -> p t e", e=E0)
                    own.did(dve.tensor_tensor(prod.rearrange("p (t k e) -> p t k e", k=K0, e=E0),
                                              oh.rearrange("p (t k e) -> p t k e", k=K0, e=E0),
                                              pos.unsqueeze(2).broadcast_to([P, TB, K0, E0]), ALU.mult))
                    own.wait()
                    own.did(dve.tensor_tensor(carry, carry, seltot, ALU.add))
                    own.did(dve.tensor_reduce(posk, prod.rearrange("p (j e) -> p j e", e=E0), AX, ALU.add))
                    own.wait()
                    own.did(dve.tensor_scalar(over, posk, float(CAP), OUT_OF_BOUNDS, ALU.is_ge, ALU.mult))
                    own.did(dve.scalar_tensor_tensor(posk, posk, float(E0), idxf, ALU.mult, ALU.add))
                    own.wait()
                    dve.tensor_tensor(dest, posk, over, ALU.add).then_inc(scat_ready, 1)

                def item(b, m):
                    n = b * ITEMS + m
                    dve.wait_ge(u_ready, n + 1)
                    dve.wait_ge(sil_ready, n + 1)
                    dve.tensor_tensor(gu, sil, up_ps[:, 0:F0], ALU.mult).then_inc(gu_ready, 1)

                def residual(b, t):
                    n = b * TB + t
                    dve.wait_ge(d_ready, n + 1)
                    dve.wait_ge(xr_in[t % 2], 16 * (b * 2 + t // 2 + 1))
                    if t >= 2 or later(b):
                        dve.wait_ge(o_out[t % 2], 16 * (b * 2 + t // 2))
                    dve.tensor_tensor(ob[t % 2], x_res[t % 2], d_ps[:, :], ALU.add).then_inc(o_ready, 1)

                def batch(b, more):
                    nxt = b + 1
                    for m in range(ITEMS):
                        item(b, m)
                        if m == 0:
                            weights(b)
                            place(b)
                        elif m % 2 == 0:
                            residual(b, m // 2 - 1)
                        if not more:
                            continue
                        if m == 1:
                            at_value(nxt)
                            scan(0)
                            scan(1)
                        elif m == 2:
                            scan(2)
                            scan(3)
                            tie_counts()
                        elif m == 3:
                            make_mask(nxt)
                        elif m == 6:
                            best(nxt)
                            one_hot(nxt)
                    residual(b, TB - 1)

                own.did(dve.memset(carry, 0.0))
                at_value(0)
                for t in range(TB):
                    scan(t)
                tie_counts()
                make_mask(0)
                best(0)
                one_hot(0)
                batch(0, True)
                with dve.Fori(1, B - 1) as i:
                    own.loop(i, PER_BATCH, 1)
                    own.wait()
                    batch(i, True)
                    own.end(B - 2)
                batch(B - 1, False)

            @block.tensor
            def _(pe):
                def tie(b):
                    pe.wait_ge(tie_in, b + 1)
                    pe.matmul(tie_ps[:, 0:5], ones, rcex, start=True, stop=False)
                    pe.matmul(tie_ps[:, 0:4], tri, rc, start=False, stop=True).then_inc(tie_ready, 1)

                def turn(b, t):
                    pe.wait_ge(mask_ready, b + 1)
                    if later(b, t):
                        pe.wait_ge(xtn_ready, b * TB + t)
                    for c in range(DC):
                        mm = pe.transpose(xt_psb[:, c * P:(c + 1) * P], mask[:, t * S + c:(t + 1) * S:DC], identb)
                    mm.then_inc(xt_ready, 1)

                def logits(b):
                    pe.wait_ge(xtn_ready, TB * (b + 1))
                    for t in range(TB):
                        for c in range(DC):
                            for k in range(3):
                                mm = pe.matmul(log_ps[:, t * E0:(t + 1) * E0], xTn[:, (t * DC + c) * P:(t * DC + c + 1) * P],
                                               gate0_parts[:, k, c, :], start=c + k == 0, stop=c == DC - 1 and k == 2)
                    mm.then_inc(log_ready, 1)

                def positions(b):
                    pe.wait_ge(sel_ready, b + 1)
                    for t in range(TB):
                        to = pos_ps[:, t * E0:(t + 1) * E0]
                        pe.matmul(to, trib, selb[:, t, :], start=True, stop=False)
                        for s in range(t):
                            pe.matmul(to, onesb, selb[:, s, :], start=False, stop=False)
                        mm = pe.matmul(to, onesb, carry, start=False, stop=True)
                    mm.then_inc(pos_ready, 1)

                def product(m, bank, column):
                    for c in range(DC):
                        for part in (sh_hi, sh_lo):
                            mm = pe.matmul(bank[:, 0:F0], xT[:, (m // 2 * DC + c) * P:(m // 2 * DC + c + 1) * P],
                                           part[:, c, column:column + F0], start=c == 0 and part is sh_hi,
                                           stop=c == DC - 1 and part is sh_lo)
                    return mm

                def gate(b, m):
                    if later(b, m):
                        pe.wait_ge(sil_ready, b * ITEMS + m)
                    product(m, gate_ps, (m % 2) * 2 * F0).then_inc(g_ready, 1)

                def up(b, m):
                    if later(b, m):
                        pe.wait_ge(gu_ready, b * ITEMS + m)
                    product(m, up_ps, (m % 2) * 2 * F0 + F0).then_inc(u_ready, 1)

                def turn_h(b, m):
                    n = b * ITEMS + m
                    pe.wait_ge(gu_ready, n + 1)
                    if later(b, m):
                        pe.wait_ge(ht_ready, n)
                    for c, (f, k) in enumerate(F0C):
                        mm = pe.transpose(t_ps[0:k, c * P:(c + 1) * P], gu[:, f:f + k], ident)
                    mm.then_inc(t_ready, 1)

                def down(b, m):
                    n = b * ITEMS + m
                    pe.wait_ge(ht_ready, n + 1)
                    if m % 2 == 0 and later(b, m):
                        pe.wait_ge(o_ready, b * TB + m // 2)
                    for c, (f, k) in enumerate(F0C):
                        mm = pe.matmul(d_ps[:, :], hT[0:k, c, :], sh_dw[0:k, 3 * (m % 2) + c, :],
                                       start=m % 2 == 0 and c == 0, stop=m % 2 == 1 and c == 2)
                    if m % 2:
                        mm.then_inc(d_ready, 1)

                def batch(b, more):
                    for m in range(ITEMS):
                        if m % 2 == 0:
                            pe.wait_ge(xt_moved, b * TB + m // 2 + 1)
                        gate(b, m)
                        if m:
                            turn_h(b, m - 1)
                        up(b, m)
                        if m == 0:
                            positions(b)
                        if more and m == 3:
                            tie(b + 1)
                        if more and m in (4, 5):
                            turn(b + 1, 2 * m - 8)
                            turn(b + 1, 2 * m - 7)
                        if more and m == 6:
                            logits(b + 1)
                        if m:
                            down(b, m - 1)
                    turn_h(b, ITEMS - 1)
                    down(b, ITEMS - 1)
                tie(0)
                for t in range(TB):
                    turn(0, t)
                logits(0)
                batch(0, True)
                with pe.Fori(1, B - 1) as i:
                    batch(i, True)
                batch(B - 1, False)

        early.close()
        middle = ctx.enter_context(ExitStack())
        PART0 = DC * F0
        space0 = sb("space0", [P, 14000], till=middle)
        parts0 = sb("parts0", [P, 8 * PART0], F32R, till=middle)
        rows0 = sb("rows0", [P, 2 * D], F32R, till=middle)

        def expert_stage(name, items, F, chunks, row_dt, rows, slots, cols, acc, region, table_at, loads, tile_cols=None, weights_in=None):
            nch = len(chunks)
            rw = D // 2 if row_dt == BF16 else D
            at = [region]

            def buf(words, dt=F32):
                at[0] += words
                return take(space0 if loads else misc, at[0] - words, words, dt)
            xrow = [buf(rw, row_dt) for _ in range(2)]
            xT = [(rows0[:, i * D:(i + 1) * D] if loads else buf(D)).rearrange("p (c n) -> p c n", c=DC) for i in range(2)]
            parts = [[[parts0[:, (4 * u + 2 * m + k) * DC * F0:(4 * u + 2 * m + k + 1) * DC * F0] for k in range(2)]
                      for m in range(2)] for u in range(2)] if loads else None
            sil, gu, hT = buf(512), buf(512), buf(512).rearrange("p (c n) -> p c n", c=4)
            ob = [buf(D) for _ in range(2)]
            table = take(misc, table_at, 2 * cols)
            idx_get = [take(misc, table_at + 2 * cols + i, 1, I32) for i in range(2)]
            idx_add = [take(misc, table_at + 2 * cols + 2 + i, 1, I32) for i in range(2)]
            gate_ps, up_ps, h_ps, d_ps, x_ps = PS[0:5]
            x_psv = x_ps[:, 0:rw] if row_dt == F32 else x_ps[:, 0:rw].bitcast(BF16)
            idm = ident if row_dt == F32 else identb

            def sm(n):
                return sem(f"{name}_{n}")
            table_in, pool_did, pool_step = sm("table_in"), sm("pool_did"), sm("pool_step")
            rows_in = [sm(f"rows_in{i}") for i in range(2)]
            add_done = [sm(f"add_done{i}") for i in range(2)]
            x_turned, x_copied, g_ready, sil_ready = sm("x_turned"), sm("x_copied"), sm("g_ready"), sm("sil_ready")
            u_ready, gu_ready, h_turned, h_copied = sm("u_ready"), sm("gu_ready"), sm("h_turned"), sm("h_copied")
            d_ready, o_ready = sm("d_ready"), sm("o_ready")
            if loads:
                wg_in, wu_in, wd_in = ([sm(f"w{k}_in{i}") for i in range(2)] for k in "gud")
                rounded, left = [sm("g_rounded"), sm("u_rounded")], [sm("g_left"), sm("u_left")]

            class Tile:

                def __init__(self, n, u, h, early=False):
                    self.n, self.u, self.h, self.early = n, u, h, early
                    self.first = early and u == 0

            def fixed(n):
                return Tile(n, n % 2, n // 2, n < 2)

            def inside(j, k, ahead=0):
                o = 1 + k + ahead
                return Tile(2 * j + o, o % 2, j + o // 2)
            PAIRS = (items - 2) // 2

            def pipeline(eng, slot):
                slot(None, fixed(0), fixed(1))
                for n in (1, 2):
                    slot(fixed(n - 1), fixed(n), fixed(n + 1))
                with eng.Fori(1, PAIRS) as j:
                    for k in range(2):
                        slot(inside(j, k, -1), inside(j, k), inside(j, k, 1))
                slot(fixed(items - 2), fixed(items - 1), None)

            with nc.Block() as block:
                @block.sync
                def _(sp):
                    if loads:
                        sp.dma_start(table, slots.rearrange("(p c) w -> p (c w)", p=P)).then_inc(table_in, 16)
                        (dg, du, dd), (bg, bu, bd) = loads

                        def in_load(t, dst, src, free, arrived):
                            if not t.early:
                                sp.wait_ge(free, t.n - 1)
                            sp.dma_start(dst[t.u], src[bass.ds(t.n, 1)].rearrange("e (p c) f -> p (e c f)", p=P)).then_inc(arrived[t.u], 16)

                        def down_load(t):
                            if not t.early:
                                sp.wait_ge(d_ready, t.n - 1)
                            sp.dma_start(bd[t.u][:, 0:2 * D].rearrange("p (c n) -> p c n", c=2),
                                         dd[bass.ds(t.n, 1), 0:2 * P, :].rearrange("e (c p) n -> p (e c) n", p=P)).then_inc(wd_in[t.u], 16)
                            sp.dma_start(bd[t.u][0:F - 2 * P, 2 * D:3 * D],
                                         dd[bass.ds(t.n, 1), 2 * P:F, :].rearrange("e p n -> p (e n)")).then_inc(wd_in[t.u], 16)

                        for n in range(2):
                            in_load(fixed(n), bg, dg, left[0], wg_in)
                            in_load(fixed(n), bu, du, left[1], wu_in)
                            if n == 0:
                                sp.wait_ge(rows_in[0], 16)
                        down_load(fixed(0))
                        in_load(fixed(2), bg, dg, left[0], wg_in)
                        in_load(fixed(2), bu, du, left[1], wu_in)
                        down_load(fixed(1))

                        def slot(j, k):
                            t = inside(j, k, 2)
                            in_load(t, bg, dg, left[0], wg_in)
                            in_load(t, bu, du, left[1], wu_in)
                            down_load(inside(j, k, 1))
                        with sp.Fori(0, PAIRS - 1) as j:
                            slot(j, 0)
                            slot(j, 1)
                        slot(PAIRS - 1, 0)
                        down_load(fixed(items - 1))
                    else:
                        with sp.Fori(1, E1) as e:
                            sp.wait_ge(weights_in, e * 16 * 3)
                            expert_load(sp, e)
                        sp.wait_ge(weights_in, 16 * 3 * E1)

                @block.gpsimd
                def _(pool):
                    own = Chain(pool, pool_did)

                    def column(t):
                        if tile_cols is None:
                            return t.n * 2
                        return pool.value_load(tile_cols[0][0:1, bass.ds(t.n, 1)], min_val=0, max_val=cols - 1) * 2

                    def gather(t):
                        if not t.early:
                            pool.wait_ge(rows_in[t.u], t.h * 16)
                        own.did(pool.tensor_copy(idx_get[t.u], table[:, bass.ds(column(t), 1)].bitcast(I32)))
                        own.wait()
                        if not t.early:
                            pool.wait_ge(x_turned, t.n - 1)
                        pool.sem_inc(pool_step, 1)
                        pool.indirect_dma_start(xrow[t.u], None, rows, bass.IndirectOffsetOnAxis(idx_get[t.u].bitcast(U32), 0)
                                                ).then_inc(rows_in[t.u], 16)

                    def add(t):
                        if not t.first:
                            pool.wait_ge(add_done[1 - t.u], (t.h + t.u) * 16)
                        own.did(pool.tensor_copy(idx_add[t.u], table[:, bass.ds(column(t), 1)].bitcast(I32)))
                        own.wait()
                        pool.wait_ge(o_ready, t.n + 1)
                        pool.sem_inc(pool_step, 1)
                        pool.indirect_dma_start(acc, bass.IndirectOffsetOnAxis(idx_add[t.u].bitcast(U32), 0), ob[t.u], None,
                                                compute_op=ALU.add).then_inc(add_done[t.u], 16)
                    if loads:
                        pool.wait_ge(table_in, 16)
                    for n in range(3):
                        gather(fixed(n))
                    for n in range(2):
                        gather(fixed(n + 3))
                        add(fixed(n))
                    with pool.Fori(1, PAIRS - 1) as j:
                        own.loop(j, 4, 1)
                        for k in range(2):
                            gather(inside(j, k, 2))
                            add(inside(j, k, -1))
                        own.end(PAIRS - 2)
                    gather(fixed(items - 1))
                    add(fixed(items - 4))
                    add(fixed(items - 3))
                    add(fixed(items - 2))
                    add(fixed(items - 1))
                    for u in range(2):
                        pool.wait_ge(add_done[u], items // 2 * 16)

                @block.scalar
                def _(act):
                    def silu(t):
                        act.wait_ge(g_ready, t.n + 1)
                        if not t.first:
                            act.wait_ge(gu_ready, t.n)
                        act.activation(sil[:, 0:F], gate_ps[:, 0:F], ACT.Silu).then_inc(sil_ready, 1)

                    def scale(t):
                        if not t.early:
                            act.wait_ge(add_done[t.u], t.h * 16)
                        col = t.n * 2 if tile_cols is None else act.value_load(
                            tile_cols[0][0:1, bass.ds(t.n, 1)], min_val=0, max_val=cols - 1) * 2
                        act.wait_ge(d_ready, t.n + 1)
                        act.activation(ob[t.u], d_ps[:, :], ACT.Copy, scale=table[:, bass.ds(col + 1, 1)]).then_inc(o_ready, 1)

                    def round_off(t, m):
                        act.wait_ge((wg_in, wu_in)[m][t.u], 16 * (t.h + 1))
                        if not t.early:
                            act.wait_ge((g_ready, u_ready)[m], t.n - 1)
                        act.copy(parts[t.u][m][0], loads[1][m][t.u]).then_inc(rounded[m], 1)

                    def slot(prev, this, nxt):
                        if loads and nxt:
                            round_off(nxt, 0)
                        silu(this)
                        if loads and nxt:
                            round_off(nxt, 1)
                        if prev:
                            scale(prev)
                    if loads:
                        for m in range(2):
                            round_off(fixed(0), m)
                    if loads:
                        act.wait_ge(table_in, 16)
                    pipeline(act, slot)
                    scale(fixed(items - 1))

                @block.vector
                def _(dve):
                    def copy_h(t):
                        dve.wait_ge(h_turned, t.n + 1)
                        full = [c for c, (_, k) in enumerate(chunks) if k == P]
                        mm = dve.tensor_copy(hT[:, 0:len(full), :].rearrange("p c n -> p (c n)"), h_ps[:, 0:len(full) * P])
                        for c, (_, k) in enumerate(chunks):
                            if k < P:
                                dve.tensor_copy(hT[0:k, c, :], h_ps[0:k, c * P:(c + 1) * P]).then_inc(h_copied, 1)
                                mm.then_inc(h_copied, 1)
                                return
                        mm.then_inc(h_copied, 2)

                    def product(t):
                        dve.wait_ge(sil_ready, t.n + 1)
                        dve.wait_ge(u_ready, t.n + 1)
                        dve.tensor_tensor(gu[:, 0:F], sil[:, 0:F], up_ps[:, 0:F], ALU.mult).then_inc(gu_ready, 1)

                    def copy_x(t):
                        dve.wait_ge(x_turned, t.n + 1)
                        if not t.early:
                            dve.wait_ge(u_ready, t.n - 1)
                        dve.tensor_copy(xT[t.u].rearrange("p c n -> p (c n)"), x_psv).then_inc(x_copied, 1)

                    def leave(t, m):
                        dve.wait_ge(rounded[m], t.n + 1)
                        dve.tensor_tensor(parts[t.u][m][1], loads[1][m][t.u], parts[t.u][m][0], ALU.subtract).then_inc(left[m], 1)

                    def slot(prev, this, nxt):
                        if prev:
                            copy_h(prev)
                        if loads and nxt:
                            leave(nxt, 0)
                        product(this)
                        if nxt:
                            copy_x(nxt)
                        if loads and nxt:
                            leave(nxt, 1)
                    copy_x(fixed(0))
                    if loads:
                        for m in range(2):
                            leave(fixed(0), m)
                    pipeline(dve, slot)
                    copy_h(fixed(items - 1))

                @block.tensor
                def _(pe):
                    def turn_x(t):
                        pe.wait_ge(rows_in[t.u], 16 * (t.h + 1))
                        if not t.first:
                            pe.wait_ge(x_copied, t.n)
                        for c in range(DC):
                            mm = pe.transpose(x_psv[:, c * P:(c + 1) * P], xrow[t.u][:, c:D:DC], idm)
                        mm.then_inc(x_turned, 1)

                    def weight(t, m, c):
                        if loads:
                            return loads[1][m][t.u][0:chunks[c][1], c * D:(c + 1) * D]
                        return arena[:, bass.ds(t.at + (m * DC * D + c * D), D)]

                    def rows_by(t, m, bank):
                        for c in range(DC):
                            of = [part[:, c * F:(c + 1) * F] for part in parts[t.u][m]] if loads else [weight(t, m, c)]
                            for k, w in enumerate(of):
                                mm = pe.matmul(bank[:, 0:F], xT[t.u][:, c, :], w, start=c + k == 0,
                                               stop=c == DC - 1 and k == len(of) - 1)
                        return mm

                    def find(t, wait=False):
                        if not loads:
                            e = pe.value_load(tile_cols[1][0:1, bass.ds(t.n, 1)], min_val=0, max_val=E1 - 1)
                            t.at = e * SLOT
                            if wait:
                                pe.wait_ge(weights_in, e * (16 * 3) + 16 * 3)

                    def gate(t):
                        pe.wait_ge(x_copied, t.n + 1)
                        if not t.first:
                            pe.wait_ge(sil_ready, t.n)
                        if loads:
                            pe.wait_ge(left[0], t.n + 1)
                        rows_by(t, 0, gate_ps).then_inc(g_ready, 1)

                    def up(t):
                        if not t.first:
                            pe.wait_ge(gu_ready, t.n)
                        if loads:
                            pe.wait_ge(left[1], t.n + 1)
                        rows_by(t, 1, up_ps).then_inc(u_ready, 1)

                    def turn_h(t):
                        pe.wait_ge(gu_ready, t.n + 1)
                        if not t.first:
                            pe.wait_ge(h_copied, 2 * t.n)
                        for c, (f, k) in enumerate(chunks):
                            src = gu[:, f:f + k] if loads else gu[:, c:F:DC]
                            mm = pe.transpose(h_ps[0:k, c * P:(c + 1) * P], src, ident)
                        mm.then_inc(h_turned, 1)

                    def down(t):
                        pe.wait_ge(h_copied, 2 * (t.n + 1))
                        if not t.first:
                            pe.wait_ge(o_ready, t.n)
                        if loads:
                            pe.wait_ge(wd_in[t.u], 32 * (t.h + 1))
                        for c, (f, k) in enumerate(chunks):
                            mm = pe.matmul(d_ps[:, :], hT[0:k, c, :], weight(t, 2, c), start=c == 0, stop=c == nch - 1)
                        mm.then_inc(d_ready, 1)

                    def slot(prev, this, nxt):
                        if prev:
                            find(prev)
                        find(this, True)
                        gate(this)
                        if prev:
                            turn_h(prev)
                        up(this)
                        if nxt:
                            turn_x(nxt)
                        if prev:
                            down(prev)
                    turn_x(fixed(0))
                    pipeline(pe, slot)
                    last = fixed(items - 1)
                    find(last)
                    turn_h(last)
                    down(last)

        wbuf = [[take(space0, u * 4352 + o, w) for u in range(2)] for o, w in ((0, 1408), (1408, 1408), (2816, 1536))]
        expert_stage("e0", E0, F0, F0C, BF16, mask_rows, slots0, E0, acc0, 2 * 4352, M2,
                     ((w_gate, w_up, w_down), wbuf))
        middle.close()

        late = ctx.enter_context(ExitStack())
        space1 = sb("space1", [P, 5152 + SLOT], till=late)
        parts1 = sb("parts1", [P, 2 * SLOT], F32R, till=late)
        cols1 = sb("cols1", [P, 6 * D], F32R, till=late)
        shared = [space1[:, 5152 + m * DC * D:5152 + (m + 1) * DC * D] for m in range(3)]
        sh1_hi, sh1_lo = ([parts1[:, (3 * k + m) * DC * D:(3 * k + m + 1) * DC * D] for m in range(3)] for k in range(2))
        y_hi, y_lo = ([cols1[:, (2 * k + i) * D:(2 * k + i + 1) * D].rearrange("p (c n) -> p c n", c=DC) for i in range(2)]
                      for k in range(2))
        h_hi, h_lo = (cols1[:, (4 + k) * D:(5 + k) * D].rearrange("p (c n) -> p c n", c=DC) for k in range(2))
        C0 = 0
        x1 = [take(space1, C0 + i * D, D) for i in range(TB)]
        HIST = 3
        x1T = [take(space1, C0 + 2048 + i * 528, DC * (P + HIST)).rearrange("p (c n) -> p c n", c=DC) for i in range(2)]
        yT = [take(space1, C0 + 3104 + i * D, D).rearrange("p (c n) -> p c n", c=DC) for i in range(2)]
        y_row = [take(space1, C0 + 4128 + i * D, D) for i in range(2)]
        sil1 = take(misc, M3, D)
        gu1 = take(misc, M3 + 512, D)
        ob1 = [take(misc, M3 + 1536 + i * D, D) for i in range(2)]
        M4 = M3 + 2560
        conv_w = take(misc, M4, 4 * DC).rearrange("p (k c) -> p k c", k=4)
        conv_bias = take(misc, M4 + 16, DC)
        gate1_w = take(misc, M4 + 20, DC * E1).rearrange("p (c e) -> p c e", c=DC)
        gb_bc = take(misc, M4 + 48, E1)
        bias_bc = take(misc, M4 + 56, E1)
        lg1 = take(misc, M4 + 64, TB * 8).rearrange("p (t e) -> p t e", e=8)
        prob = take(misc, M4 + 96, TB * 8).rearrange("p (t e) -> p t e", e=8)
        biased = take(misc, M4 + 128, TB * 8).rearrange("p (t e) -> p t e", e=8)
        top1 = take(misc, M4 + 160, TB * 8).rearrange("p (t e) -> p t e", e=8)
        idx1 = take(misc, M4 + 192, TB * 8, U32).rearrange("p (t e) -> p t e", e=8)
        mx1 = take(misc, M4 + 224, TB)
        idxf1 = take(misc, M4 + 228, TB * K1)
        oh1 = take(misc, M4 + 240, TB * K1 * 8)
        prod1 = take(misc, M4 + 336, TB * K1 * 8)
        pk1 = take(misc, M4 + 432, TB * K1)
        s3 = take(misc, M4 + 444, TB)
        pp1 = take(misc, M4 + 448, TB * K1)
        posi = take(misc, M4 + 460, TB * K1, I32)
        hi_i = take(misc, M4 + 472, TB * K1, I32)
        lo_i = take(misc, M4 + 484, TB * K1, I32)
        hi_f = take(misc, M4 + 496, TB * K1)
        lo_f = take(misc, M4 + 508, TB * K1)
        dest1 = take(misc, M4 + 520, TB * K1, I32)
        pairs1 = take(misc, M4 + 532, TB * K1 * 2)
        sel1 = take(misc, M4 + 556, TB * 4, BF16).rearrange("p (t e) -> p t e", e=8)
        carry1 = take(misc, M4 + 572, 4, BF16)
        seltot1 = take(misc, M4 + 576, 8)
        M5 = 8300
        assert M4 + 584 <= M5 and M3 + 4608 <= M5

        names = ("small_in c_x_turned c_x_copied conv_done c_log_ready y_turned y_copied c_g c_sil c_u c_gu c_ht c_hc c_d c_o "
                 "c_lm c_exp c_sel c_pos c_scat c_scat_done c_dve c_step c_pstep sh1_rounded sh1_left y_rounded y_left h_rounded c_act")
        (small_in, c_x_turned, c_x_copied, conv_done, c_log_ready, y_turned, y_copied, c_g, c_sil, c_u, c_gu, c_ht, c_hc,
         c_d, c_o, c_lm, c_exp, c_sel, c_pos, c_scat, c_scat_done, c_dve, c_step, c_pstep, sh1_rounded, sh1_left, y_rounded, y_left, h_rounded, c_act) = (
            sem(n) for n in names.split())
        sh1_in = [sem(f"sh1_in{m}") for m in range(3)]
        x1_in = [sem(f"x1_in{i}") for i in range(TB)]
        y_out = [sem(f"y_out{i}") for i in range(2)]
        out_out = [sem(f"out_out{i}") for i in range(2)]
        out_t = out[0:T].rearrange("(t p) d -> t p d", p=P)
        y_t = y_rows[0:T].rearrange("(t p) d -> t p d", p=P)
        ybk_ps, log1_ps, pos1_ps = PS[5:8]
        log1 = log1_ps[:, 0:TB * 8].rearrange("p (t e) -> p t e", e=8)

        def nxt_tile(b, t):
            return (b, t + 1) if t + 1 < TB else (b + 1, 0)

        with nc.Block() as block:
            @block.sync
            def _(sp):
                sp.dma_start(gate1_w, gate1.rearrange("(p c) e -> p c e", c=DC)).then_inc(small_in, 16)
                sp.dma_start(conv_w, cond.rearrange("k (p c) -> p k c", c=DC)).then_inc(small_in, 16)
                sp.dma_start(conv_bias, conv_b.rearrange("(p c) -> p c", c=DC)).then_inc(small_in, 16)
                sp.dma_start(gb_bc, gate1_b.partition_broadcast(P)).then_inc(small_in, 16)
                sp.dma_start(bias_bc, biases.partition_broadcast(P)).then_inc(small_in, 16)

                def batch(b, more):
                    for t in range(TB):
                        n = b * TB + t
                        if more or t < TB - 1:
                            nb, nt = nxt_tile(b, t)
                            sp.wait_ge(y_copied, n + 2)
                            sp.dma_start(y_t[nb * TB + nt], y_row[nt % 2]).then_inc(y_out[nt % 2], 16)
                        sp.wait_ge(c_o, n + 1)
                        sp.dma_start(out_t[n], ob1[t % 2]).then_inc(out_out[t % 2], 16)
                        if more:
                            sp.dma_start(x1[t], acc0_t[n + TB]).then_inc(x1_in[t], 16)
                for t in range(TB):
                    sp.dma_start(x1[t], acc0_t[t]).then_inc(x1_in[t], 16)
                    if t < 3:
                        sp.dma_start(shared[t], w_res[:, t * DC * D:(t + 1) * DC * D]).then_inc(sh1_in[t], 16)
                sp.wait_ge(y_copied, 1)
                sp.dma_start(y_t[0], y_row[0]).then_inc(y_out[0], 16)
                batch(0, True)
                with sp.Fori(1, B - 1) as b:
                    batch(b, True)
                batch(B - 1, False)
                for i in range(2):
                    sp.wait_ge(y_out[i], 16 * TT // 2)
                    sp.wait_ge(out_out[i], 16 * TT // 2)

            @block.gpsimd
            def _(pool):
                with pool.Fori(0, B) as b:
                    pool.wait_ge(c_scat, b + 1)
                    pool.sem_inc(c_pstep, 1)
                    for j in range(TB * K1):
                        pool.indirect_dma_start(slots1, bass.IndirectOffsetOnAxis(dest1[:, j:j + 1].bitcast(U32), 0),
                                                pairs1[:, 2 * j:2 * j + 2], None).then_inc(c_scat_done, 16)
                pool.wait_ge(c_scat_done, 16 * TT * K1)

            @block.scalar
            def _(act):
                def copy_x(b, t):
                    n = b * TB + t
                    act.wait_ge(c_x_turned, n + 1)
                    if t == 0:
                        if later(b):
                            act.wait_ge(conv_done, n)
                        act.activation(x1T[0][:, :, 0:HIST], cf[:, CF_ONE:CF_ONE + DC * HIST].rearrange("p (c n) -> p c n", c=DC),
                                       ACT.Copy, scale=0.0).then_inc(c_act, 1)
                    else:
                        act.wait_ge(conv_done, n - 1)
                        act.wait_ge(c_x_copied, n)
                        act.copy(x1T[t % 2][:, :, 0:HIST], x1T[1 - t % 2][:, :, P:P + HIST]).then_inc(c_act, 1)
                    act.copy(x1T[t % 2][:, :, HIST:HIST + P], PS[4][:, :].rearrange("p (c n) -> p c n", c=DC)).then_inc(c_x_copied, 1)

                def copy_y(b, t):
                    n = b * TB + t
                    act.wait_ge(y_turned, n + 1)
                    if later(b) or t >= 2:
                        act.wait_ge(y_out[t % 2], 16 * (b * 2 + t // 2))
                    act.copy(y_row[t % 2], ybk_ps[:, :]).then_inc(y_copied, 1)

                def silu(b, t):
                    n = b * TB + t
                    act.wait_ge(c_g, n + 1)
                    if later(b, t):
                        act.wait_ge(c_gu, n)
                    act.activation(sil1, PS[0][:, :], ACT.Silu).then_inc(c_sil, 1)

                def round_weights(m):
                    act.wait_ge(sh1_in[m], 16)
                    act.copy(sh1_hi[m], shared[m]).then_inc(sh1_rounded, 1)

                def round_y(b, t):
                    n = b * TB + t
                    act.wait_ge(conv_done, n + 1)
                    if later(b) or t >= 2:
                        act.wait_ge(c_u, n - 1)
                    act.copy(y_hi[t % 2], yT[t % 2]).then_inc(y_rounded, 1)

                def round_h(b, t):
                    n = b * TB + t
                    act.wait_ge(c_ht, n + 1)
                    if later(b, t):
                        act.wait_ge(c_d, n)
                    act.copy(h_hi, PS[2][:, :].rearrange("p (c n) -> p c n", c=DC)).then_inc(h_rounded, 1)

                def batch(b, more):
                    for t in range(TB):
                        front = more or t < TB - 1
                        if front:
                            copy_x(*nxt_tile(b, t))
                        silu(b, t)
                        if t:
                            round_h(b, t - 1)
                        elif later(b):
                            round_h(b - 1, TB - 1)
                        if front:
                            round_y(*nxt_tile(b, t))
                            copy_y(*nxt_tile(b, t))
                        if t == TB - 1:
                            act.wait_ge(c_lm, b + 1)
                            act.activation(lg1[:, :, 0:E1], lg1[:, :, 0:E1], ACT.Exp).then_inc(c_exp, 1)
                copy_x(0, 0)
                round_weights(0)
                round_y(0, 0)
                round_weights(1)
                copy_y(0, 0)
                round_weights(2)
                batch(0, True)
                with act.Fori(1, B - 1) as b:
                    batch(b, True)
                batch(B - 1, False)
                round_h(B - 1, TB - 1)

            @block.vector
            def _(dve):
                own = Chain(dve, c_dve)

                def conv(b, t):
                    n = b * TB + t
                    xs, ys = x1T[t % 2], yT[t % 2]
                    dve.wait_ge(c_x_copied, n + 1)
                    dve.wait_ge(c_act, n + 1)
                    if later(b) or t >= 2:
                        dve.wait_ge(c_u, n - 1)
                        dve.wait_ge(y_turned, n - 1)
                    for c in range(DC):
                        own.did(dve.tensor_scalar(ys[:, c, :], xs[:, c, 3:3 + P], conv_w[:, 3, c:c + 1], conv_bias[:, c:c + 1],
                                                  ALU.mult, ALU.add))
                    for k in (2, 1):
                        for c in range(DC):
                            own.wait(own.n - 3)
                            own.did(dve.scalar_tensor_tensor(ys[:, c, :], xs[:, c, k:k + P], conv_w[:, k, c:c + 1], ys[:, c, :],
                                                             ALU.mult, ALU.add))
                    for c in range(DC):
                        own.wait(own.n - 3 + c)
                        dve.scalar_tensor_tensor(ys[:, c, :], xs[:, c, 0:P], conv_w[:, 0, c:c + 1], ys[:, c, :],
                                                 ALU.mult, ALU.add).then_inc(conv_done if c == DC - 1 else c_step, 1)

                def leave_weights(m):
                    dve.wait_ge(sh1_rounded, m + 1)
                    dve.tensor_tensor(sh1_lo[m], shared[m], sh1_hi[m], ALU.subtract).then_inc(sh1_left, 1)

                def leave_y(b, t):
                    dve.wait_ge(y_rounded, b * TB + t + 1)
                    dve.tensor_tensor(y_lo[t % 2], yT[t % 2], y_hi[t % 2], ALU.subtract).then_inc(y_left, 1)

                def leave_h(b, t):
                    dve.wait_ge(h_rounded, b * TB + t + 1)
                    dve.tensor_tensor(h_lo, PS[2][:, :].rearrange("p (c n) -> p c n", c=DC), h_hi, ALU.subtract).then_inc(c_hc, 1)

                def product(b, t):
                    n = b * TB + t
                    dve.wait_ge(c_sil, n + 1)
                    dve.wait_ge(c_u, n + 1)
                    dve.tensor_tensor(gu1, sil1, PS[1][:, :], ALU.mult).then_inc(c_gu, 1)

                def residual(b, t):
                    n = b * TB + t
                    dve.wait_ge(c_d, n + 1)
                    if later(b) or t >= 2:
                        dve.wait_ge(out_out[t % 2], 16 * (b * 2 + t // 2))
                    dve.tensor_tensor(ob1[t % 2], x1[t], PS[3][:, :], ALU.add).then_inc(c_o, 1)

                def scores(b):
                    dve.wait_ge(c_log_ready, TB * (b + 1))
                    own.did(dve.tensor_tensor(lg1[:, :, 0:E1], log1[:, :, 0:E1], gb_bc.unsqueeze(1).broadcast_to([P, TB, E1]), ALU.add))
                    own.wait()
                    own.did(dve.tensor_reduce(mx1, lg1[:, :, 0:E1], AX, ALU.max))
                    own.wait()
                    dve.tensor_tensor(lg1[:, :, 0:E1], lg1[:, :, 0:E1], mx1.unsqueeze(2).broadcast_to([P, TB, E1]),
                                      ALU.subtract).then_inc(c_lm, 1)

                def choose(b):
                    dve.wait_ge(c_exp, b + 1)
                    own.did(dve.tensor_reduce(mx1, lg1[:, :, 0:E1], AX, ALU.add))
                    own.wait()
                    own.did(dve.reciprocal(mx1, mx1))
                    own.wait()
                    own.did(dve.tensor_tensor(prob[:, :, 0:E1], lg1[:, :, 0:E1], mx1.unsqueeze(2).broadcast_to([P, TB, E1]), ALU.mult))
                    own.wait()
                    own.did(dve.tensor_tensor(biased[:, :, 0:E1], prob[:, :, 0:E1], bias_bc.unsqueeze(1).broadcast_to([P, TB, E1]), ALU.add))
                    own.wait()
                    dve.sem_inc(c_step, 1)
                    for t in range(TB):
                        own.did(dve.max(top1[:, t, :], biased[:, t, :]))
                    own.wait()
                    dve.sem_inc(c_step, 1)
                    for t in range(TB):
                        own.did(dve.max_index(idx1[:, t, :], top1[:, t, :], biased[:, t, :]))
                    own.wait()
                    own.did(dve.tensor_copy(idxf1.rearrange("p (t k) -> p t k", k=K1), idx1[:, :, 0:K1]))
                    own.wait()
                    own.did(dve.tensor_tensor(oh1.rearrange("p (j e) -> p j e", e=8),
                                              cf[:, CF_I8:CF_I8 + 8].unsqueeze(1).broadcast_to([P, TB * K1, 8]),
                                              idxf1.unsqueeze(2).broadcast_to([P, TB * K1, 8]), ALU.is_equal))
                    own.wait()
                    with nc.allow_low_precision("0 or 1"):
                        dve.tensor_reduce(sel1, oh1.rearrange("p (t k e) -> p t e k", k=K1, e=8), AX, ALU.add).then_inc(c_sel, 1)
                    ohv1 = oh1.rearrange("p (t k e) -> p t k e", k=K1, e=8)
                    prv1 = prod1.rearrange("p (t k e) -> p t k e", k=K1, e=8)
                    own.did(dve.tensor_tensor(prv1, ohv1, prob.unsqueeze(2).broadcast_to([P, TB, K1, 8]), ALU.mult))
                    own.wait()
                    own.did(dve.tensor_reduce(pk1, prod1.rearrange("p (j e) -> p j e", e=8), AX, ALU.add))
                    own.wait()
                    own.did(dve.tensor_reduce(s3, pk1.rearrange("p (t k) -> p t k", k=K1), AX, ALU.add))
                    own.wait()
                    own.did(dve.reciprocal(s3, s3))
                    own.wait()
                    if later(b):
                        dve.wait_ge(c_scat_done, 16 * TB * K1 * b)
                    pv = pairs1.rearrange("p (t k w) -> p t k w", k=K1, w=2)
                    own.did(dve.tensor_tensor(pv[:, :, :, 1], pk1.rearrange("p (t k) -> p t k", k=K1),
                                              s3.unsqueeze(2).broadcast_to([P, TB, K1]), ALU.mult))
                    own.did(dve.tensor_copy(pv[:, :, :, 0].bitcast(I32), ci[:, bass.ds(b * TB + CI_TOK, TB)]
                                            .unsqueeze(2).broadcast_to([P, TB, K1])))

                def place(b):
                    dve.wait_ge(c_pos, b + 1)
                    own.did(dve.tensor_reduce(seltot1, sel1.rearrange("p t e -> p e t"), AX, ALU.add))
                    own.did(dve.tensor_tensor(prod1.rearrange("p (t k e) -> p t k e", k=K1, e=8),
                                              oh1.rearrange("p (t k e) -> p t k e", k=K1, e=8),
                                              pos1_ps[:, 0:TB * 8].rearrange("p (t e) -> p t e", e=8).unsqueeze(2)
                                              .broadcast_to([P, TB, K1, 8]), ALU.mult))
                    own.wait()
                    own.did(dve.tensor_tensor(carry1, carry1, seltot1, ALU.add))
                    own.did(dve.tensor_reduce(pp1, prod1.rearrange("p (j e) -> p j e", e=8), AX, ALU.add))
                    own.wait()
                    own.did(dve.tensor_copy(posi, pp1))
                    own.wait()
                    own.did(dve.tensor_scalar(hi_i, posi, 7, None, ALU.logical_shift_right))
                    own.did(dve.tensor_scalar(lo_i, posi, P - 1, None, ALU.bitwise_and))
                    own.wait()
                    own.did(dve.tensor_copy(hi_f, hi_i))
                    own.did(dve.tensor_copy(lo_f, lo_i))
                    own.wait()
                    own.did(dve.scalar_tensor_tensor(hi_f, idxf1, float(TT), hi_f, ALU.mult, ALU.add))
                    own.wait()
                    dve.scalar_tensor_tensor(dest1, lo_f, float(COLS1), hi_f, ALU.mult, ALU.add).then_inc(c_scat, 1)

                def batch(b, more, first=False):
                    for t in range(TB):
                        if t == TB - 1:
                            scores(b)
                        if t >= 2:
                            residual(b, t - 2)
                        elif later(b):
                            residual(b - 1, TB - 2 + t)
                        if more or t < TB - 1:
                            conv(*nxt_tile(b, t))
                        if t:
                            leave_h(b, t - 1)
                        elif later(b):
                            leave_h(b - 1, TB - 1)
                        product(b, t)
                        if more or t < TB - 1:
                            leave_y(*nxt_tile(b, t))
                        if first and t == 0:
                            leave_weights(2)
                        if t == TB - 1:
                            choose(b)
                            place(b)
                own.did(dve.memset(prob, 0.0))
                own.did(dve.memset(biased, -1.0e30))
                own.did(dve.memset(carry1, 0.0))
                dve.wait_ge(small_in, 80)
                own.wait()
                conv(0, 0)
                leave_weights(0)
                leave_y(0, 0)
                leave_weights(1)
                batch(0, True, True)
                with dve.Fori(1, B - 1) as b:
                    own.loop(b, PER_BATCH_C, 1)
                    own.wait()
                    batch(b, True)
                    own.end(B - 2)
                batch(B - 1, False)
                residual(B - 1, TB - 2)
                leave_h(B - 1, TB - 1)
                residual(B - 1, TB - 1)

            @block.tensor
            def _(pe):
                def turn_x(b, t):
                    n = b * TB + t
                    pe.wait_ge(x1_in[t], 16 * (b + 1))
                    if later(b, t):
                        pe.wait_ge(c_x_copied, n)
                    for c in range(DC):
                        mm = pe.transpose(PS[4][:, c * P:(c + 1) * P], x1[t][:, c:D:DC], ident)
                    mm.then_inc(c_x_turned, 1)

                def logits_and_rows(b, t):
                    n = b * TB + t
                    pe.wait_ge(conv_done, n + 1)
                    if t == 0 and later(b):
                        pe.wait_ge(c_lm, b)
                    for c in range(DC):
                        mm = pe.matmul(log1[:, t, 0:E1], yT[t % 2][:, c, :], gate1_w[:, c, :], start=c == 0, stop=c == DC - 1)
                    mm.then_inc(c_log_ready, 1)
                    if later(b, t):
                        pe.wait_ge(y_copied, n)
                    for c in range(DC):
                        mm = pe.transpose(ybk_ps[:, c:D:DC], yT[t % 2][:, c, :], ident)
                    mm.then_inc(y_turned, 1)

                def product(m, cols_hi, cols_lo, bank):
                    for c in range(DC):
                        w = slice(c * D, (c + 1) * D)
                        for k, (x_part, w_part) in enumerate(((cols_hi, sh1_hi[m]), (cols_hi, sh1_lo[m]), (cols_lo, sh1_hi[m]))):
                            mm = pe.matmul(bank[:, :], x_part[:, c, :], w_part[:, w], start=c + k == 0,
                                           stop=c == DC - 1 and k == 2)
                    return mm

                def products(b, t, m, bank, done, free):
                    n = b * TB + t
                    if later(b, t):
                        pe.wait_ge(free, n)
                    else:
                        pe.wait_ge(sh1_left, m + 1)
                    pe.wait_ge(y_left, n + 1)
                    product(m, y_hi[t % 2], y_lo[t % 2], bank).then_inc(done, 1)

                def turn_h(b, t):
                    n = b * TB + t
                    pe.wait_ge(c_gu, n + 1)
                    if later(b, t):
                        pe.wait_ge(c_hc, n)
                    for c in range(DC):
                        mm = pe.transpose(PS[2][:, c * P:(c + 1) * P], gu1[:, c:D:DC], ident)
                    mm.then_inc(c_ht, 1)

                def down(b, t):
                    n = b * TB + t
                    pe.wait_ge(c_hc, n + 1)
                    if later(b, t):
                        pe.wait_ge(c_o, n)
                    else:
                        pe.wait_ge(sh1_left, 3)
                    product(2, h_hi, h_lo, PS[3]).then_inc(c_d, 1)

                def positions(b):
                    pe.wait_ge(c_sel, b + 1)
                    for t in range(TB):
                        to = pos1_ps[:, t * 8:(t + 1) * 8]
                        pe.matmul(to, trib, sel1[:, t, :], start=True, stop=False)
                        for s in range(t):
                            pe.matmul(to, onesb, sel1[:, s, :], start=False, stop=False)
                        mm = pe.matmul(to, onesb, carry1, start=False, stop=True)
                    mm.then_inc(c_pos, 1)

                def batch(b, more, first=False):
                    for t in range(TB):
                        prev = None if first and t == 0 else ((b, t - 1) if t else (b - 1, TB - 1))
                        if more or t < TB - 1:
                            turn_x(*nxt_tile(b, t))
                        products(b, t, 0, PS[0], c_g, c_sil)
                        if prev:
                            turn_h(*prev)
                        products(b, t, 1, PS[1], c_u, c_gu)
                        if more or t < TB - 1:
                            logits_and_rows(*nxt_tile(b, t))
                        if prev:
                            down(*prev)
                        if t == TB - 1:
                            positions(b)
                pe.wait_ge(small_in, 80)
                turn_x(0, 0)
                logits_and_rows(0, 0)
                batch(0, True, True)
                with pe.Fori(1, B - 1) as b:
                    batch(b, True)
                batch(B - 1, False)
                turn_h(B - 1, TB - 1)
                down(B - 1, TB - 1)

        late.close()
        arena = sb("arena", [P, E1 * SLOT])

        n_e = take(misc, M2, 8)
        nf = take(misc, M2 + 8, 8)
        ni = take(misc, M2 + 16, 8, I32)
        tiles_e = take(misc, M2 + 24, 8)
        ends = take(misc, M2 + 32, 8)
        past = take(misc, M2 + 40, TILES1 * E1).rearrange("p (j e) -> p j e", e=E1)
        past_n = take(misc, M2 + 420, TILES1 * E1).rearrange("p (j e) -> p j e", e=E1)
        tile_e = take(misc, M5, TILES1)
        tile_b = take(misc, M5 + 54, TILES1)
        expert_i = take(misc, M5 + 108, TILES1, I32)
        column_i = take(misc, M5 + 162, TILES1, I32)
        M6 = M5 + 216
        w_in, table1_in, l_pe, l_dve = sem("w_in"), sem("table1_in"), sem("l_pe"), sem("l_dve")

        def expert_load(sp, e):
            for m in range(3):
                sp.dma_start(arena[:, bass.ds(e * SLOT + m * DC * D, DC * D)],
                             w_res[:, bass.ds(e * SLOT + SLOT + m * DC * D, DC * D)]).then_inc(w_in, 16)

        with nc.Block() as block:
            @block.sync
            def _(sp):
                sp.dma_start(take(misc, M6, 2 * COLS1), slots1.rearrange("(p c) w -> p (c w)", p=P)).then_inc(table1_in, 16)
                expert_load(sp, 0)
                sp.wait_ge(table1_in, 16)

            @block.tensor
            def _(pe):
                pe.matmul(PS[7][:, 0:8], onesb, carry1, start=True, stop=True).then_inc(l_pe, 1)

            @block.vector
            def _(dve):
                own = Chain(dve, l_dve)

                def step(ins):
                    own.did(ins)
                    own.wait()
                dve.wait_ge(l_pe, 1)
                step(dve.tensor_scalar(n_e, PS[7][:, 0:8], float(P - 1), None, ALU.add))
                step(dve.tensor_copy(ni, n_e))
                step(dve.tensor_scalar(ni, ni, 7, None, ALU.logical_shift_right))
                step(dve.tensor_copy(tiles_e, ni))
                step(dve.tensor_copy(ends, tiles_e))
                for e in range(1, E1):
                    step(dve.tensor_tensor(ends[:, e:e + 1], ends[:, e - 1:e], tiles_e[:, e:e + 1], ALU.add))
                step(dve.tensor_tensor(past, cf[:, CF_J:CF_J + TILES1].unsqueeze(2).broadcast_to([P, TILES1, E1]),
                                       ends[:, 0:E1].unsqueeze(1).broadcast_to([P, TILES1, E1]), ALU.is_ge))
                step(dve.tensor_tensor(past_n, past, tiles_e[:, 0:E1].unsqueeze(1).broadcast_to([P, TILES1, E1]), ALU.mult))
                step(dve.tensor_reduce(tile_e, past, AX, ALU.add))
                step(dve.tensor_reduce(tile_b, past_n, AX, ALU.add))
                step(dve.tensor_tensor(tile_b, cf[:, CF_J:CF_J + TILES1], tile_b, ALU.subtract))
                step(dve.scalar_tensor_tensor(tile_b, tile_e, float(TT), tile_b, ALU.mult, ALU.add))
                step(dve.tensor_scalar(column_i, tile_b, float(BINS), None, ALU.min))
                step(dve.tensor_scalar(expert_i, tile_e, float(E1 - 1), None, ALU.min))

        expert_stage("e1", TILES1, D, [(0, P)] * DC, F32, y_rows, slots1, COLS1, out, M3, M6, None,
                     (column_i, expert_i), w_in)


def layout(inputs):
    import numpy as np
    g = {k: np.asarray(v) for k, v in inputs.items()}
    sg, su = g["L0_ffn_sh_gate"].T, g["L0_ffn_sh_up"].T
    cf = np.zeros((P, NCF), np.float32)
    cf[:, CF_ID:CF_ID + P] = np.eye(P)
    cf[:, CF_ONE:CF_ONE + P] = 1
    cf[:, CF_TRI:CF_TRI + P] = np.triu(np.ones((P, P)), 1)
    cf[:, CF_BIT:CF_BIT + STEPS] = [-1.0] + [2.0 ** (30 - i) for i in range(31)]
    cf[:, CF_I64:CF_I64 + E0] = np.arange(E0)
    cf[:, CF_J:CF_J + TILES1] = np.arange(TILES1)
    cf[:, CF_I8:CF_I8 + 8] = np.arange(8)
    cf[:, CF_HALF:CF_HALF + P] = -0.5
    ci = np.zeros((P, 49), np.int32)
    ci[:, CI_BIT:CI_BIT + STEPS] = [2 ** (30 - i) for i in range(31)] + [0]
    ci[:, CI_TOK:CI_TOK + TT] = np.arange(T).reshape(TT, P).T
    ci[:, CI_PAD] = T + np.arange(P)
    routed = [g["L1_ffn_W1"], g["L1_ffn_Wg"], g["L1_ffn_W2"]]
    experts = [[w[e] for w in routed] for e in range(E1)]
    experts.insert(0, [g["L1_ffn_Ws1"], g["L1_ffn_Wsg"], g["L1_ffn_Ws2"]])
    w_res = np.concatenate([w.reshape(P, DC * D) for e in experts for w in e], 1)
    return {
        "x": g["x"].reshape(T, D), "fside": g["fside_BxSx1_0"].reshape(TT, P).T, "cond": g["cond_2048"],
        "gate0": g["L0_ffn_gate_w"].T, "w_gate": g["L0_ffn_w_gate"], "w_up": g["L0_ffn_w_up"],
        "w_down": g["L0_ffn_w_down"],
        "sh_in": np.concatenate([sg[:, :F0], su[:, :F0], sg[:, F0:], su[:, F0:]], 1),
        "sh_down": g["L0_ffn_sh_down"].T, "conv_b": g["L1_cond_b"], "w_res": w_res,
        "gate1": g["L1_ffn_gate_w"], "gate1_b": g["L1_ffn_gate_b"], "biases": g["L1_ffn_biases"],
        "c_f32": cf, "c_i32": ci,
    }


def kernel(**inputs):
    import numpy as np
    import concourse.bacc as bacc
    from concourse.bass_utils import run_bass_kernel_spmd

    arrays = {n: np.ascontiguousarray(a) for n, a in layout(inputs).items()}
    nc = bacc.Bacc("TRN2", target_bir_lowering=False, num_devices=1)
    args = {n: nc.dram_tensor(f"in_{n}", a.shape, mybir.dt.from_np(a.dtype), kind="ExternalInput").ap()
            for n, a in arrays.items()}
    result = nc.dram_tensor("out_rows", (T + P, D), F32, kind="ExternalOutput").ap()
    build(nc, out=result, **args)
    ran = run_bass_kernel_spmd(nc, [{f"in_{n}": a for n, a in arrays.items()}], core_ids=[0])
    return ran.results[0]["out_rows"][:T].reshape(B, S, D)
```

```python
from contextlib import ExitStack

import concourse.bass as bass
from concourse import mybir

ALU = mybir.AluOpType
ACT = mybir.ActivationFunctionType
AX = mybir.AxisListType.X
F32, F32R, BF16 = mybir.dt.float32, mybir.dt.float32r, mybir.dt.bfloat16
I32, U32 = mybir.dt.int32, mybir.dt.uint32

P = 128
B, S, D = 4, 512, 512
T = B * S
TB = S // P
TT = T // P
DC = D // P
KEEP = 5120
E0, K0, F0, CAP = 64, 6, 352, 128
HALVES = 2
F0C = [(0, 128), (128, 128), (256, 96)]
E1, K1 = 7, 3
BINS = E1 * TT
COLS1 = BINS + 2
PAIRS1 = T * K1 // (2 * P) + E1 - 1
TILES1 = 2 * PAIRS1
STEPS = 32
DIAG = -3.0e38
INV_SQRT_N = 0.04419417306780815
OUT_OF_BOUNDS = 1.0e6
COARSE, FINE = 1152, 896
ABOVE = 1.0 + 2.0 ** -10
PER_BATCH = 38
PER_BATCH_C = 80

CF_ID, CF_ONE, CF_TRI, CF_BIT, CF_I64 = 0, 128, 256, 384, 416
CF_J, CF_I8 = 480, 480 + PAIRS1
CF_HALF = CF_I8 + 8
NCF = CF_HALF + P
CI_BIT, CI_TOK, CI_PAD = 0, 32, 48


class Chain:

    def __init__(self, eng, sem):
        self.eng, self.sem, self.n, self.i, self.per = eng, sem, 0, None, 0

    def did(self, ins):
        ins.then_inc(self.sem, 1)
        self.n += 1
        return self.n

    def at(self, n):
        return n if self.i is None else self.i * self.per + n

    def wait(self, n=None):
        self.eng.wait_ge(self.sem, self.at(self.n if n is None else n))

    def loop(self, i, per, first=0):
        self.start, self.i, self.per, self.first = self.n, i, per, first
        self.n = self.start - first * per

    def end(self, count):
        assert self.n == self.start - self.first * self.per + self.per, (self.n, self.start, self.per)
        self.i, self.n = None, self.start + count * self.per


def build(nc, x, fside, cond, gate0, w_gate, w_up, w_down, sh_in, sh_down, conv_b, w_res,
          gate1, gate1_b, biases, c_f32, c_i32, out):
    with ExitStack() as ctx:
        def sb(name, shape, dt=F32, till=ctx):
            return till.enter_context(nc.sbuf_tensor(name, shape, dt))

        def sem(name):
            return ctx.enter_context(nc.semaphore(name))

        def dram(name, shape, dt=F32):
            return nc.dram_tensor(name, shape, dt, kind="Internal").ap()

        mask_rows = dram("mask_rows", (T + P, D), BF16)
        acc0 = dram("acc0", (T + P, D))
        y_rows = dram("y_rows", (T + P, D))
        slots0 = dram("slots0", (P * E0, 2))
        slots1 = dram("slots1", (P * COLS1, 2))

        SLOT = 3 * DC * D
        misc = sb("misc", [P, 6100])
        cf = sb("cf", [P, NCF])
        cb = sb("cb", [P, 384], BF16)
        ci = sb("ci", [P, 49], I32)
        early = ctx.enter_context(ExitStack())
        front = sb("front", [P, 8192 + 6 * D + DC * E0 + 15488], till=early)
        sh_parts = sb("sh_parts", [P, 2 * DC * 4 * F0], F32R, till=early)
        mask_cols = sb("mask_cols", [P, TB * DC * P], F32R, till=early)
        PS = [ctx.enter_context(nc.psum_tensor(f"ps{i}", [P, 512], F32)) for i in range(8)]

        ident, ones, tri = cf[:, CF_ID:CF_ID + P], cf[:, CF_ONE:CF_ONE + P], cf[:, CF_TRI:CF_TRI + P]
        identb, trib, onesb = (cb[:, c:c + P] for c in (CF_ID, CF_TRI, CF_ONE))

        def take(region, at, words, dt=F32):
            v = region[:, at:at + words]
            return v if dt == F32 else v.bitcast(dt)

        def later(b, t=0):
            return t > 0 or not isinstance(b, int) or b > 0

        val = take(front, 0, TT * S)
        sh_dw = take(front, TT * S, 6 * D).rearrange("p (c n) -> p c n", c=6)
        gate0_w = take(front, TT * S + 6 * D, DC * E0).rearrange("p (c e) -> p c e", c=DC)
        A2 = TT * S + 6 * D + DC * E0
        junk = take(front, A2, 1024, BF16)
        junk_a = take(front, A2 + 1024, 1024, BF16)
        cond_bc = take(front, A2 + 2048, B * S)
        val16 = take(front, A2 + 4096, TT * S // 2, BF16)
        sh_w = take(front, A2 + 8192, DC * 4 * F0).rearrange("p (c f) -> p c f", c=DC)
        sh_hi, sh_lo = (sh_parts[:, i * DC * 4 * F0:(i + 1) * DC * 4 * F0].rearrange("p (c f) -> p c f", c=DC)
                        for i in range(2))

        gate0_parts = take(misc, 5400, 3 * DC * E0 // 2, BF16).rearrange("p (k c e) -> p k c e", k=3, c=DC)
        gate0_left = take(misc, 5400 + 3 * DC * E0 // 2, DC * E0).rearrange("p (c e) -> p c e", c=DC)

        fs = take(misc, 0, TT)
        rmax = take(misc, 16, TT)
        nmax = take(misc, 32, TT)
        esum = take(misc, 48, TT)
        rsum = take(misc, 64, TT)
        fac = take(misc, 80, TT)
        cnt = take(misc, 96, B)
        cand = take(misc, 100, B, I32)
        incr = take(misc, 104, B, I32)
        candf = take(misc, 100, B)
        cand16 = candf.bitcast(BF16)[:, 1:2 * B:2]
        cnt_a = take(misc, 340 + D, B)
        step_f = take(misc, 348 + D, B)
        step_i = take(misc, 352 + D, B, I32)
        empty = take(misc, 110, COLS1 * 2, I32).rearrange("p (c w) -> p c w", w=2)
        MZ = 110 + COLS1 * 2
        zeros = take(misc, MZ, D)
        M2 = MZ + D + 20
        assert MZ <= 340

        x_t = x.rearrange("(t p) d -> p t d", p=P)
        x_in = [sem(f"x_in{b}") for b in range(B)]
        const_in, side_in, shw_in, init_out = sem("const_in"), sem("side_in"), sem("shw_in"), sem("init_out")
        empty_ready, cand_ready, counted_a, halved = sem("empty_ready"), sem("cand_ready"), sem("counted_a"), sem("halved")
        max_ready, exp_ready, scored, diag_set = sem("max_ready"), sem("exp_ready"), sem("scored"), sem("diag_set")
        counted, totalled, split = sem("counted"), sem("totalled"), sem("split")
        dve_did = sem("dve_did")

        with nc.Block() as block:
            @block.sync
            def _(sp):
                for b in range(B):
                    sp.dma_start(val[:, b * TB * S:(b + 1) * TB * S].rearrange("p (t d) -> p t d", t=TB),
                                 x_t[:, b * TB:(b + 1) * TB, :]).then_inc(x_in[b], 16)
                    if b == 0:
                        sp.dma_start(cf[:, :], c_f32).then_inc(const_in, 16)
                        sp.dma_start(ci[:, :], c_i32).then_inc(const_in, 16)
                        sp.dma_start(fs, fside).then_inc(side_in, 16)
                        sp.dma_start(cond_bc, cond.rearrange("b d -> (b d)").partition_broadcast(P)).then_inc(side_in, 16)
                sp.dma_start(sh_w, sh_in.rearrange("(p c) f -> p c f", c=DC)).then_inc(shw_in, 16)
                for h in range(HALVES):
                    sp.dma_start(sh_dw[:, 3 * h:3 * h + 2, :],
                                 sh_down[h * F0:h * F0 + 256, :].rearrange("(c p) n -> p c n", p=P)).then_inc(shw_in, 16)
                    sp.dma_start(sh_dw[0:96, 3 * h + 2, :], sh_down[h * F0 + 256:(h + 1) * F0, :]).then_inc(shw_in, 16)
                sp.dma_start(gate0_w, gate0.rearrange("(p c) e -> p c e", c=DC)).then_inc(shw_in, 16)
                sp.wait_ge(shw_in, 96)
                sp.wait_ge(empty_ready, 3)
                sp.dma_start(slots0.rearrange("(p c) w -> p (c w)", p=P), empty[:, 0:E0, :].rearrange("p c w -> p (c w)")
                             .bitcast(F32)).then_inc(init_out, 16)
                sp.dma_start(slots1.rearrange("(p c) w -> p (c w)", p=P), empty.rearrange("p c w -> p (c w)")
                             .bitcast(F32)).then_inc(init_out, 16)
                sp.dma_start(mask_rows[T:T + P, :], zeros[:, 0:D // 2].bitcast(BF16)).then_inc(init_out, 16)
                for rows in (acc0, y_rows, out):
                    sp.dma_start(rows[T:T + P, :], zeros).then_inc(init_out, 16)
                sp.wait_ge(init_out, 96)

            @block.vector
            def _(dve):
                own = Chain(dve, dve_did)
                dve.memset(zeros, 0.0).then_inc(empty_ready, 1)
                dve.memset(empty[:, :, 1], 0).then_inc(empty_ready, 1)
                own.did(dve.memset(cand, 0))
                dve.wait_ge(const_in, 32)
                own.did(dve.tensor_copy(cb[:, :], cf[:, 0:3 * P]))
                dve.tensor_copy(empty[:, :, 0], ci[:, CI_PAD:CI_PAD + 1].broadcast_to([P, COLS1])).then_inc(empty_ready, 1)

                def maxima(b):
                    t4 = slice(b * TB, (b + 1) * TB)
                    dve.wait_ge(x_in[b], 16)
                    own.did(dve.tensor_reduce(rmax[:, t4], val[:, b * TB * S:(b + 1) * TB * S]
                                              .rearrange("p (t d) -> p t d", t=TB), AX, ALU.max))
                    own.wait()
                    dve.tensor_scalar(nmax[:, t4], rmax[:, t4], -1.0, None, ALU.mult).then_inc(max_ready, 1)

                def score(b):
                    t4 = slice(b * TB, (b + 1) * TB)
                    dve.wait_ge(exp_ready, TB * (b + 1))
                    own.did(dve.reciprocal(rsum[:, t4], esum[:, t4]))
                    own.wait()
                    own.did(dve.tensor_scalar(rsum[:, t4], rsum[:, t4], INV_SQRT_N, None, ALU.mult))
                    own.wait()
                    own.did(dve.tensor_tensor(fac[:, t4], rsum[:, t4], fs[:, t4], ALU.mult))
                    own.wait()
                    for t in range(b * TB, (b + 1) * TB):
                        v = val[:, t * S:(t + 1) * S]
                        dve.scalar_tensor_tensor(v, v, fac[:, t:t + 1], cond_bc[:, b * S:(b + 1) * S],
                                                 ALU.mult, ALU.mult).then_inc(scored, 1)
                maxima(0)
                dve.wait_ge(side_in, 32)
                for b in range(1, B):
                    maxima(b)
                    score(b - 1)
                score(B - 1)

                def count(b, i, coarse):
                    if later(i, b):
                        dve.wait_ge(counted, 4 * i + b)
                    own_, at, n = (val16, cand16, COARSE) if coarse else (val, candf, FINE)
                    dve.tensor_scalar(junk[:, 0:n], own_[:, b * TB * S:b * TB * S + n], at[:, b:b + 1], 0.0,
                                      ALU.is_ge, ALU.add, accum_out=cnt[:, b:b + 1]).then_inc(counted, 1)

                def judge(c, i, coarse):
                    dve.wait_ge(totalled, 4 * i + c + 2)
                    signs = TB * S - (COARSE if coarse else FINE)
                    own.did(dve.tensor_scalar(incr[:, c:c + 2], PS[c // 2][:, c:c + 2], KEEP - 0.5 - signs * P / 2,
                                              cf[:, bass.ds(i + CF_BIT, 1)], ALU.is_lt, ALU.mult))

                def next_bit(c, i):
                    own.wait()
                    dve.scalar_tensor_tensor(cand[:, c:c + 2], incr[:, c:c + 2], ci[:, bass.ds(i + CI_BIT, 1)],
                                             cand[:, c:c + 2], ALU.bitwise_xor, ALU.bitwise_xor).then_inc(cand_ready, 1)

                def rounds(i, coarse, before):
                    dve.wait_ge(cand_ready, 2 * i)
                    count(0, i, coarse)
                    judge(2, i - 1, before)
                    count(1, i, coarse)
                    next_bit(2, i - 1)
                    dve.wait_ge(cand_ready, 2 * i + 1)
                    count(2, i, coarse)
                    judge(0, i, coarse)
                    count(3, i, coarse)
                    next_bit(0, i)

                dve.sem_inc(cand_ready, 1)
                for b in range(B):
                    dve.wait_ge(halved, b + 1)
                    count(b, 0, True)
                judge(0, 0, True)
                next_bit(0, 0)
                HALF = STEPS // 2
                rounds(1, True, True)
                with dve.Fori(1, HALF // 2) as j:
                    own.loop(j, 4, 1)
                    rounds(2 * j, True, True)
                    rounds(2 * j + 1, True, True)
                    own.end(HALF // 2 - 1)
                rounds(HALF, False, True)
                rounds(HALF + 1, False, False)
                with dve.Fori(HALF // 2 + 1, STEPS // 2) as j:
                    own.loop(j, 4, HALF // 2 + 1)
                    rounds(2 * j, False, False)
                    rounds(2 * j + 1, False, False)
                    own.end(HALF // 2 - 1)
                judge(2, STEPS - 1, False)
                next_bit(2, STEPS - 1)
                dve.wait_ge(cand_ready, 2 * STEPS + 1)
                own.did(dve.tensor_scalar(step_f, candf, 0.0, -2.0, ALU.is_lt, ALU.mult))
                own.wait()
                own.did(dve.tensor_scalar(step_f, step_f, 1.0, None, ALU.add))
                own.wait()
                own.did(dve.tensor_copy(step_i, step_f))
                own.wait()
                own.did(dve.tensor_tensor(cand, cand, step_i, ALU.add))
                own.wait()
                for b in range(B):
                    dve.wait_ge(counted, B * STEPS + b)
                    dve.tensor_scalar(junk[:, 0:TB * S], val[:, b * TB * S:(b + 1) * TB * S], candf[:, b:b + 1], 0.0,
                                      ALU.is_ge, ALU.add, accum_out=cnt[:, b:b + 1]).then_inc(counted, 1)
                for c in (0, 2):
                    dve.wait_ge(totalled, 4 * STEPS + c + 2)
                    own.did(dve.tensor_scalar(step_f[:, c:c + 2], PS[c // 2][:, c:c + 2], float(KEEP), None, ALU.is_lt))
                own.wait()
                own.did(dve.scalar_tensor_tensor(step_f, step_f, -1.0, step_i, ALU.mult, ALU.mult))
                own.wait()
                own.did(dve.tensor_copy(step_i, step_f))
                own.wait()
                own.did(dve.tensor_tensor(cand, cand, step_i, ALU.add))
                own.wait()

            @block.scalar
            def _(act):
                for b in range(B):
                    act.wait_ge(max_ready, b + 1)
                    for t in range(b * TB, (b + 1) * TB):
                        v = val[:, t * S:(t + 1) * S]
                        act.activation(v, v, ACT.Exp, bias=nmax[:, t:t + 1], accum_out=esum[:, t:t + 1]).then_inc(exp_ready, 1)
                upper = val.bitcast(BF16)[:, 1:2 * TT * S:2]
                for b in range(B):
                    c = slice(b * TB * S, (b + 1) * TB * S)
                    act.wait_ge(diag_set, b + 1)
                    act.copy(val16[:, c], upper[:, c]).then_inc(halved, 1)

                def count(b, i, coarse):
                    if b % 2 == 0:
                        act.wait_ge(cand_ready, 2 * i + b // 2 if later(i) else 1)
                    if later(i, b):
                        act.wait_ge(counted_a, 4 * i + b)
                    if later(i):
                        act.wait_ge(totalled, 4 * (i - 1) + b + 1)
                    own_, n = (val16, COARSE) if coarse else (val, FINE)
                    act.activation(junk_a[:, 0:TB * S - n], own_[:, b * TB * S + n:(b + 1) * TB * S], ACT.Sign,
                                   scale=-ABOVE if coarse else -1.0, bias=candf[:, b:b + 1], accum_out=cnt_a[:, b:b + 1]).then_inc(counted_a, 1)
                act.wait_ge(halved, B)
                for b in range(B):
                    count(b, 0, True)
                for b in range(B):
                    count(b, 1, True)
                for first, last, coarse in ((1, STEPS // 4, True), (STEPS // 4, STEPS // 2, False)):
                    with act.Fori(first, last) as j:
                        for u in range(2):
                            for b in range(B):
                                count(b, 2 * j + u, coarse)

            @block.gpsimd
            def _(pool):
                for b in range(B):
                    pool.wait_ge(scored, TB * (b + 1))
                    v = val[:, b * TB * S:(b + 1) * TB * S].rearrange("p (t d) -> p t d", t=TB)
                    pool.affine_select(out=v, in_=v, compare_op=ALU.not_equal, fill=DIAG, base=0,
                                       pattern=[[P, TB], [-1, S]], channel_multiplier=1).then_inc(diag_set, 1)
                pool.wait_ge(shw_in, 96)
                pool.tensor_copy(sh_hi, sh_w).then_inc(split, 1)
                pool.wait_ge(split, 1)
                pool.tensor_tensor(sh_lo, sh_w, sh_hi, ALU.subtract).then_inc(split, 1)
                pool.tensor_copy(gate0_parts[:, 0], gate0_w).then_inc(split, 1)
                pool.wait_ge(split, 3)
                pool.tensor_tensor(gate0_left, gate0_w, gate0_parts[:, 0], ALU.subtract).then_inc(split, 1)
                pool.wait_ge(split, 4)
                pool.tensor_copy(gate0_parts[:, 1], gate0_left).then_inc(split, 1)
                pool.wait_ge(split, 5)
                pool.tensor_tensor(gate0_left, gate0_left, gate0_parts[:, 1], ALU.subtract).then_inc(split, 1)
                pool.wait_ge(split, 6)
                pool.tensor_copy(gate0_parts[:, 2], gate0_left).then_inc(split, 1)

            @block.tensor
            def _(pe):
                half = cf[:, CF_HALF:CF_HALF + P]

                def total(b, i):
                    pe.wait_ge(counted, 4 * i + b + 1)
                    pe.matmul(PS[b // 2][:, b:b + 1], ones, cnt[:, b:b + 1], start=True, stop=False)
                    pe.wait_ge(counted_a, 4 * i + b + 1)
                    pe.matmul(PS[b // 2][:, b:b + 1], half, cnt_a[:, b:b + 1], start=False, stop=True).then_inc(totalled, 1)
                pe.wait_ge(const_in, 32)
                for i in range(2):
                    for b in range(B):
                        total(b, i)
                with pe.Fori(1, STEPS // 2) as j:
                    for u in range(2):
                        for b in range(B):
                            total(b, 2 * j + u)
                for b in range(B):
                    pe.wait_ge(counted, 4 * STEPS + b + 1)
                    pe.matmul(PS[b // 2][:, b:b + 1], ones, cnt[:, b:b + 1], start=True, stop=True).then_inc(totalled, 1)

        xTn = take(front, A2, TB * DC * P // 2, BF16)
        xT = mask_cols
        ge = take(front, A2 + 2048, TB * S)
        eq = take(front, A2 + 4096, TB * S)
        cum = take(front, A2 + 6144, TB * S)
        mask = take(front, A2 + 8192, TB * S // 2, BF16)
        oh = take(front, A2 + 9216, TB * K0 * E0)
        prod = take(front, A2 + 10752, TB * K0 * E0)
        x_res = [take(front, A2 + 12288 + i * D, D) for i in range(2)]
        ob = [take(front, A2 + 13312 + i * D, D) for i in range(2)]
        sil = take(front, A2 + 14336, F0)
        gu = take(front, A2 + 14720, F0)
        hT = take(front, A2 + 15104, 384).rearrange("p (c n) -> p c n", c=3)
        gecnt = take(misc, M2, 1)
        rc = take(misc, M2 + 4, TB)
        rcex = take(misc, M2 + 8, 5)
        lim = take(misc, M2 + 16, 5)
        top = take(misc, M2 + 24, TB * 8).rearrange("p (t k) -> p t k", k=8)
        idx = take(misc, M2 + 56, TB * 8, U32).rearrange("p (t k) -> p t k", k=8)
        idxf = take(misc, M2 + 88, TB * K0)
        es = take(misc, M2 + 112, TB)
        td = take(misc, M2 + 116, TB * 8).rearrange("p (t k) -> p t k", k=8)
        posk = take(misc, M2 + 148, TB * K0)
        over = take(misc, M2 + 172, TB * K0)
        dest = take(misc, M2 + 196, TB * K0, I32)
        pairs = take(misc, M2 + 220, TB * K0 * 2)
        lm = take(misc, M2 + 268, TB * E0).rearrange("p (t e) -> p t e", e=E0)
        selb = take(misc, M2 + 524, TB * E0 // 2, BF16).rearrange("p (t e) -> p t e", e=E0)
        carry = take(misc, M2 + 652, E0 // 2, BF16)
        seltot = take(misc, M2 + 684, E0)
        M3 = M2 + 748

        names = ("g_ready sil_ready u_ready gu_ready t_ready ht_ready d_ready o_ready tie_in tie_ready mask_ready "
                 "xt_ready xtn_ready xt_moved log_ready lm_ready exp_done sel_ready pos_ready scat_ready scat_done "
                 "mask_out pool_step dve_step dve2")
        (g_ready, sil_ready, u_ready, gu_ready, t_ready, ht_ready, d_ready, o_ready, tie_in, tie_ready, mask_ready,
         xt_ready, xtn_ready, xt_moved, log_ready, lm_ready, exp_done, sel_ready, pos_ready, scat_ready, scat_done,
         mask_out, pool_step, dve_step, dve2) = (sem(n) for n in names.split())
        o_out = [sem(f"o_out{i}") for i in range(2)]
        xr_in = [sem(f"xr_in{i}") for i in range(2)]
        gate_ps, up_ps, t_ps, d_ps, xt_ps, tie_ps, log_ps, pos_ps = PS
        xt_psb = xt_ps[:, 0:DC * P // 2].bitcast(BF16)
        ITEMS = TB * HALVES
        acc0_t = acc0[0:T].rearrange("(t p) d -> t p d", p=P)
        x_tp = x.rearrange("(t p) d -> t p d", p=P)
        mask_bt = mask_rows[0:T].rearrange("(b t p) d -> b p t d", p=P, t=TB)

        with nc.Block() as block:
            @block.sync
            def _(sp):
                def load_x(b, t):
                    sp.dma_start(x_res[t % 2], x_tp[b * TB + t]).then_inc(xr_in[t % 2], 16)

                def mask_store(b):
                    sp.wait_ge(mask_ready, b + 1)
                    sp.dma_start(mask_bt[b], mask.rearrange("p (t d) -> p t d", t=TB)).then_inc(mask_out, 16)

                def batch(b, more):
                    for t in range(TB):
                        if t == 2 and more:
                            mask_store(b + 1)
                        sp.wait_ge(o_ready, b * TB + t + 1)
                        sp.dma_start(acc0_t[b * TB + t], ob[t % 2]).then_inc(o_out[t % 2], 16)
                        if t < 2 or more:
                            load_x(b if t < 2 else b + 1, (t + 2) % TB)
                load_x(0, 0)
                load_x(0, 1)
                mask_store(0)
                batch(0, True)
                with sp.Fori(1, B - 1) as i:
                    batch(i, True)
                batch(B - 1, False)
                sp.wait_ge(mask_out, 16 * B)
                for i in range(2):
                    sp.wait_ge(o_out[i], 16 * TT // 2)

            @block.gpsimd
            def _(pool):
                with pool.Fori(0, B) as b:
                    pool.wait_ge(scat_ready, b + 1)
                    pool.sem_inc(pool_step, 1)
                    for j in range(TB * K0):
                        pool.indirect_dma_start(slots0, bass.IndirectOffsetOnAxis(dest[:, j:j + 1].bitcast(U32), 0),
                                                pairs[:, 2 * j:2 * j + 2], None, bounds_check=P * E0 - 1,
                                                oob_is_err=False).then_inc(scat_done, 16)
                pool.wait_ge(scat_done, 16 * TT * K0)

            @block.scalar
            def _(act):
                def copy_x(b, t):
                    act.wait_ge(xt_ready, b * TB + t + 1)
                    act.copy(xTn[:, t * DC * P:(t + 1) * DC * P], xt_psb).then_inc(xtn_ready, 1)

                def softmax(b):
                    act.wait_ge(lm_ready, 2 * b + 2)
                    act.activation(lm, lm, ACT.Exp).then_inc(exp_done, 1)
                    act.activation(td, td, ACT.Exp).then_inc(exp_done, 1)

                def item(b, m):
                    n = b * ITEMS + m
                    act.wait_ge(g_ready, n + 1)
                    if later(b, m):
                        act.wait_ge(gu_ready, n)
                    act.activation(sil, gate_ps[:, 0:F0], ACT.Silu).then_inc(sil_ready, 1)

                def copy_h(b, m):
                    act.wait_ge(t_ready, b * ITEMS + m + 1)
                    act.copy(hT[:, 0:2, :], t_ps[:, 0:256].rearrange("p (c n) -> p c n", c=2))
                    act.copy(hT[0:96, 2, :], t_ps[0:96, 256:384]).then_inc(ht_ready, 1)

                def move(b, t):
                    act.wait_ge(xtn_ready, b * TB + t + 1)
                    if later(b):
                        act.wait_ge(u_ready, (b - 1) * ITEMS + 2 * t + 2)
                    c = slice(t * DC * P, (t + 1) * DC * P)
                    act.copy(xT[:, c], xTn[:, c]).then_inc(xt_moved, 1)

                def batch(b, more):
                    if more:
                        act.wait_ge(xt_moved, TB * (b + 1))
                        act.wait_ge(log_ready, b + 1)
                    for m in range(ITEMS):
                        item(b, m)
                        if m:
                            copy_h(b, m - 1)
                        if more and m in (4, 5):
                            copy_x(b + 1, 2 * m - 8)
                            copy_x(b + 1, 2 * m - 7)
                        if more and m == 7:
                            for t in range(TB - 1):
                                move(b + 1, t)
                            softmax(b + 1)
                    copy_h(b, ITEMS - 1)
                    if more:
                        move(b + 1, TB - 1)
                for t in range(TB):
                    copy_x(0, t)
                    move(0, t)
                softmax(0)
                batch(0, True)
                with act.Fori(1, B - 1) as i:
                    batch(i, True)
                batch(B - 1, False)

            @block.vector
            def _(dve):
                own = Chain(dve, dve2)

                def at_value(b):
                    v = val[:, bass.ds(b * TB * S, TB * S)]
                    thr = candf[:, bass.ds(b, 1)]
                    own.did(dve.tensor_scalar(eq, v, thr, None, ALU.is_equal))
                    own.did(dve.tensor_scalar(ge, v, thr, 0.0, ALU.is_ge, ALU.add, accum_out=gecnt))
                    own.wait()

                def scan(t):
                    c = slice(t * S, (t + 1) * S)
                    own.did(dve.tensor_tensor_scan(cum[:, c], eq[:, c], eq[:, c], 0.0, ALU.add, ALU.max))

                def tie_counts():
                    last = cum.rearrange("p (t s) -> p t s", t=TB)[:, :, S - 1]
                    own.wait()
                    own.did(dve.tensor_copy(rc, last))
                    own.did(dve.memset(rcex[:, 0:1], 0.0))
                    own.wait()
                    for t in range(TB):
                        own.did(dve.tensor_tensor(rcex[:, t + 1:t + 2], rcex[:, t:t + 1], rc[:, t:t + 1], ALU.add))
                        own.wait()
                    dve.tensor_tensor(rcex[:, 4:5], gecnt, rcex[:, 4:5], ALU.subtract).then_inc(tie_in, 1)

                def make_mask(b):
                    dve.wait_ge(tie_ready, b + 1)
                    own.did(dve.tensor_scalar(lim[:, 4:5], tie_ps[:, 4:5], -1.0, float(KEEP), ALU.mult, ALU.add))
                    own.wait()
                    own.did(dve.tensor_scalar(lim[:, 0:4], tie_ps[:, 0:4], lim[:, 4:5], -1.0, ALU.subtract, ALU.mult))
                    own.wait()
                    for t in range(TB):
                        c = slice(t * S, (t + 1) * S)
                        own.did(dve.scalar_tensor_tensor(eq[:, c], cum[:, c], lim[:, t:t + 1], eq[:, c],
                                                         ALU.is_gt, ALU.mult))
                    own.wait()
                    if later(b):
                        dve.wait_ge(mask_out, 16 * b)
                        dve.wait_ge(xt_ready, TB * b)
                    dve.tensor_tensor(mask, ge, eq, ALU.subtract).then_inc(mask_ready, 1)

                def best(b):
                    dve.wait_ge(log_ready, b + 1)
                    dve.sem_inc(dve_step, 1)
                    for t in range(TB):
                        own.did(dve.max(top[:, t, :], log_ps[:, t * E0:(t + 1) * E0]))
                    own.wait()
                    dve.sem_inc(dve_step, 1)
                    for t in range(TB):
                        own.did(dve.max_index(idx[:, t, :], top[:, t, :], log_ps[:, t * E0:(t + 1) * E0]))
                    largest = top[:, :, 0:1]
                    dve.tensor_tensor(lm, log_ps[:, 0:TB * E0].rearrange("p (t e) -> p t e", e=E0),
                                      largest.broadcast_to([P, TB, E0]), ALU.subtract).then_inc(lm_ready, 1)
                    dve.tensor_tensor(td, top, largest.broadcast_to([P, TB, 8]), ALU.subtract).then_inc(lm_ready, 1)
                    own.wait()
                    own.did(dve.tensor_copy(idxf.rearrange("p (t k) -> p t k", k=K0), idx[:, :, 0:K0]))
                    own.wait()

                ohv = oh.rearrange("p (j e) -> p j e", e=E0)

                def one_hot(b):
                    own.did(dve.tensor_tensor(ohv, cf[:, CF_I64:CF_I64 + E0].unsqueeze(1).broadcast_to([P, TB * K0, E0]),
                                              idxf.unsqueeze(2).broadcast_to([P, TB * K0, E0]), ALU.is_equal))
                    own.wait()
                    with nc.allow_low_precision("0 or 1"):
                        dve.tensor_reduce(selb, oh.rearrange("p (t k e) -> p t e k", k=K0, e=E0), AX,
                                          ALU.add).then_inc(sel_ready, 1)

                def weights(b):
                    dve.wait_ge(exp_done, 2 * b + 2)
                    own.did(dve.tensor_reduce(es, lm, AX, ALU.add))
                    own.wait()
                    own.did(dve.reciprocal(es, es))
                    own.wait()
                    if later(b):
                        dve.wait_ge(scat_done, 16 * TB * K0 * b)
                    pv = pairs.rearrange("p (t k w) -> p t k w", k=K0, w=2)
                    own.did(dve.tensor_tensor(pv[:, :, :, 1], td[:, :, 0:K0],
                                              es.unsqueeze(2).broadcast_to([P, TB, K0]), ALU.mult))
                    own.did(dve.tensor_copy(pv[:, :, :, 0].bitcast(I32), ci[:, bass.ds(b * TB + CI_TOK, TB)]
                                            .unsqueeze(2).broadcast_to([P, TB, K0])))

                def place(b):
                    dve.wait_ge(pos_ready, b + 1)
                    own.did(dve.tensor_reduce(seltot, selb.rearrange("p t e -> p e t"), AX, ALU.add))
                    pos = pos_ps[:, 0:TB * E0].rearrange("p (t e) -> p t e", e=E0)
                    own.did(dve.tensor_tensor(prod.rearrange("p (t k e) -> p t k e", k=K0, e=E0),
                                              oh.rearrange("p (t k e) -> p t k e", k=K0, e=E0),
                                              pos.unsqueeze(2).broadcast_to([P, TB, K0, E0]), ALU.mult))
                    own.wait()
                    own.did(dve.tensor_tensor(carry, carry, seltot, ALU.add))
                    own.did(dve.tensor_reduce(posk, prod.rearrange("p (j e) -> p j e", e=E0), AX, ALU.add))
                    own.wait()
                    own.did(dve.tensor_scalar(over, posk, float(CAP), OUT_OF_BOUNDS, ALU.is_ge, ALU.mult))
                    own.did(dve.scalar_tensor_tensor(posk, posk, float(E0), idxf, ALU.mult, ALU.add))
                    own.wait()
                    dve.tensor_tensor(dest, posk, over, ALU.add).then_inc(scat_ready, 1)

                def item(b, m):
                    n = b * ITEMS + m
                    dve.wait_ge(u_ready, n + 1)
                    dve.wait_ge(sil_ready, n + 1)
                    dve.tensor_tensor(gu, sil, up_ps[:, 0:F0], ALU.mult).then_inc(gu_ready, 1)

                def residual(b, t):
                    n = b * TB + t
                    dve.wait_ge(d_ready, n + 1)
                    dve.wait_ge(xr_in[t % 2], 16 * (b * 2 + t // 2 + 1))
                    if t >= 2 or later(b):
                        dve.wait_ge(o_out[t % 2], 16 * (b * 2 + t // 2))
                    dve.tensor_tensor(ob[t % 2], x_res[t % 2], d_ps[:, :], ALU.add).then_inc(o_ready, 1)

                def batch(b, more):
                    nxt = b + 1
                    for m in range(ITEMS):
                        item(b, m)
                        if m == 0:
                            weights(b)
                            place(b)
                        elif m % 2 == 0:
                            residual(b, m // 2 - 1)
                        if not more:
                            continue
                        if m == 1:
                            at_value(nxt)
                            scan(0)
                            scan(1)
                        elif m == 2:
                            scan(2)
                            scan(3)
                            tie_counts()
                        elif m == 3:
                            make_mask(nxt)
                        elif m == 6:
                            best(nxt)
                            one_hot(nxt)
                    residual(b, TB - 1)

                own.did(dve.memset(carry, 0.0))
                at_value(0)
                for t in range(TB):
                    scan(t)
                tie_counts()
                make_mask(0)
                best(0)
                one_hot(0)
                batch(0, True)
                with dve.Fori(1, B - 1) as i:
                    own.loop(i, PER_BATCH, 1)
                    own.wait()
                    batch(i, True)
                    own.end(B - 2)
                batch(B - 1, False)

            @block.tensor
            def _(pe):
                def tie(b):
                    pe.wait_ge(tie_in, b + 1)
                    pe.matmul(tie_ps[:, 0:5], ones, rcex, start=True, stop=False)
                    pe.matmul(tie_ps[:, 0:4], tri, rc, start=False, stop=True).then_inc(tie_ready, 1)

                def turn(b, t):
                    pe.wait_ge(mask_ready, b + 1)
                    if later(b, t):
                        pe.wait_ge(xtn_ready, b * TB + t)
                    for c in range(DC):
                        mm = pe.transpose(xt_psb[:, c * P:(c + 1) * P], mask[:, t * S + c:(t + 1) * S:DC], identb)
                    mm.then_inc(xt_ready, 1)

                def logits(b):
                    pe.wait_ge(xtn_ready, TB * (b + 1))
                    for t in range(TB):
                        for c in range(DC):
                            for k in range(3):
                                mm = pe.matmul(log_ps[:, t * E0:(t + 1) * E0], xTn[:, (t * DC + c) * P:(t * DC + c + 1) * P],
                                               gate0_parts[:, k, c, :], start=c + k == 0, stop=c == DC - 1 and k == 2)
                    mm.then_inc(log_ready, 1)

                def positions(b):
                    pe.wait_ge(sel_ready, b + 1)
                    for t in range(TB):
                        to = pos_ps[:, t * E0:(t + 1) * E0]
                        pe.matmul(to, trib, selb[:, t, :], start=True, stop=False)
                        for s in range(t):
                            pe.matmul(to, onesb, selb[:, s, :], start=False, stop=False)
                        mm = pe.matmul(to, onesb, carry, start=False, stop=True)
                    mm.then_inc(pos_ready, 1)

                def product(m, bank, column):
                    for c in range(DC):
                        for part in (sh_hi, sh_lo):
                            mm = pe.matmul(bank[:, 0:F0], xT[:, (m // 2 * DC + c) * P:(m // 2 * DC + c + 1) * P],
                                           part[:, c, column:column + F0], start=c == 0 and part is sh_hi,
                                           stop=c == DC - 1 and part is sh_lo)
                    return mm

                def gate(b, m):
                    if later(b, m):
                        pe.wait_ge(sil_ready, b * ITEMS + m)
                    product(m, gate_ps, (m % 2) * 2 * F0).then_inc(g_ready, 1)

                def up(b, m):
                    if later(b, m):
                        pe.wait_ge(gu_ready, b * ITEMS + m)
                    product(m, up_ps, (m % 2) * 2 * F0 + F0).then_inc(u_ready, 1)

                def turn_h(b, m):
                    n = b * ITEMS + m
                    pe.wait_ge(gu_ready, n + 1)
                    if later(b, m):
                        pe.wait_ge(ht_ready, n)
                    for c, (f, k) in enumerate(F0C):
                        mm = pe.transpose(t_ps[0:k, c * P:(c + 1) * P], gu[:, f:f + k], ident)
                    mm.then_inc(t_ready, 1)

                def down(b, m):
                    n = b * ITEMS + m
                    pe.wait_ge(ht_ready, n + 1)
                    if m % 2 == 0 and later(b, m):
                        pe.wait_ge(o_ready, b * TB + m // 2)
                    for c, (f, k) in enumerate(F0C):
                        mm = pe.matmul(d_ps[:, :], hT[0:k, c, :], sh_dw[0:k, 3 * (m % 2) + c, :],
                                       start=m % 2 == 0 and c == 0, stop=m % 2 == 1 and c == 2)
                    if m % 2:
                        mm.then_inc(d_ready, 1)

                def batch(b, more):
                    for m in range(ITEMS):
                        if m % 2 == 0:
                            pe.wait_ge(xt_moved, b * TB + m // 2 + 1)
                        gate(b, m)
                        if m:
                            turn_h(b, m - 1)
                        up(b, m)
                        if m == 0:
                            positions(b)
                        if more and m == 3:
                            tie(b + 1)
                        if more and m in (4, 5):
                            turn(b + 1, 2 * m - 8)
                        if more and m == 6:
                            logits(b + 1)
                        if m:
                            down(b, m - 1)
                        if more and m in (4, 5):
                            turn(b + 1, 2 * m - 7)
                    turn_h(b, ITEMS - 1)
                    down(b, ITEMS - 1)
                tie(0)
                for t in range(TB):
                    turn(0, t)
                logits(0)
                batch(0, True)
                with pe.Fori(1, B - 1) as i:
                    batch(i, True)
                batch(B - 1, False)

        early.close()
        middle = ctx.enter_context(ExitStack())
        PART0 = DC * F0
        space0 = sb("space0", [P, 14000], till=middle)
        parts0 = sb("parts0", [P, 8 * PART0], F32R, till=middle)
        rows0 = sb("rows0", [P, 2 * D], F32R, till=middle)

        def expert_stage(name, items, F, chunks, row_dt, rows, slots, cols, acc, region, table_at, loads, tile_cols=None,
                         ends_row=None, weights_in=None):
            rw = D // 2 if row_dt == BF16 else D
            at = [region]

            def buf(words, dt=F32):
                at[0] += words
                return take(space0 if loads else misc, at[0] - words, words, dt)
            xrow = [buf(rw, row_dt) for _ in range(2)]
            def turned(of, i):
                return of[:, i * D:(i + 1) * D].rearrange("p (c n) -> p c n", c=DC)
            if loads:
                parts = [[[parts0[:, (4 * u + 2 * m + k) * DC * F0:(4 * u + 2 * m + k + 1) * DC * F0] for k in range(2)]
                          for m in range(2)] for u in range(2)]
                xT = [[turned(rows0, u)] for u in range(2)]
                hT = buf(512).rearrange("p (c n) -> p c n", c=4)
            else:
                parts = [[[split1[:, (2 * m + k) * DC * D:(2 * m + k + 1) * DC * D] for k in range(2)] for m in range(3)]] * 2
                xT = [[turned(cols2, 2 * u + k) for k in range(2)] for u in range(2)]
                hT = [turned(cols2, 4 + k) for k in range(2)]
            sil, gu = buf(512), buf(512)
            ob = [buf(D) for _ in range(2)]
            table = take(misc, table_at, 2 * cols)
            idx_get = [take(misc, table_at + 2 * cols + i, 1, I32) for i in range(2)]
            idx_add = [take(misc, table_at + 2 * cols + 2 + i, 1, I32) for i in range(2)]
            gate_ps, up_ps, h_ps, d_ps, x_ps = PS[0:5]
            x_psv = x_ps[:, 0:rw] if row_dt == F32 else x_ps[:, 0:rw].bitcast(BF16)
            idm = ident if row_dt == F32 else identb

            def sm(n):
                return sem(f"{name}_{n}")
            table_in, pool_did, pool_step = sm("table_in"), sm("pool_did"), sm("pool_step")
            rows_in = [sm(f"rows_in{i}") for i in range(2)]
            add_done = [sm(f"add_done{i}") for i in range(2)]
            x_turned, x_copied, g_ready, sil_ready = sm("x_turned"), sm("x_copied"), sm("g_ready"), sm("sil_ready")
            u_ready, gu_ready, h_turned, h_copied = sm("u_ready"), sm("gu_ready"), sm("h_turned"), sm("h_copied")
            d_ready, o_ready = sm("d_ready"), sm("o_ready")
            rounded, left = ([sm(f"{m}_{what}") for m in "gud"] for what in ("rounded", "left"))
            x_rounded, h_rounded = sm("x_rounded"), sm("h_rounded")
            if loads:
                wg_in, wu_in, wd_in = ([sm(f"w{k}_in{i}") for i in range(2)] for k in "gud")

            class Tile:

                def __init__(self, n, u, h, early=False):
                    self.n, self.u, self.h, self.early = n, u, h, early
                    self.first = early and u == 0

            def fixed(n):
                return Tile(n, n % 2, n // 2, n < 2)

            def inside(j, k, ahead=0):
                o = 1 + k + ahead
                return Tile(2 * j + o, o % 2, j + o // 2)
            PAIRS = (items - 2) // 2

            def pipeline(eng, slot):
                slot(None, fixed(0), fixed(1))
                for n in (1, 2):
                    slot(fixed(n - 1), fixed(n), fixed(n + 1))
                with eng.Fori(1, PAIRS) as j:
                    for k in range(2):
                        slot(inside(j, k, -1), inside(j, k), inside(j, k, 1))
                slot(fixed(items - 2), fixed(items - 1), None)

            def pipeline_of_pairs(eng, slot):
                def at(j, o):
                    return fixed(2 * j + o) if isinstance(j, int) else Tile(2 * j + o, o % 2, j + o // 2)

                def pair(j, first=False, last=False):
                    slot(None if first else at(j, -1), at(j, 0), at(j, 1), None if last else at(j, 2))
                    slot(at(j, 0), at(j, 1), None if last else at(j, 2), None)
                pair(0, first=True)
                pair(1)
                with eng.Fori(2, items // 2 - 1) as j:
                    pair(j)
                pair(items // 2 - 1, last=True)

            with nc.Block() as block:
                @block.sync
                def _(sp):
                    if loads:
                        sp.dma_start(table, slots.rearrange("(p c) w -> p (c w)", p=P)).then_inc(table_in, 16)
                        (dg, du, dd), (bg, bu, bd) = loads

                        def in_load(t, dst, src, free, arrived):
                            if not t.early:
                                sp.wait_ge(free, t.n - 1)
                            sp.dma_start(dst[t.u], src[bass.ds(t.n, 1)].rearrange("e (p c) f -> p (e c f)", p=P)).then_inc(arrived[t.u], 16)

                        def down_load(t):
                            if not t.early:
                                sp.wait_ge(d_ready, t.n - 1)
                            sp.dma_start(bd[t.u][:, 0:2 * D].rearrange("p (c n) -> p c n", c=2),
                                         dd[bass.ds(t.n, 1), 0:2 * P, :].rearrange("e (c p) n -> p (e c) n", p=P)).then_inc(wd_in[t.u], 16)
                            sp.dma_start(bd[t.u][0:F - 2 * P, 2 * D:3 * D],
                                         dd[bass.ds(t.n, 1), 2 * P:F, :].rearrange("e p n -> p (e n)")).then_inc(wd_in[t.u], 16)

                        for n in range(2):
                            in_load(fixed(n), bg, dg, left[0], wg_in)
                            in_load(fixed(n), bu, du, left[1], wu_in)
                            if n == 0:
                                sp.wait_ge(rows_in[0], 16)
                        down_load(fixed(0))
                        in_load(fixed(2), bg, dg, left[0], wg_in)
                        in_load(fixed(2), bu, du, left[1], wu_in)
                        down_load(fixed(1))

                        def slot(j, k):
                            t = inside(j, k, 2)
                            in_load(t, bg, dg, left[0], wg_in)
                            in_load(t, bu, du, left[1], wu_in)
                            down_load(inside(j, k, 1))
                        with sp.Fori(0, PAIRS - 1) as j:
                            slot(j, 0)
                            slot(j, 1)
                        slot(PAIRS - 1, 0)
                        down_load(fixed(items - 1))
                    else:
                        with sp.Fori(1, RING) as e:
                            sp.wait_ge(weights_in, e * 16 * 3)
                            expert_load(sp, e, e)
                        for e in range(RING, E1):
                            end = sp.value_load(ends_row[0:1, e - RING:e - RING + 1], min_val=1, max_val=items // 2)
                            sp.wait_ge(d_ready, end * 2)
                            sp.wait_ge(weights_in, e * 16 * 3)
                            expert_load(sp, e, e - RING)
                        sp.wait_ge(weights_in, 16 * 3 * E1)

                class Found:

                    def __init__(self, eng):
                        self.eng, self.place = eng, None

                    def ahead(self, this, then):
                        self.place = self.load(2, this, RING)
                        self.next(then)

                    def next(self, then):
                        if then:
                            self.next_place = self.load(2, then, RING)

                    def load(self, row, t, count):
                        return self.eng.value_load(tile_cols[row][0:1, bass.ds(t.h, 1)], min_val=0, max_val=count - 1)

                def matrix(found, m):
                    place = found.place if m == 2 else found.next_place
                    return ring[:, bass.ds(place * SLOT + m * DC * D, DC * D)]

                @block.gpsimd
                def _(pool):
                    own = Chain(pool, pool_did)

                    def column(t):
                        if tile_cols is None:
                            return t.n * 2
                        return pool.value_load(tile_cols[0][0:1, bass.ds(t.h, 1)], min_val=0, max_val=cols - 2) * 2 + 2 * t.u

                    def gather(t):
                        col = column(t)
                        if not t.early:
                            pool.wait_ge(rows_in[t.u], t.h * 16)
                        own.did(pool.tensor_copy(idx_get[t.u], table[:, bass.ds(col, 1)].bitcast(I32)))
                        own.wait()
                        if not t.early:
                            pool.wait_ge(x_turned, t.n - 1)
                        pool.sem_inc(pool_step, 1)
                        pool.indirect_dma_start(xrow[t.u], None, rows, bass.IndirectOffsetOnAxis(idx_get[t.u].bitcast(U32), 0)
                                                ).then_inc(rows_in[t.u], 16)

                    def add(t):
                        col = column(t)
                        if not t.first:
                            pool.wait_ge(add_done[1 - t.u], (t.h + t.u) * 16)
                        own.did(pool.tensor_copy(idx_add[t.u], table[:, bass.ds(col, 1)].bitcast(I32)))
                        own.wait()
                        pool.wait_ge(o_ready, t.n + 1)
                        pool.sem_inc(pool_step, 1)
                        pool.indirect_dma_start(acc, bass.IndirectOffsetOnAxis(idx_add[t.u].bitcast(U32), 0), ob[t.u], None,
                                                compute_op=ALU.add).then_inc(add_done[t.u], 16)
                    if loads:
                        pool.wait_ge(table_in, 16)
                    for n in range(3):
                        gather(fixed(n))
                    for n in range(2):
                        gather(fixed(n + 3))
                        add(fixed(n))
                    with pool.Fori(1, PAIRS - 1) as j:
                        own.loop(j, 4, 1)
                        for k in range(2):
                            gather(inside(j, k, 2))
                            add(inside(j, k, -1))
                        own.end(PAIRS - 2)
                    gather(fixed(items - 1))
                    add(fixed(items - 4))
                    add(fixed(items - 3))
                    add(fixed(items - 2))
                    add(fixed(items - 1))
                    for u in range(2):
                        pool.wait_ge(add_done[u], items // 2 * 16)

                @block.scalar
                def _(act):
                    def silu(t):
                        act.wait_ge(g_ready, t.n + 1)
                        if not t.first:
                            act.wait_ge(gu_ready, t.n)
                        act.activation(sil[:, 0:F], gate_ps[:, 0:F], ACT.Silu).then_inc(sil_ready, 1)

                    def scale(t):
                        col = t.n * 2 if tile_cols is None else act.value_load(
                            tile_cols[0][0:1, bass.ds(t.h, 1)], min_val=0, max_val=cols - 2) * 2 + 2 * t.u
                        if not t.early:
                            act.wait_ge(add_done[t.u], t.h * 16)
                        act.wait_ge(d_ready, t.n + 1)
                        act.activation(ob[t.u], d_ps[:, :], ACT.Copy, scale=table[:, bass.ds(col + 1, 1)]).then_inc(o_ready, 1)

                    def round_off(t, m):
                        if loads:
                            act.wait_ge((wg_in, wu_in)[m][t.u], 16 * (t.h + 1))
                            if not t.early:
                                act.wait_ge((g_ready, u_ready)[m], t.n - 1)
                            act.copy(parts[t.u][m][0], loads[1][m][t.u]).then_inc(rounded[m], 1)
                            return
                        if t.u:
                            return
                        if m == 0:
                            act.wait_ge(weights_in, found.expert * (16 * 3) + 16 * 3)
                        if not t.first:
                            act.wait_ge((g_ready, u_ready, d_ready)[m], t.n)
                        act.copy(parts[t.u][m][0], matrix(found, m)).then_inc(rounded[m], 1)

                    def round_x(t):
                        act.wait_ge(x_turned, t.n + 1)
                        if not t.early:
                            act.wait_ge(u_ready, t.n - 1)
                        act.copy(xT[t.u][0], x_psv.rearrange("p (c n) -> p c n", c=DC)).then_inc(x_rounded, 1)

                    def round_h(t):
                        act.wait_ge(h_turned, t.n + 1)
                        if not t.first:
                            act.wait_ge(d_ready, t.n)
                        act.copy(hT[0], h_ps[:, :].rearrange("p (c n) -> p c n", c=DC)).then_inc(h_rounded, 1)

                    if loads:
                        def slot(prev, this, nxt):
                            if nxt:
                                round_off(nxt, 0)
                            silu(this)
                            if nxt:
                                round_off(nxt, 1)
                            if prev:
                                scale(prev)
                        for m in range(2):
                            round_off(fixed(0), m)
                        act.wait_ge(table_in, 16)
                    else:
                        found = Found(act)

                        def look_up(this, then):
                            found.ahead(this, then)
                            if then:
                                found.expert = found.load(1, then, E1)

                        def slot(prev, this, nxt, then):
                            if this.u:
                                round_off(prev, 2)
                            silu(this)
                            if prev:
                                round_h(prev)
                            if nxt:
                                round_off(nxt, 0)
                                round_x(nxt)
                                round_off(nxt, 1)
                            if this.u == 0:
                                look_up(this, then)
                            if prev:
                                scale(prev)
                        head = fixed(0)
                        found.next(head)
                        found.expert = found.load(1, head, E1)
                        round_off(head, 0)
                        round_x(head)
                        round_off(head, 1)
                    (pipeline if loads else pipeline_of_pairs)(act, slot)
                    last = fixed(items - 1)
                    if not loads:
                        round_h(last)
                    scale(last)

                @block.vector
                def _(dve):
                    def copy_h(t):
                        dve.wait_ge(h_turned, t.n + 1)
                        full = [c for c, (_, k) in enumerate(chunks) if k == P]
                        mm = dve.tensor_copy(hT[:, 0:len(full), :].rearrange("p c n -> p (c n)"), h_ps[:, 0:len(full) * P])
                        for c, (_, k) in enumerate(chunks):
                            if k < P:
                                dve.tensor_copy(hT[0:k, c, :], h_ps[0:k, c * P:(c + 1) * P]).then_inc(h_copied, 1)
                                mm.then_inc(h_copied, 1)
                                return
                        mm.then_inc(h_copied, 2)

                    def product(t):
                        dve.wait_ge(sil_ready, t.n + 1)
                        dve.wait_ge(u_ready, t.n + 1)
                        dve.tensor_tensor(gu[:, 0:F], sil[:, 0:F], up_ps[:, 0:F], ALU.mult).then_inc(gu_ready, 1)

                    def copy_x(t):
                        dve.wait_ge(x_turned, t.n + 1)
                        if not t.early:
                            dve.wait_ge(u_ready, t.n - 1)
                        dve.tensor_copy(xT[t.u][0].rearrange("p c n -> p (c n)"), x_psv).then_inc(x_copied, 1)

                    def leave(t, m):
                        if t.u and not loads:
                            return
                        dve.wait_ge(rounded[m], (t.n if loads else t.h) + 1)
                        dve.tensor_tensor(parts[t.u][m][1], loads[1][m][t.u] if loads else matrix(found, m),
                                          parts[t.u][m][0], ALU.subtract).then_inc(left[m], 1)

                    def leave_x(t):
                        dve.wait_ge(x_rounded, t.n + 1)
                        dve.tensor_tensor(xT[t.u][1], x_psv.rearrange("p (c n) -> p c n", c=DC), xT[t.u][0],
                                          ALU.subtract).then_inc(x_copied, 1)

                    def leave_h(t):
                        dve.wait_ge(h_rounded, t.n + 1)
                        dve.tensor_tensor(hT[1], h_ps[:, :].rearrange("p (c n) -> p c n", c=DC), hT[0],
                                          ALU.subtract).then_inc(h_copied, 2)

                    if loads:
                        def slot(prev, this, nxt):
                            if prev:
                                copy_h(prev)
                            if nxt:
                                leave(nxt, 0)
                            product(this)
                            if nxt:
                                copy_x(nxt)
                                leave(nxt, 1)
                        copy_x(fixed(0))
                        for m in range(2):
                            leave(fixed(0), m)
                        pipeline(dve, slot)
                        copy_h(fixed(items - 1))
                    else:
                        found = Found(dve)

                        def slot(prev, this, nxt, then):
                            if this.u:
                                leave(prev, 2)
                            if prev:
                                leave_h(prev)
                            if this.u == 0:
                                product(this)
                            if nxt:
                                leave(nxt, 0)
                                leave_x(nxt)
                            if this.u:
                                product(this)
                            if nxt:
                                leave(nxt, 1)
                            if this.u == 0:
                                found.ahead(this, then)
                        head = fixed(0)
                        found.next(head)
                        leave(head, 0)
                        leave_x(head)
                        leave(head, 1)
                        pipeline_of_pairs(dve, slot)
                        leave_h(fixed(items - 1))

                @block.tensor
                def _(pe):
                    def turn_x(t):
                        pe.wait_ge(rows_in[t.u], 16 * (t.h + 1))
                        if not t.first:
                            pe.wait_ge(x_copied, t.n)
                        for c in range(DC):
                            mm = pe.transpose(x_psv[:, c * P:(c + 1) * P], xrow[t.u][:, c:D:DC], idm)
                        mm.then_inc(x_turned, 1)

                    pairs_of = ((0, 0), (0, 1)) if loads else ((0, 0), (0, 1), (1, 0))

                    def rows_by(cols_t, t, m, bank, width):
                        for c in range(DC):
                            for k, (r, w) in enumerate(pairs_of):
                                mm = pe.matmul(bank[:, 0:width], cols_t[r][:, c, :], parts[t.u][m][w][:, c * width:(c + 1) * width],
                                               start=c + k == 0, stop=c == DC - 1 and k == len(pairs_of) - 1)
                        return mm

                    def gate(t):
                        pe.wait_ge(x_copied, t.n + 1)
                        if not t.first:
                            pe.wait_ge(sil_ready, t.n)
                        pe.wait_ge(left[0], (t.n if loads else t.h) + 1)
                        rows_by(xT[t.u], t, 0, gate_ps, F).then_inc(g_ready, 1)

                    def up(t):
                        if not t.first:
                            pe.wait_ge(gu_ready, t.n)
                        pe.wait_ge(left[1], (t.n if loads else t.h) + 1)
                        rows_by(xT[t.u], t, 1, up_ps, F).then_inc(u_ready, 1)

                    def turn_h(t):
                        pe.wait_ge(gu_ready, t.n + 1)
                        if not t.first:
                            pe.wait_ge(h_copied, 2 * t.n)
                        for c, (f, k) in enumerate(chunks):
                            src = gu[:, f:f + k] if loads else gu[:, c:F:DC]
                            mm = pe.transpose(h_ps[0:k, c * P:(c + 1) * P], src, ident)
                        mm.then_inc(h_turned, 1)

                    def down(t):
                        pe.wait_ge(h_copied, 2 * (t.n + 1))
                        if not t.first:
                            pe.wait_ge(o_ready, t.n)
                        if not loads:
                            pe.wait_ge(left[2], t.h + 1)
                            rows_by(hT, t, 2, d_ps, D).then_inc(d_ready, 1)
                            return
                        pe.wait_ge(wd_in[t.u], 32 * (t.h + 1))
                        for c, (f, k) in enumerate(chunks):
                            mm = pe.matmul(d_ps[:, :], hT[0:k, c, :], loads[1][2][t.u][0:k, c * D:(c + 1) * D],
                                           start=c == 0, stop=c == len(chunks) - 1)
                        mm.then_inc(d_ready, 1)

                    def slot(prev, this, nxt, then=None):
                        gate(this)
                        if prev:
                            turn_h(prev)
                        up(this)
                        if nxt:
                            turn_x(nxt)
                        if prev:
                            down(prev)
                    turn_x(fixed(0))
                    (pipeline if loads else pipeline_of_pairs)(pe, slot)
                    turn_h(fixed(items - 1))
                    down(fixed(items - 1))

        wbuf = [[take(space0, u * 4352 + o, w) for u in range(2)] for o, w in ((0, 1408), (1408, 1408), (2816, 1536))]
        expert_stage("e0", E0, F0, F0C, BF16, mask_rows, slots0, E0, acc0, 2 * 4352, M2,
                     ((w_gate, w_up, w_down), wbuf))
        middle.close()

        late = ctx.enter_context(ExitStack())
        space1 = sb("space1", [P, 5152 + SLOT], till=late)
        parts1 = sb("parts1", [P, 2 * SLOT], F32R, till=late)
        cols1 = sb("cols1", [P, 6 * D], F32R, till=late)
        shared = [space1[:, 5152 + m * DC * D:5152 + (m + 1) * DC * D] for m in range(3)]
        sh1_hi, sh1_lo = ([parts1[:, (3 * k + m) * DC * D:(3 * k + m + 1) * DC * D] for m in range(3)] for k in range(2))
        y_hi, y_lo = ([cols1[:, (2 * k + i) * D:(2 * k + i + 1) * D].rearrange("p (c n) -> p c n", c=DC) for i in range(2)]
                      for k in range(2))
        h_hi, h_lo = (cols1[:, (4 + k) * D:(5 + k) * D].rearrange("p (c n) -> p c n", c=DC) for k in range(2))
        x1 = [take(space1, i * D, D) for i in range(TB)]
        HIST = 3
        x1T = [take(space1, 2048 + i * 528, DC * (P + HIST)).rearrange("p (c n) -> p c n", c=DC) for i in range(2)]
        yT = [take(space1, 3104 + i * D, D).rearrange("p (c n) -> p c n", c=DC) for i in range(2)]
        y_row = [take(space1, 4128 + i * D, D) for i in range(2)]
        sil1 = take(misc, M3, D)
        gu1 = take(misc, M3 + 512, D)
        ob1 = [take(misc, M3 + 1536 + i * D, D) for i in range(2)]
        M4 = M3 + 2560
        conv_w = take(misc, M4, 4 * DC).rearrange("p (k c) -> p k c", k=4)
        conv_bias = take(misc, M4 + 16, DC)
        gate1_w = take(misc, M4 + 20, DC * E1).rearrange("p (c e) -> p c e", c=DC)
        gb_bc = take(misc, M4 + 48, E1)
        bias_bc = take(misc, M4 + 56, E1)
        lg1 = take(misc, M4 + 64, TB * 8).rearrange("p (t e) -> p t e", e=8)
        prob = take(misc, M4 + 96, TB * 8).rearrange("p (t e) -> p t e", e=8)
        biased = take(misc, M4 + 128, TB * 8).rearrange("p (t e) -> p t e", e=8)
        top1 = take(misc, M4 + 160, TB * 8).rearrange("p (t e) -> p t e", e=8)
        idx1 = take(misc, M4 + 192, TB * 8, U32).rearrange("p (t e) -> p t e", e=8)
        mx1 = take(misc, M4 + 224, TB)
        idxf1 = take(misc, M4 + 228, TB * K1)
        oh1 = take(misc, M4 + 240, TB * K1 * 8)
        prod1 = take(misc, M4 + 336, TB * K1 * 8)
        pk1 = take(misc, M4 + 432, TB * K1)
        s3 = take(misc, M4 + 444, TB)
        pp1 = take(misc, M4 + 448, TB * K1)
        posi = take(misc, M4 + 460, TB * K1, I32)
        hi_i = take(misc, M4 + 472, TB * K1, I32)
        lo_i = take(misc, M4 + 484, TB * K1, I32)
        hi_f = take(misc, M4 + 496, TB * K1)
        lo_f = take(misc, M4 + 508, TB * K1)
        dest1 = take(misc, M4 + 520, TB * K1, I32)
        pairs1 = take(misc, M4 + 532, TB * K1 * 2)
        sel1 = take(misc, M4 + 556, TB * 4, BF16).rearrange("p (t e) -> p t e", e=8)
        carry1 = take(misc, M4 + 572, 4, BF16)
        seltot1 = take(misc, M4 + 576, 8)
        M5 = 4800
        assert M4 + 584 <= M5 and M3 + 3072 <= M5

        names = ("small_in c_x_turned c_x_copied conv_done c_log_ready y_turned y_copied c_g c_sil c_u c_gu c_ht c_hc c_d c_o "
                 "c_lm c_exp c_sel c_pos c_scat c_scat_done c_dve c_step c_pstep sh1_rounded sh1_left y_rounded y_left h_rounded c_act")
        (small_in, c_x_turned, c_x_copied, conv_done, c_log_ready, y_turned, y_copied, c_g, c_sil, c_u, c_gu, c_ht, c_hc,
         c_d, c_o, c_lm, c_exp, c_sel, c_pos, c_scat, c_scat_done, c_dve, c_step, c_pstep, sh1_rounded, sh1_left, y_rounded, y_left, h_rounded, c_act) = (
            sem(n) for n in names.split())
        sh1_in = [sem(f"sh1_in{m}") for m in range(3)]
        x1_in = [sem(f"x1_in{i}") for i in range(TB)]
        y_out = [sem(f"y_out{i}") for i in range(2)]
        out_out = [sem(f"out_out{i}") for i in range(2)]
        out_t = out[0:T].rearrange("(t p) d -> t p d", p=P)
        y_t = y_rows[0:T].rearrange("(t p) d -> t p d", p=P)
        ybk_ps, log1_ps, pos1_ps = PS[5:8]
        log1 = log1_ps[:, 0:TB * 8].rearrange("p (t e) -> p t e", e=8)

        def nxt_tile(b, t):
            return (b, t + 1) if t + 1 < TB else (b + 1, 0)

        with nc.Block() as block:
            @block.sync
            def _(sp):
                sp.dma_start(gate1_w, gate1.rearrange("(p c) e -> p c e", c=DC)).then_inc(small_in, 16)
                sp.dma_start(conv_w, cond.rearrange("k (p c) -> p k c", c=DC)).then_inc(small_in, 16)
                sp.dma_start(conv_bias, conv_b.rearrange("(p c) -> p c", c=DC)).then_inc(small_in, 16)
                sp.dma_start(gb_bc, gate1_b.partition_broadcast(P)).then_inc(small_in, 16)
                sp.dma_start(bias_bc, biases.partition_broadcast(P)).then_inc(small_in, 16)

                def batch(b, more):
                    for t in range(TB):
                        n = b * TB + t
                        if more or t < TB - 1:
                            nb, nt = nxt_tile(b, t)
                            sp.wait_ge(y_copied, n + 2)
                            sp.dma_start(y_t[nb * TB + nt], y_row[nt % 2]).then_inc(y_out[nt % 2], 16)
                        sp.wait_ge(c_o, n + 1)
                        sp.dma_start(out_t[n], ob1[t % 2]).then_inc(out_out[t % 2], 16)
                        if more:
                            sp.dma_start(x1[t], acc0_t[n + TB]).then_inc(x1_in[t], 16)
                for t in range(TB):
                    sp.dma_start(x1[t], acc0_t[t]).then_inc(x1_in[t], 16)
                    if t < 3:
                        sp.dma_start(shared[t], w_res[:, t * DC * D:(t + 1) * DC * D]).then_inc(sh1_in[t], 16)
                sp.wait_ge(y_copied, 1)
                sp.dma_start(y_t[0], y_row[0]).then_inc(y_out[0], 16)
                batch(0, True)
                with sp.Fori(1, B - 1) as b:
                    batch(b, True)
                batch(B - 1, False)
                for i in range(2):
                    sp.wait_ge(y_out[i], 16 * TT // 2)
                    sp.wait_ge(out_out[i], 16 * TT // 2)

            @block.gpsimd
            def _(pool):
                with pool.Fori(0, B) as b:
                    pool.wait_ge(c_scat, b + 1)
                    pool.sem_inc(c_pstep, 1)
                    for j in range(TB * K1):
                        pool.indirect_dma_start(slots1, bass.IndirectOffsetOnAxis(dest1[:, j:j + 1].bitcast(U32), 0),
                                                pairs1[:, 2 * j:2 * j + 2], None).then_inc(c_scat_done, 16)
                pool.wait_ge(c_scat_done, 16 * TT * K1)

            @block.scalar
            def _(act):
                def copy_x(b, t):
                    n = b * TB + t
                    act.wait_ge(c_x_turned, n + 1)
                    if t == 0:
                        if later(b):
                            act.wait_ge(conv_done, n)
                        act.activation(x1T[0][:, :, 0:HIST], cf[:, CF_ONE:CF_ONE + DC * HIST].rearrange("p (c n) -> p c n", c=DC),
                                       ACT.Copy, scale=0.0).then_inc(c_act, 1)
                    else:
                        act.wait_ge(conv_done, n - 1)
                        act.wait_ge(c_x_copied, n)
                        act.copy(x1T[t % 2][:, :, 0:HIST], x1T[1 - t % 2][:, :, P:P + HIST]).then_inc(c_act, 1)
                    act.copy(x1T[t % 2][:, :, HIST:HIST + P], PS[4][:, :].rearrange("p (c n) -> p c n", c=DC)).then_inc(c_x_copied, 1)

                def copy_y(b, t):
                    n = b * TB + t
                    act.wait_ge(y_turned, n + 1)
                    if later(b) or t >= 2:
                        act.wait_ge(y_out[t % 2], 16 * (b * 2 + t // 2))
                    act.copy(y_row[t % 2], ybk_ps[:, :]).then_inc(y_copied, 1)

                def silu(b, t):
                    n = b * TB + t
                    act.wait_ge(c_g, n + 1)
                    if later(b, t):
                        act.wait_ge(c_gu, n)
                    act.activation(sil1, PS[0][:, :], ACT.Silu).then_inc(c_sil, 1)

                def exponentials(b):
                    act.wait_ge(c_lm, b + 1)
                    act.activation(lg1[:, :, 0:E1], lg1[:, :, 0:E1], ACT.Exp).then_inc(c_exp, 1)

                def round_weights(m):
                    act.wait_ge(sh1_in[m], 16)
                    act.copy(sh1_hi[m], shared[m]).then_inc(sh1_rounded, 1)

                def round_y(b, t):
                    n = b * TB + t
                    act.wait_ge(conv_done, n + 1)
                    if later(b) or t >= 2:
                        act.wait_ge(c_u, n - 1)
                    act.copy(y_hi[t % 2], yT[t % 2]).then_inc(y_rounded, 1)

                def round_h(b, t):
                    n = b * TB + t
                    act.wait_ge(c_ht, n + 1)
                    if later(b, t):
                        act.wait_ge(c_d, n)
                    act.copy(h_hi, PS[2][:, :].rearrange("p (c n) -> p c n", c=DC)).then_inc(h_rounded, 1)

                def batch(b, more):
                    for t in range(TB):
                        front = more or t < TB - 1
                        if front:
                            copy_x(*nxt_tile(b, t))
                        if t == TB - 1 and not more:
                            exponentials(b)
                        silu(b, t)
                        if t:
                            round_h(b, t - 1)
                        elif later(b):
                            round_h(b - 1, TB - 1)
                        if front:
                            round_y(*nxt_tile(b, t))
                            copy_y(*nxt_tile(b, t))
                        if t == TB - 1 and more:
                            exponentials(b)
                copy_x(0, 0)
                round_weights(0)
                round_y(0, 0)
                round_weights(1)
                copy_y(0, 0)
                round_weights(2)
                batch(0, True)
                with act.Fori(1, B - 1) as b:
                    batch(b, True)
                batch(B - 1, False)
                round_h(B - 1, TB - 1)

            @block.vector
            def _(dve):
                own = Chain(dve, c_dve)

                def conv(b, t):
                    n = b * TB + t
                    xs, ys = x1T[t % 2], yT[t % 2]
                    dve.wait_ge(c_x_copied, n + 1)
                    dve.wait_ge(c_act, n + 1)
                    if later(b) or t >= 2:
                        dve.wait_ge(c_u, n - 1)
                        dve.wait_ge(y_turned, n - 1)
                    for c in range(DC):
                        own.did(dve.tensor_scalar(ys[:, c, :], xs[:, c, 3:3 + P], conv_w[:, 3, c:c + 1], conv_bias[:, c:c + 1],
                                                  ALU.mult, ALU.add))
                    for k in (2, 1):
                        for c in range(DC):
                            own.wait(own.n - 3)
                            own.did(dve.scalar_tensor_tensor(ys[:, c, :], xs[:, c, k:k + P], conv_w[:, k, c:c + 1], ys[:, c, :],
                                                             ALU.mult, ALU.add))
                    for c in range(DC):
                        own.wait(own.n - 3 + c)
                        dve.scalar_tensor_tensor(ys[:, c, :], xs[:, c, 0:P], conv_w[:, 0, c:c + 1], ys[:, c, :],
                                                 ALU.mult, ALU.add).then_inc(conv_done if c == DC - 1 else c_step, 1)

                def leave_weights(m):
                    dve.wait_ge(sh1_rounded, m + 1)
                    dve.tensor_tensor(sh1_lo[m], shared[m], sh1_hi[m], ALU.subtract).then_inc(sh1_left, 1)

                def leave_y(b, t):
                    dve.wait_ge(y_rounded, b * TB + t + 1)
                    dve.tensor_tensor(y_lo[t % 2], yT[t % 2], y_hi[t % 2], ALU.subtract).then_inc(y_left, 1)

                def leave_h(b, t):
                    dve.wait_ge(h_rounded, b * TB + t + 1)
                    dve.tensor_tensor(h_lo, PS[2][:, :].rearrange("p (c n) -> p c n", c=DC), h_hi, ALU.subtract).then_inc(c_hc, 1)

                def product(b, t):
                    n = b * TB + t
                    dve.wait_ge(c_sil, n + 1)
                    dve.wait_ge(c_u, n + 1)
                    dve.tensor_tensor(gu1, sil1, PS[1][:, :], ALU.mult).then_inc(c_gu, 1)

                def residual(b, t):
                    n = b * TB + t
                    dve.wait_ge(c_d, n + 1)
                    if later(b) or t >= 2:
                        dve.wait_ge(out_out[t % 2], 16 * (b * 2 + t // 2))
                    dve.tensor_tensor(ob1[t % 2], x1[t], PS[3][:, :], ALU.add).then_inc(c_o, 1)

                def scores(b):
                    dve.wait_ge(c_log_ready, TB * (b + 1))
                    own.did(dve.tensor_tensor(lg1[:, :, 0:E1], log1[:, :, 0:E1], gb_bc.unsqueeze(1).broadcast_to([P, TB, E1]), ALU.add))
                    own.wait()
                    own.did(dve.tensor_reduce(mx1, lg1[:, :, 0:E1], AX, ALU.max))
                    own.wait()
                    dve.tensor_tensor(lg1[:, :, 0:E1], lg1[:, :, 0:E1], mx1.unsqueeze(2).broadcast_to([P, TB, E1]),
                                      ALU.subtract).then_inc(c_lm, 1)

                def choose(b):
                    dve.wait_ge(c_exp, b + 1)
                    own.did(dve.tensor_reduce(mx1, lg1[:, :, 0:E1], AX, ALU.add))
                    own.wait()
                    own.did(dve.reciprocal(mx1, mx1))
                    own.wait()
                    own.did(dve.tensor_tensor(prob[:, :, 0:E1], lg1[:, :, 0:E1], mx1.unsqueeze(2).broadcast_to([P, TB, E1]), ALU.mult))
                    own.wait()
                    own.did(dve.tensor_tensor(biased[:, :, 0:E1], prob[:, :, 0:E1], bias_bc.unsqueeze(1).broadcast_to([P, TB, E1]), ALU.add))
                    own.wait()
                    dve.sem_inc(c_step, 1)
                    for t in range(TB):
                        own.did(dve.max(top1[:, t, :], biased[:, t, :]))
                    own.wait()
                    dve.sem_inc(c_step, 1)
                    for t in range(TB):
                        own.did(dve.max_index(idx1[:, t, :], top1[:, t, :], biased[:, t, :]))
                    own.wait()
                    own.did(dve.tensor_copy(idxf1.rearrange("p (t k) -> p t k", k=K1), idx1[:, :, 0:K1]))
                    own.wait()
                    own.did(dve.tensor_tensor(oh1.rearrange("p (j e) -> p j e", e=8),
                                              cf[:, CF_I8:CF_I8 + 8].unsqueeze(1).broadcast_to([P, TB * K1, 8]),
                                              idxf1.unsqueeze(2).broadcast_to([P, TB * K1, 8]), ALU.is_equal))
                    own.wait()
                    with nc.allow_low_precision("0 or 1"):
                        dve.tensor_reduce(sel1, oh1.rearrange("p (t k e) -> p t e k", k=K1, e=8), AX, ALU.add).then_inc(c_sel, 1)
                    ohv1 = oh1.rearrange("p (t k e) -> p t k e", k=K1, e=8)
                    prv1 = prod1.rearrange("p (t k e) -> p t k e", k=K1, e=8)
                    own.did(dve.tensor_tensor(prv1, ohv1, prob.unsqueeze(2).broadcast_to([P, TB, K1, 8]), ALU.mult))
                    own.wait()
                    own.did(dve.tensor_reduce(pk1, prod1.rearrange("p (j e) -> p j e", e=8), AX, ALU.add))
                    own.wait()
                    own.did(dve.tensor_reduce(s3, pk1.rearrange("p (t k) -> p t k", k=K1), AX, ALU.add))
                    own.wait()
                    own.did(dve.reciprocal(s3, s3))
                    own.wait()
                    if later(b):
                        dve.wait_ge(c_scat_done, 16 * TB * K1 * b)
                    pv = pairs1.rearrange("p (t k w) -> p t k w", k=K1, w=2)
                    own.did(dve.tensor_tensor(pv[:, :, :, 1], pk1.rearrange("p (t k) -> p t k", k=K1),
                                              s3.unsqueeze(2).broadcast_to([P, TB, K1]), ALU.mult))
                    own.did(dve.tensor_copy(pv[:, :, :, 0].bitcast(I32), ci[:, bass.ds(b * TB + CI_TOK, TB)]
                                            .unsqueeze(2).broadcast_to([P, TB, K1])))

                def place(b):
                    dve.wait_ge(c_pos, b + 1)
                    own.did(dve.tensor_reduce(seltot1, sel1.rearrange("p t e -> p e t"), AX, ALU.add))
                    own.did(dve.tensor_tensor(prod1.rearrange("p (t k e) -> p t k e", k=K1, e=8),
                                              oh1.rearrange("p (t k e) -> p t k e", k=K1, e=8),
                                              pos1_ps[:, 0:TB * 8].rearrange("p (t e) -> p t e", e=8).unsqueeze(2)
                                              .broadcast_to([P, TB, K1, 8]), ALU.mult))
                    own.wait()
                    own.did(dve.tensor_tensor(carry1, carry1, seltot1, ALU.add))
                    own.did(dve.tensor_reduce(pp1, prod1.rearrange("p (j e) -> p j e", e=8), AX, ALU.add))
                    own.wait()
                    own.did(dve.tensor_copy(posi, pp1))
                    own.wait()
                    own.did(dve.tensor_scalar(hi_i, posi, 7, None, ALU.logical_shift_right))
                    own.did(dve.tensor_scalar(lo_i, posi, P - 1, None, ALU.bitwise_and))
                    own.wait()
                    own.did(dve.tensor_copy(hi_f, hi_i))
                    own.did(dve.tensor_copy(lo_f, lo_i))
                    own.wait()
                    own.did(dve.scalar_tensor_tensor(hi_f, idxf1, float(TT), hi_f, ALU.mult, ALU.add))
                    own.wait()
                    dve.scalar_tensor_tensor(dest1, lo_f, float(COLS1), hi_f, ALU.mult, ALU.add).then_inc(c_scat, 1)

                def batch(b, more, first=False):
                    for t in range(TB):
                        if t == TB - 1:
                            scores(b)
                        if t >= 2:
                            residual(b, t - 2)
                        elif later(b):
                            residual(b - 1, TB - 2 + t)
                        if more or t < TB - 1:
                            conv(*nxt_tile(b, t))
                        else:
                            choose(b)
                        if t:
                            leave_h(b, t - 1)
                        elif later(b):
                            leave_h(b - 1, TB - 1)
                        product(b, t)
                        if more or t < TB - 1:
                            leave_y(*nxt_tile(b, t))
                        if first and t == 0:
                            leave_weights(2)
                        if t == TB - 1:
                            if more:
                                choose(b)
                            place(b)
                own.did(dve.memset(prob, 0.0))
                own.did(dve.memset(biased, -1.0e30))
                own.did(dve.memset(carry1, 0.0))
                dve.wait_ge(small_in, 80)
                own.wait()
                conv(0, 0)
                leave_weights(0)
                leave_y(0, 0)
                leave_weights(1)
                batch(0, True, True)
                with dve.Fori(1, B - 1) as b:
                    own.loop(b, PER_BATCH_C, 1)
                    own.wait()
                    batch(b, True)
                    own.end(B - 2)
                batch(B - 1, False)
                residual(B - 1, TB - 2)
                leave_h(B - 1, TB - 1)
                residual(B - 1, TB - 1)

            @block.tensor
            def _(pe):
                def turn_x(b, t):
                    n = b * TB + t
                    pe.wait_ge(x1_in[t], 16 * (b + 1))
                    if later(b, t):
                        pe.wait_ge(c_x_copied, n)
                    for c in range(DC):
                        mm = pe.transpose(PS[4][:, c * P:(c + 1) * P], x1[t][:, c:D:DC], ident)
                    mm.then_inc(c_x_turned, 1)

                def logits_and_rows(b, t):
                    n = b * TB + t
                    pe.wait_ge(conv_done, n + 1)
                    if t == 0 and later(b):
                        pe.wait_ge(c_lm, b)
                    for c in range(DC):
                        mm = pe.matmul(log1[:, t, 0:E1], yT[t % 2][:, c, :], gate1_w[:, c, :], start=c == 0, stop=c == DC - 1)
                    mm.then_inc(c_log_ready, 1)
                    if later(b, t):
                        pe.wait_ge(y_copied, n)
                    for c in range(DC):
                        mm = pe.transpose(ybk_ps[:, c:D:DC], yT[t % 2][:, c, :], ident)
                    mm.then_inc(y_turned, 1)

                def product(m, cols_hi, cols_lo, bank):
                    for c in range(DC):
                        w = slice(c * D, (c + 1) * D)
                        for k, (x_part, w_part) in enumerate(((cols_hi, sh1_hi[m]), (cols_hi, sh1_lo[m]), (cols_lo, sh1_hi[m]))):
                            mm = pe.matmul(bank[:, :], x_part[:, c, :], w_part[:, w], start=c + k == 0,
                                           stop=c == DC - 1 and k == 2)
                    return mm

                def products(b, t, m, bank, done, free):
                    n = b * TB + t
                    if later(b, t):
                        pe.wait_ge(free, n)
                    else:
                        pe.wait_ge(sh1_left, m + 1)
                    pe.wait_ge(y_left, n + 1)
                    product(m, y_hi[t % 2], y_lo[t % 2], bank).then_inc(done, 1)

                def turn_h(b, t):
                    n = b * TB + t
                    pe.wait_ge(c_gu, n + 1)
                    if later(b, t):
                        pe.wait_ge(c_hc, n)
                    for c in range(DC):
                        mm = pe.transpose(PS[2][:, c * P:(c + 1) * P], gu1[:, c:D:DC], ident)
                    mm.then_inc(c_ht, 1)

                def down(b, t):
                    n = b * TB + t
                    pe.wait_ge(c_hc, n + 1)
                    if later(b, t):
                        pe.wait_ge(c_o, n)
                    else:
                        pe.wait_ge(sh1_left, 3)
                    product(2, h_hi, h_lo, PS[3]).then_inc(c_d, 1)

                def positions(b):
                    pe.wait_ge(c_sel, b + 1)
                    for t in range(TB):
                        to = pos1_ps[:, t * 8:(t + 1) * 8]
                        pe.matmul(to, trib, sel1[:, t, :], start=True, stop=False)
                        for s in range(t):
                            pe.matmul(to, onesb, sel1[:, s, :], start=False, stop=False)
                        mm = pe.matmul(to, onesb, carry1, start=False, stop=True)
                    mm.then_inc(c_pos, 1)

                def batch(b, more, first=False):
                    for t in range(TB):
                        prev = None if first and t == 0 else ((b, t - 1) if t else (b - 1, TB - 1))
                        if more or t < TB - 1:
                            turn_x(*nxt_tile(b, t))
                        products(b, t, 0, PS[0], c_g, c_sil)
                        if prev:
                            turn_h(*prev)
                        products(b, t, 1, PS[1], c_u, c_gu)
                        if more or t < TB - 1:
                            logits_and_rows(*nxt_tile(b, t))
                        if t == TB - 1 and not more:
                            positions(b)
                        if prev:
                            down(*prev)
                        if t == TB - 1 and more:
                            positions(b)
                pe.wait_ge(small_in, 80)
                turn_x(0, 0)
                logits_and_rows(0, 0)
                batch(0, True, True)
                with pe.Fori(1, B - 1) as b:
                    batch(b, True)
                batch(B - 1, False)
                turn_h(B - 1, TB - 1)
                down(B - 1, TB - 1)

        late.close()
        RING = 5
        ring = sb("ring", [P, RING * SLOT])
        split1 = sb("split1", [P, 2 * SLOT], F32R)
        cols2 = sb("cols2", [P, 6 * D], F32R)

        n_e = take(misc, M2, 8)
        ni = take(misc, M2 + 16, 8, I32)
        pairs_e = take(misc, M2 + 24, 8)
        ends = take(misc, M2 + 32, 8)
        past = take(misc, M2 + 40, PAIRS1 * E1).rearrange("p (j e) -> p j e", e=E1)
        past_n = take(misc, M2 + 420, PAIRS1 * E1).rearrange("p (j e) -> p j e", e=E1)
        pair_e = take(misc, M5, PAIRS1)
        pair_b = take(misc, M5 + 54, PAIRS1)
        expert_i = take(misc, M5 + 108, PAIRS1, I32)
        column_i = take(misc, M5 + 162, PAIRS1, I32)
        place_i = take(misc, M5 + 216, PAIRS1, I32)
        ends_i = take(misc, M5 + 270, 8, I32)
        M6 = M5 + 278
        w_in, table1_in, l_pe, l_dve = sem("w_in"), sem("table1_in"), sem("l_pe"), sem("l_dve")

        def expert_load(sp, e, place):
            for m in range(3):
                sp.dma_start(ring[:, bass.ds(place * SLOT + m * DC * D, DC * D)],
                             w_res[:, bass.ds(e * SLOT + SLOT + m * DC * D, DC * D)]).then_inc(w_in, 16)

        with nc.Block() as block:
            @block.sync
            def _(sp):
                sp.dma_start(take(misc, M6, 2 * COLS1), slots1.rearrange("(p c) w -> p (c w)", p=P)).then_inc(table1_in, 16)
                expert_load(sp, 0, 0)
                sp.wait_ge(table1_in, 16)

            @block.tensor
            def _(pe):
                pe.matmul(PS[7][:, 0:8], onesb, carry1, start=True, stop=True).then_inc(l_pe, 1)

            @block.vector
            def _(dve):
                own = Chain(dve, l_dve)

                def step(ins):
                    own.did(ins)
                    own.wait()
                dve.wait_ge(l_pe, 1)
                step(dve.tensor_scalar(n_e, PS[7][:, 0:8], float(2 * P - 1), None, ALU.add))
                step(dve.tensor_copy(ni, n_e))
                step(dve.tensor_scalar(ni, ni, 8, None, ALU.logical_shift_right))
                step(dve.tensor_copy(pairs_e, ni))
                step(dve.tensor_copy(ends, pairs_e))
                for e in range(1, E1):
                    step(dve.tensor_tensor(ends[:, e:e + 1], ends[:, e - 1:e], pairs_e[:, e:e + 1], ALU.add))
                step(dve.tensor_tensor(past, cf[:, CF_J:CF_J + PAIRS1].unsqueeze(2).broadcast_to([P, PAIRS1, E1]),
                                       ends[:, 0:E1].unsqueeze(1).broadcast_to([P, PAIRS1, E1]), ALU.is_ge))
                step(dve.tensor_tensor(past_n, past, pairs_e[:, 0:E1].unsqueeze(1).broadcast_to([P, PAIRS1, E1]), ALU.mult))
                step(dve.tensor_reduce(pair_e, past, AX, ALU.add))
                step(dve.tensor_reduce(pair_b, past_n, AX, ALU.add))
                step(dve.tensor_tensor(pair_b, cf[:, CF_J:CF_J + PAIRS1], pair_b, ALU.subtract))
                step(dve.scalar_tensor_tensor(pair_b, pair_e, float(TT // 2), pair_b, ALU.mult, ALU.add))
                step(dve.tensor_scalar(pair_b, pair_b, 2.0, None, ALU.mult))
                step(dve.tensor_scalar(column_i, pair_b, float(BINS), None, ALU.min))
                step(dve.tensor_scalar(pair_e, pair_e, float(E1 - 1), None, ALU.min))
                step(dve.tensor_copy(expert_i, pair_e))
                step(dve.tensor_scalar(pair_b, pair_e, float(RING), -float(RING), ALU.is_ge, ALU.mult))
                step(dve.tensor_tensor(place_i, pair_e, pair_b, ALU.add))
                step(dve.tensor_scalar(ends_i, ends, 1.0, None, ALU.max))

        expert_stage("e1", TILES1, D, [(0, P)] * DC, F32, y_rows, slots1, COLS1, out, M3, M6, None,
                     (column_i, expert_i, place_i), ends_i, w_in)


def layout(inputs):
    import numpy as np
    g = {k: np.asarray(v) for k, v in inputs.items()}
    sg, su = g["L0_ffn_sh_gate"].T, g["L0_ffn_sh_up"].T
    cf = np.zeros((P, NCF), np.float32)
    cf[:, CF_ID:CF_ID + P] = np.eye(P)
    cf[:, CF_ONE:CF_ONE + P] = 1
    cf[:, CF_TRI:CF_TRI + P] = np.triu(np.ones((P, P)), 1)
    cf[:, CF_BIT:CF_BIT + STEPS] = [-1.0] + [2.0 ** (30 - i) for i in range(31)]
    cf[:, CF_I64:CF_I64 + E0] = np.arange(E0)
    cf[:, CF_J:CF_J + PAIRS1] = np.arange(PAIRS1)
    cf[:, CF_I8:CF_I8 + 8] = np.arange(8)
    cf[:, CF_HALF:CF_HALF + P] = -0.5
    ci = np.zeros((P, 49), np.int32)
    ci[:, CI_BIT:CI_BIT + STEPS] = [2 ** (30 - i) for i in range(31)] + [0]
    ci[:, CI_TOK:CI_TOK + TT] = np.arange(T).reshape(TT, P).T
    ci[:, CI_PAD] = T + np.arange(P)
    routed = [g["L1_ffn_W1"], g["L1_ffn_Wg"], g["L1_ffn_W2"]]
    experts = [[w[e] for w in routed] for e in range(E1)]
    experts.insert(0, [g["L1_ffn_Ws1"], g["L1_ffn_Wsg"], g["L1_ffn_Ws2"]])
    w_res = np.concatenate([w.reshape(P, DC * D) for e in experts for w in e], 1)
    return {
        "x": g["x"].reshape(T, D), "fside": g["fside_BxSx1_0"].reshape(TT, P).T, "cond": g["cond_2048"],
        "gate0": g["L0_ffn_gate_w"].T, "w_gate": g["L0_ffn_w_gate"], "w_up": g["L0_ffn_w_up"],
        "w_down": g["L0_ffn_w_down"],
        "sh_in": np.concatenate([sg[:, :F0], su[:, :F0], sg[:, F0:], su[:, F0:]], 1),
        "sh_down": g["L0_ffn_sh_down"].T, "conv_b": g["L1_cond_b"], "w_res": w_res,
        "gate1": g["L1_ffn_gate_w"], "gate1_b": g["L1_ffn_gate_b"], "biases": g["L1_ffn_biases"],
        "c_f32": cf, "c_i32": ci,
    }


def kernel(**inputs):
    import numpy as np
    import concourse.bacc as bacc
    from concourse.bass_utils import run_bass_kernel_spmd

    arrays = {n: np.ascontiguousarray(a) for n, a in layout(inputs).items()}
    nc = bacc.Bacc("TRN2", target_bir_lowering=False, num_devices=1)
    args = {n: nc.dram_tensor(f"in_{n}", a.shape, mybir.dt.from_np(a.dtype), kind="ExternalInput").ap()
            for n, a in arrays.items()}
    result = nc.dram_tensor("out_rows", (T + P, D), F32, kind="ExternalOutput").ap()
    build(nc, out=result, **args)
    ran = run_bass_kernel_spmd(nc, [{f"in_{n}": a for n, a in arrays.items()}], core_ids=[0])
    return ran.results[0]["out_rows"][:T].reshape(B, S, D)
```
